# Optimizing a Trainium2 kernel written in Bass

```python
import numpy as np
import jax
import jax.numpy as jnp

def _softmax(x, axis=-1):
    return jax.nn.softmax(x, axis=axis)

def _gelu(x):
    return jax.nn.gelu(x, approximate=True)

def _silu(x):
    return jax.nn.silu(x)

def _sigmoid(x):
    return jax.nn.sigmoid(x)

def _layernorm(x, axis=-1, eps=1e-05):
    m = jnp.mean(x, axis=axis, keepdims=True)
    v = jnp.var(x, axis=axis, keepdims=True)
    return (x - m) / jnp.sqrt(v + eps)

def _scatter_add(tgt, idx, src, axis=0):
    return tgt.at[idx].add(src)

def _segment_sum(src, seg, n):
    return jax.ops.segment_sum(src, seg, n)
kernel_name = 'mk_hybrid_d2_jaxref_r8_86de9d'

def setup_inputs(seed: int=0):
    np.random.seed(seed)
    _w = jnp.asarray

    def _L0_attn_a_setup():
        import jax, jax.numpy as jnp
        import numpy as np
        D_MODEL = 128
        D_STATE = 16
        D_CONV = 4
        EXPAND = 2
        D_INNER = EXPAND * D_MODEL
        DT_RANK = (D_MODEL + 15) // 16
        B_SZ = 4
        SEQ = 256
        EPS = 1e-12

        def rmsnorm(x, w, eps=EPS):
            return x * jax.lax.rsqrt(jnp.mean(x * x, axis=-1, keepdims=True) + eps) * w

        def causal_dwconv(x, w, b):
            xc = jnp.swapaxes(x, 1, 2)
            out = jax.lax.conv_general_dilated(xc, w[:, None, :], window_strides=(1,), padding=[(w.shape[1] - 1, 0)], dimension_numbers=('NCH', 'OIH', 'NCH'), feature_group_count=w.shape[0])
            return jnp.swapaxes(out, 1, 2) + b

        def selective_scan(u, delta, A, Bm, Cm):

            def step(h, inp):
                d_t, u_t, b_t, c_t = inp
                dA = jnp.exp(d_t[..., None] * A)
                h = dA * h + (d_t * u_t)[..., None] * b_t[:, None, :]
                y = jnp.einsum('bdn,bn->bd', h, c_t)
                return (h, y)
            h0 = jnp.zeros((u.shape[0], u.shape[2], A.shape[1]), u.dtype)
            xs = (jnp.swapaxes(delta, 0, 1), jnp.swapaxes(u, 0, 1), jnp.swapaxes(Bm, 0, 1), jnp.swapaxes(Cm, 0, 1))
            _, ys = jax.lax.scan(step, h0, xs)
            return jnp.swapaxes(ys, 0, 1)

        def mamba_block(x, in_proj_w, conv_w, conv_b, x_proj_w, dt_proj_w, dt_proj_b, A_log, D, out_proj_w):
            xz = x @ in_proj_w.T
            u, z = jnp.split(xz, 2, axis=-1)
            u = jax.nn.silu(causal_dwconv(u, conv_w, conv_b))
            x_dbl = u @ x_proj_w.T
            dt = x_dbl[..., :DT_RANK]
            Bm = x_dbl[..., DT_RANK:DT_RANK + D_STATE]
            Cm = x_dbl[..., DT_RANK + D_STATE:]
            delta = jax.nn.softplus(dt @ dt_proj_w.T + dt_proj_b)
            A = -jnp.exp(A_log)
            y = selective_scan(u, delta, A, Bm, Cm) + u * D
            y = y * jax.nn.silu(z)
            return y @ out_proj_w.T
        key = jax.random.key(seed)
        ks = jax.random.split(key, 12)
        s = 0.02
        n = lambda k, sh: jax.random.normal(k, sh, jnp.float32) * s
        A_log = jnp.log(jnp.broadcast_to(jnp.arange(1, D_STATE + 1, dtype=jnp.float32), (D_INNER, D_STATE)))
        return {'input_tensor': jax.random.normal(ks[0], (B_SZ, SEQ, D_MODEL), jnp.float32), 'in_proj_w': n(ks[1], (2 * D_INNER, D_MODEL)), 'conv_w': n(ks[2], (D_INNER, D_CONV)), 'conv_b': n(ks[3], (D_INNER,)), 'x_proj_w': n(ks[4], (DT_RANK + 2 * D_STATE, D_INNER)), 'dt_proj_w': n(ks[5], (D_INNER, DT_RANK)), 'dt_proj_b': jax.random.uniform(ks[6], (D_INNER,), jnp.float32, -4.0, -2.0), 'A_log': A_log, 'D': jnp.ones((D_INNER,), jnp.float32), 'out_proj_w': n(ks[7], (D_MODEL, D_INNER)), 'norm_w': jnp.ones((D_MODEL,), jnp.float32), 'ffn_w1': n(ks[8], (4 * D_MODEL, D_MODEL)), 'ffn_b1': jnp.zeros((4 * D_MODEL,), jnp.float32), 'ffn_w2': n(ks[9], (D_MODEL, 4 * D_MODEL)), 'ffn_b2': jnp.zeros((D_MODEL,), jnp.float32), 'ffn_norm_w': jnp.ones((D_MODEL,), jnp.float32)}
    _L0_attn_a_in = _L0_attn_a_setup()

    def _L0_attn_b_setup():
        import jax, jax.numpy as jnp
        import numpy as np
        B, N, D, H = (4, 256, 128, 16)
        DH = D // H
        EPS = 1e-05
        key = jax.random.key(seed)
        k1, k2, k3, k4 = jax.random.split(key, 4)
        return {'x': jax.random.normal(k1, (B, N, D), dtype=jnp.float32), 'g_ln': jnp.ones((D,), dtype=jnp.float32), 'Wq': jax.random.normal(k2, (D, D), dtype=jnp.float32) * 0.02, 'Wkv': jax.random.normal(k3, (D, 2 * D), dtype=jnp.float32) * 0.02, 'Wo': jax.random.normal(k4, (D, D), dtype=jnp.float32) * 0.02}
    _L0_attn_b_in = _L0_attn_b_setup()

    def _L0_ffn_setup():
        import jax, jax.numpy as jnp
        import numpy as np
        B, S, H, DFF, E, K = (2, 256, 128, 256, 8, 2)

        def _moe(x, Wg, W1, b1, W2, b2, W3, b3):
            Bm, Sm, Hm = x.shape
            xt = x.reshape(-1, Hm)
            gout = xt @ Wg.T
            topv, topi = jax.lax.top_k(gout, K)
            w = jax.nn.softmax(topv, axis=-1)
            comb = jnp.einsum('tke,tk->te', jax.nn.one_hot(topi, E, dtype=x.dtype), w)
            g = jnp.einsum('th,efh->etf', xt, W1) + b1[:, None, :]
            v = jnp.einsum('th,efh->etf', xt, W2) + b2[:, None, :]
            h = jax.nn.silu(g) * v
            eo = jnp.einsum('etf,ehf->eth', h, W3) + b3[:, None, :]
            out = jnp.einsum('eth,te->th', eo, comb)
            return out.reshape(Bm, Sm, Hm)
        key = jax.random.key(seed)
        ks = jax.random.split(key, 8)
        sc_h = 1.0 / np.sqrt(H)
        sc_f = 1.0 / np.sqrt(DFF)
        x = jax.random.normal(ks[0], (B, S, H), dtype=jnp.float32)
        Wg = jax.random.uniform(ks[1], (E, H), jnp.float32, -sc_h, sc_h)
        W1 = jax.random.uniform(ks[2], (E, DFF, H), jnp.float32, -sc_h, sc_h)
        b1 = jax.random.uniform(ks[3], (E, DFF), jnp.float32, -sc_h, sc_h)
        W2 = jax.random.uniform(ks[4], (E, DFF, H), jnp.float32, -sc_h, sc_h)
        b2 = jax.random.uniform(ks[5], (E, DFF), jnp.float32, -sc_h, sc_h)
        W3 = jax.random.uniform(ks[6], (E, H, DFF), jnp.float32, -sc_f, sc_f)
        b3 = jax.random.uniform(ks[7], (E, H), jnp.float32, -sc_f, sc_f)
        return {'x': x, 'Wg': Wg, 'W1': W1, 'b1': b1, 'W2': W2, 'b2': b2, 'W3': W3, 'b3': b3}
    _L0_ffn_in = _L0_ffn_setup()

    def _L1_attn_a_setup():
        import jax, jax.numpy as jnp
        import numpy as np
        D_MODEL = 128
        N_STATE = 16
        D_INNER = 2 * D_MODEL
        DT_RANK = (D_MODEL + 15) // 16
        K_CONV = 4
        B, L = (1, 128)

        def _causal_dw_conv(x, w, b):
            K = w.shape[1]
            xp = jnp.pad(x, ((0, 0), (K - 1, 0), (0, 0)))
            Lx = x.shape[1]
            out = b
            for k in range(K):
                out = out + xp[:, k:k + Lx, :] * w[:, k]
            return out

        def _selective_scan(u, delta, A, Bm, Cm, D):
            dA = jnp.exp(delta[..., None] * A)
            dBu = delta[..., None] * Bm[:, :, None, :] * u[..., None]
            dA_t = jnp.moveaxis(dA, 1, 0)
            dBu_t = jnp.moveaxis(dBu, 1, 0)
            C_t = jnp.moveaxis(Cm, 1, 0)

            def step(h, inp):
                dA_i, dBu_i, C_i = inp
                h = dA_i * h + dBu_i
                y = jnp.einsum('bdn,bn->bd', h, C_i)
                return (h, y)
            h0 = jnp.zeros(u.shape[:1] + A.shape, dtype=u.dtype)
            _, ys = jax.lax.scan(step, h0, (dA_t, dBu_t, C_t))
            y = jnp.moveaxis(ys, 0, 1)
            return y + u * D
        key = jax.random.key(seed)
        ks = jax.random.split(key, 9)
        s = lambda fan_in: 1.0 / np.sqrt(fan_in)
        x = jax.random.normal(ks[0], (B, L, D_MODEL), dtype=jnp.float32)
        W_in = jax.random.normal(ks[1], (D_MODEL, 2 * D_INNER), dtype=jnp.float32) * s(D_MODEL)
        conv_w = jax.random.normal(ks[2], (D_INNER, K_CONV), dtype=jnp.float32) * s(K_CONV)
        conv_b = jnp.zeros((D_INNER,), dtype=jnp.float32)
        W_x = jax.random.normal(ks[3], (D_INNER, DT_RANK + 2 * N_STATE), dtype=jnp.float32) * s(D_INNER)
        W_dt = jax.random.normal(ks[4], (DT_RANK, D_INNER), dtype=jnp.float32) * s(DT_RANK)
        b_dt = jax.random.normal(ks[5], (D_INNER,), dtype=jnp.float32) * 0.01
        A_log = jnp.log(jnp.broadcast_to(jnp.arange(1, N_STATE + 1, dtype=jnp.float32), (D_INNER, N_STATE)))
        D = jnp.ones((D_INNER,), dtype=jnp.float32)
        W_out = jax.random.normal(ks[6], (D_INNER, D_MODEL), dtype=jnp.float32) * s(D_INNER)
        return {'x': x, 'W_in': W_in, 'conv_w': conv_w, 'conv_b': conv_b, 'W_x': W_x, 'W_dt': W_dt, 'b_dt': b_dt, 'A_log': A_log, 'D': D, 'W_out': W_out}
    _L1_attn_a_in = _L1_attn_a_setup()

    def _L1_attn_b_setup():
        import jax, jax.numpy as jnp
        import numpy as np
        NUM_HEADS = 16
        N_EMBD = 128

        def alibi_bias(num_heads: int, seq_len: int) -> jnp.ndarray:
            pos = jnp.arange(seq_len, dtype=jnp.float32)
            dgrid = pos[None, :] - pos[:, None]
            slopes = 2.0 ** (-8.0 / num_heads * (jnp.arange(num_heads, dtype=jnp.float32) + 1.0))
            bias = slopes[:, None, None] * dgrid[None, :, :]
            return jnp.where(dgrid[None, :, :] > 0, -jnp.inf, bias)
        key = jax.random.key(seed)
        k1, k2, k3 = jax.random.split(key, 3)
        B, L, E = (2, 256, N_EMBD)
        x = jax.random.normal(k1, (B, L, E), dtype=jnp.float32)
        w_in = jax.random.normal(k2, (3 * E, E), dtype=jnp.float32) * 0.02
        w_out = jax.random.normal(k3, (E, E), dtype=jnp.float32) * 0.02
        return {'x': x, 'w_in': w_in, 'w_out': w_out}
    _L1_attn_b_in = _L1_attn_b_setup()

    def _L1_ffn_setup():
        import jax, jax.numpy as jnp
        import numpy as np
        GROUP = 16
        EPS = 1e-05

        def _dequant(q, scale):
            w = q.astype(jnp.float32) / 7.5 - 1.0
            return w * jnp.repeat(scale, GROUP, axis=1)

        def _qlora_linear(x, q, scale, bias, la, lb):
            w = _dequant(q, scale)
            base = jnp.einsum('btd,od->bto', x, w) + bias
            lora = jnp.einsum('btr,or->bto', jnp.einsum('btd,rd->btr', x, la), lb)
            return base + lora

        def _layernorm(x, g, b):
            mu = jnp.mean(x, axis=-1, keepdims=True)
            var = jnp.mean(jnp.square(x - mu), axis=-1, keepdims=True)
            return (x - mu) * jax.lax.rsqrt(var + EPS) * g + b
        key = jax.random.key(seed)
        ks = jax.random.split(key, 6)
        D, R, B, T = (128, 32, 8, 512)
        x = jax.random.normal(ks[0], (B, T, D), dtype=jnp.float32)
        qweights = jax.random.randint(ks[1], (6, D, D), 0, 16, dtype=jnp.int32)
        scales = jax.random.uniform(ks[2], (6, D, D // GROUP), dtype=jnp.float32)
        biases = jax.random.normal(ks[3], (6, D), dtype=jnp.float32) * 0.02
        lora_a = jax.random.normal(ks[4], (6, R, D), dtype=jnp.float32) * 0.02
        lora_b = jax.random.normal(ks[5], (6, D, R), dtype=jnp.float32) * 0.02
        ln_gamma = jnp.ones((3, D), dtype=jnp.float32)
        ln_beta = jnp.zeros((3, D), dtype=jnp.float32)
        return {'x': x, 'qweights': qweights, 'scales': scales, 'biases': biases, 'lora_a': lora_a, 'lora_b': lora_b, 'ln_gamma': ln_gamma, 'ln_beta': ln_beta}
    _L1_ffn_in = _L1_ffn_setup()
    _d = {'L0_attn_a_input_tensor': _L0_attn_a_in['input_tensor'], 'L0_attn_a_in_proj_w': _L0_attn_a_in['in_proj_w'], 'L0_attn_a_conv_w': _L0_attn_a_in['conv_w'], 'L0_attn_a_conv_b': _L0_attn_a_in['conv_b'], 'L0_attn_a_x_proj_w': _L0_attn_a_in['x_proj_w'], 'L0_attn_a_dt_proj_w': _L0_attn_a_in['dt_proj_w'], 'L0_attn_a_dt_proj_b': _L0_attn_a_in['dt_proj_b'], 'L0_attn_a_A_log': _L0_attn_a_in['A_log'], 'L0_attn_a_D': _L0_attn_a_in['D'], 'L0_attn_a_out_proj_w': _L0_attn_a_in['out_proj_w'], 'L0_attn_a_norm_w': _L0_attn_a_in['norm_w'], 'L0_attn_a_ffn_w1': _L0_attn_a_in['ffn_w1'], 'L0_attn_a_ffn_b1': _L0_attn_a_in['ffn_b1'], 'L0_attn_a_ffn_w2': _L0_attn_a_in['ffn_w2'], 'L0_attn_a_ffn_b2': _L0_attn_a_in['ffn_b2'], 'L0_attn_a_ffn_norm_w': _L0_attn_a_in['ffn_norm_w'], 'L0_attn_b_g_ln': _L0_attn_b_in['g_ln'], 'L0_attn_b_Wq': _L0_attn_b_in['Wq'], 'L0_attn_b_Wkv': _L0_attn_b_in['Wkv'], 'L0_attn_b_Wo': _L0_attn_b_in['Wo'], 'L0_ffn_Wg': _L0_ffn_in['Wg'], 'L0_ffn_W1': _L0_ffn_in['W1'], 'L0_ffn_b1': _L0_ffn_in['b1'], 'L0_ffn_W2': _L0_ffn_in['W2'], 'L0_ffn_b2': _L0_ffn_in['b2'], 'L0_ffn_W3': _L0_ffn_in['W3'], 'L0_ffn_b3': _L0_ffn_in['b3'], 'L1_attn_a_W_in': _L1_attn_a_in['W_in'], 'L1_attn_a_conv_w': _L1_attn_a_in['conv_w'], 'L1_attn_a_conv_b': _L1_attn_a_in['conv_b'], 'L1_attn_a_W_x': _L1_attn_a_in['W_x'], 'L1_attn_a_W_dt': _L1_attn_a_in['W_dt'], 'L1_attn_a_b_dt': _L1_attn_a_in['b_dt'], 'L1_attn_a_A_log': _L1_attn_a_in['A_log'], 'L1_attn_a_D': _L1_attn_a_in['D'], 'L1_attn_a_W_out': _L1_attn_a_in['W_out'], 'L1_attn_b_w_in': _L1_attn_b_in['w_in'], 'L1_attn_b_w_out': _L1_attn_b_in['w_out'], 'L1_ffn_qweights': _L1_ffn_in['qweights'], 'L1_ffn_scales': _L1_ffn_in['scales'], 'L1_ffn_biases': _L1_ffn_in['biases'], 'L1_ffn_lora_a': _L1_ffn_in['lora_a'], 'L1_ffn_lora_b': _L1_ffn_in['lora_b'], 'L1_ffn_ln_gamma': _L1_ffn_in['ln_gamma'], 'L1_ffn_ln_beta': _L1_ffn_in['ln_beta']}
    _x0 = _d['L0_attn_a_input_tensor']
    _d['L0_attn_a_input_tensor'] = jax.random.normal(jax.random.fold_in(jax.random.key(seed), 1), (1, 2048, 128), dtype=_x0.dtype)
    del _x0
    return _d

def reference(L0_attn_a_input_tensor, L0_attn_a_in_proj_w, L0_attn_a_conv_w, L0_attn_a_conv_b, L0_attn_a_x_proj_w, L0_attn_a_dt_proj_w, L0_attn_a_dt_proj_b, L0_attn_a_A_log, L0_attn_a_D, L0_attn_a_out_proj_w, L0_attn_a_norm_w, L0_attn_a_ffn_w1, L0_attn_a_ffn_b1, L0_attn_a_ffn_w2, L0_attn_a_ffn_b2, L0_attn_a_ffn_norm_w, L0_attn_b_g_ln, L0_attn_b_Wq, L0_attn_b_Wkv, L0_attn_b_Wo, L0_ffn_Wg, L0_ffn_W1, L0_ffn_b1, L0_ffn_W2, L0_ffn_b2, L0_ffn_W3, L0_ffn_b3, L1_attn_a_W_in, L1_attn_a_conv_w, L1_attn_a_conv_b, L1_attn_a_W_x, L1_attn_a_W_dt, L1_attn_a_b_dt, L1_attn_a_A_log, L1_attn_a_D, L1_attn_a_W_out, L1_attn_b_w_in, L1_attn_b_w_out, L1_ffn_qweights, L1_ffn_scales, L1_ffn_biases, L1_ffn_lora_a, L1_ffn_lora_b, L1_ffn_ln_gamma, L1_ffn_ln_beta):

    def _L0_attn_a_ref(input_tensor, in_proj_w, conv_w, conv_b, x_proj_w, dt_proj_w, dt_proj_b, A_log, D, out_proj_w, norm_w, ffn_w1, ffn_b1, ffn_w2, ffn_b2, ffn_norm_w):
        import jax, jax.numpy as jnp
        import numpy as np
        D_MODEL = 128
        D_STATE = 16
        D_CONV = 4
        EXPAND = 2
        D_INNER = EXPAND * D_MODEL
        DT_RANK = (D_MODEL + 15) // 16
        B_SZ = 4
        SEQ = 256
        EPS = 1e-12

        def rmsnorm(x, w, eps=EPS):
            return x * jax.lax.rsqrt(jnp.mean(x * x, axis=-1, keepdims=True) + eps) * w

        def causal_dwconv(x, w, b):
            xc = jnp.swapaxes(x, 1, 2)
            out = jax.lax.conv_general_dilated(xc, w[:, None, :], window_strides=(1,), padding=[(w.shape[1] - 1, 0)], dimension_numbers=('NCH', 'OIH', 'NCH'), feature_group_count=w.shape[0])
            return jnp.swapaxes(out, 1, 2) + b

        def selective_scan(u, delta, A, Bm, Cm):

            def step(h, inp):
                d_t, u_t, b_t, c_t = inp
                dA = jnp.exp(d_t[..., None] * A)
                h = dA * h + (d_t * u_t)[..., None] * b_t[:, None, :]
                y = jnp.einsum('bdn,bn->bd', h, c_t)
                return (h, y)
            h0 = jnp.zeros((u.shape[0], u.shape[2], A.shape[1]), u.dtype)
            xs = (jnp.swapaxes(delta, 0, 1), jnp.swapaxes(u, 0, 1), jnp.swapaxes(Bm, 0, 1), jnp.swapaxes(Cm, 0, 1))
            _, ys = jax.lax.scan(step, h0, xs)
            return jnp.swapaxes(ys, 0, 1)

        def mamba_block(x, in_proj_w, conv_w, conv_b, x_proj_w, dt_proj_w, dt_proj_b, A_log, D, out_proj_w):
            xz = x @ in_proj_w.T
            u, z = jnp.split(xz, 2, axis=-1)
            u = jax.nn.silu(causal_dwconv(u, conv_w, conv_b))
            x_dbl = u @ x_proj_w.T
            dt = x_dbl[..., :DT_RANK]
            Bm = x_dbl[..., DT_RANK:DT_RANK + D_STATE]
            Cm = x_dbl[..., DT_RANK + D_STATE:]
            delta = jax.nn.softplus(dt @ dt_proj_w.T + dt_proj_b)
            A = -jnp.exp(A_log)
            y = selective_scan(u, delta, A, Bm, Cm) + u * D
            y = y * jax.nn.silu(z)
            return y @ out_proj_w.T
        h = mamba_block(input_tensor, in_proj_w, conv_w, conv_b, x_proj_w, dt_proj_w, dt_proj_b, A_log, D, out_proj_w)
        h = rmsnorm(h + input_tensor, norm_w)
        ff = jax.nn.gelu(h @ ffn_w1.T + ffn_b1, approximate=False) @ ffn_w2.T + ffn_b2
        return rmsnorm(ff + h, ffn_norm_w)

    def _L0_attn_b_ref(x, g_ln, Wq, Wkv, Wo):
        import jax, jax.numpy as jnp
        import numpy as np
        B, N, D, H = (4, 256, 128, 16)
        DH = D // H
        EPS = 1e-05
        mu = jnp.mean(x, axis=-1, keepdims=True)
        var = jnp.mean(jnp.square(x - mu), axis=-1, keepdims=True)
        xn = (x - mu) * jax.lax.rsqrt(var + EPS) * g_ln
        b, n, d = xn.shape
        q = (xn @ Wq).reshape(b, n, H, DH).transpose(0, 2, 1, 3)
        kv = xn @ Wkv
        k, v = jnp.split(kv, 2, axis=-1)
        k = k.reshape(b, n, H, DH).transpose(0, 2, 1, 3)
        v = v.reshape(b, n, H, DH).transpose(0, 2, 1, 3)
        scale = DH ** (-0.5)
        dots = jnp.einsum('bhid,bhjd->bhij', q, k) * scale
        mask_value = -jnp.finfo(dots.dtype).max
        causal = jnp.triu(jnp.ones((n, n), dtype=bool), k=1)
        dots = jnp.where(causal, mask_value, dots)
        attn = jax.nn.softmax(dots.astype(jnp.float32), axis=-1).astype(dots.dtype)
        out = jnp.einsum('bhij,bhjd->bhid', attn, v)
        out = out.transpose(0, 2, 1, 3).reshape(b, n, d)
        return out @ Wo

    def _L0_ffn_ref(x, Wg, W1, b1, W2, b2, W3, b3):
        import jax, jax.numpy as jnp
        import numpy as np
        B, S, H, DFF, E, K = (2, 256, 128, 256, 8, 2)

        def _moe(x, Wg, W1, b1, W2, b2, W3, b3):
            Bm, Sm, Hm = x.shape
            xt = x.reshape(-1, Hm)
            gout = xt @ Wg.T
            topv, topi = jax.lax.top_k(gout, K)
            w = jax.nn.softmax(topv, axis=-1)
            comb = jnp.einsum('tke,tk->te', jax.nn.one_hot(topi, E, dtype=x.dtype), w)
            g = jnp.einsum('th,efh->etf', xt, W1) + b1[:, None, :]
            v = jnp.einsum('th,efh->etf', xt, W2) + b2[:, None, :]
            h = jax.nn.silu(g) * v
            eo = jnp.einsum('etf,ehf->eth', h, W3) + b3[:, None, :]
            out = jnp.einsum('eth,te->th', eo, comb)
            return out.reshape(Bm, Sm, Hm)
        return _moe(x, Wg, W1, b1, W2, b2, W3, b3)

    def _L1_attn_a_ref(x, W_in, conv_w, conv_b, W_x, W_dt, b_dt, A_log, D, W_out):
        import jax, jax.numpy as jnp
        import numpy as np
        D_MODEL = 128
        N_STATE = 16
        D_INNER = 2 * D_MODEL
        DT_RANK = (D_MODEL + 15) // 16
        K_CONV = 4
        B, L = (1, 128)

        def _causal_dw_conv(x, w, b):
            K = w.shape[1]
            xp = jnp.pad(x, ((0, 0), (K - 1, 0), (0, 0)))
            Lx = x.shape[1]
            out = b
            for k in range(K):
                out = out + xp[:, k:k + Lx, :] * w[:, k]
            return out

        def _selective_scan(u, delta, A, Bm, Cm, D):
            dA = jnp.exp(delta[..., None] * A)
            dBu = delta[..., None] * Bm[:, :, None, :] * u[..., None]
            dA_t = jnp.moveaxis(dA, 1, 0)
            dBu_t = jnp.moveaxis(dBu, 1, 0)
            C_t = jnp.moveaxis(Cm, 1, 0)

            def step(h, inp):
                dA_i, dBu_i, C_i = inp
                h = dA_i * h + dBu_i
                y = jnp.einsum('bdn,bn->bd', h, C_i)
                return (h, y)
            h0 = jnp.zeros(u.shape[:1] + A.shape, dtype=u.dtype)
            _, ys = jax.lax.scan(step, h0, (dA_t, dBu_t, C_t))
            y = jnp.moveaxis(ys, 0, 1)
            return y + u * D
        silu = jax.nn.silu
        x_and_res = x @ W_in
        x_in, res = jnp.split(x_and_res, 2, axis=-1)
        x_conv = silu(_causal_dw_conv(x_in, conv_w, conv_b))
        x_dbl = x_conv @ W_x
        dt, Bm, Cm = jnp.split(x_dbl, [DT_RANK, DT_RANK + N_STATE], axis=-1)
        delta = jax.nn.softplus(dt @ W_dt + b_dt)
        A = -jnp.exp(A_log)
        y = _selective_scan(x_conv, delta, A, Bm, Cm, D)
        return y * silu(res) @ W_out

    def _L1_attn_b_ref(x, w_in, w_out):
        import jax, jax.numpy as jnp
        import numpy as np
        NUM_HEADS = 16
        N_EMBD = 128

        def alibi_bias(num_heads: int, seq_len: int) -> jnp.ndarray:
            pos = jnp.arange(seq_len, dtype=jnp.float32)
            dgrid = pos[None, :] - pos[:, None]
            slopes = 2.0 ** (-8.0 / num_heads * (jnp.arange(num_heads, dtype=jnp.float32) + 1.0))
            bias = slopes[:, None, None] * dgrid[None, :, :]
            return jnp.where(dgrid[None, :, :] > 0, -jnp.inf, bias)
        B, L, E = x.shape
        H = NUM_HEADS
        D = E // H
        qkv = jnp.einsum('ble,fe->blf', x, w_in)
        q, k, v = jnp.split(qkv, 3, axis=-1)

        def to_heads(t):
            return t.reshape(B, L, H, D).transpose(0, 2, 1, 3)
        q, k, v = (to_heads(q), to_heads(k), to_heads(v))
        scale = 1.0 / jnp.sqrt(jnp.asarray(D, dtype=x.dtype))
        scores = jnp.einsum('bhqd,bhkd->bhqk', q, k) * scale
        scores = scores + alibi_bias(H, L)[None]
        attn = jax.nn.softmax(scores, axis=-1)
        ctx = jnp.einsum('bhqk,bhkd->bhqd', attn, v)
        ctx = ctx.transpose(0, 2, 1, 3).reshape(B, L, E)
        return jnp.einsum('ble,fe->blf', ctx, w_out)

    def _L1_ffn_ref(x, qweights, scales, biases, lora_a, lora_b, ln_gamma, ln_beta):
        import jax, jax.numpy as jnp
        import numpy as np
        GROUP = 16
        EPS = 1e-05

        def _dequant(q, scale):
            w = q.astype(jnp.float32) / 7.5 - 1.0
            return w * jnp.repeat(scale, GROUP, axis=1)

        def _qlora_linear(x, q, scale, bias, la, lb):
            w = _dequant(q, scale)
            base = jnp.einsum('btd,od->bto', x, w) + bias
            lora = jnp.einsum('btr,or->bto', jnp.einsum('btd,rd->btr', x, la), lb)
            return base + lora

        def _layernorm(x, g, b):
            mu = jnp.mean(x, axis=-1, keepdims=True)
            var = jnp.mean(jnp.square(x - mu), axis=-1, keepdims=True)
            return (x - mu) * jax.lax.rsqrt(var + EPS) * g + b
        h = x
        for blk in range(3):
            i0, i1 = (2 * blk, 2 * blk + 1)
            y = _qlora_linear(h, qweights[i0], scales[i0], biases[i0], lora_a[i0], lora_b[i0])
            y = _layernorm(y, ln_gamma[blk], ln_beta[blk])
            y = jax.nn.gelu(y, approximate=False)
            y = _qlora_linear(y, qweights[i1], scales[i1], biases[i1], lora_a[i1], lora_b[i1])
            h = y + h
        return h
    x = L0_attn_a_input_tensor
    x = x + _L0_attn_a_ref(_layernorm(x, axis=-1), L0_attn_a_in_proj_w, L0_attn_a_conv_w, L0_attn_a_conv_b, L0_attn_a_x_proj_w, L0_attn_a_dt_proj_w, L0_attn_a_dt_proj_b, L0_attn_a_A_log, L0_attn_a_D, L0_attn_a_out_proj_w, L0_attn_a_norm_w, L0_attn_a_ffn_w1, L0_attn_a_ffn_b1, L0_attn_a_ffn_w2, L0_attn_a_ffn_b2, L0_attn_a_ffn_norm_w)
    x = x + _L0_ffn_ref(_layernorm(x, axis=-1), L0_ffn_Wg, L0_ffn_W1, L0_ffn_b1, L0_ffn_W2, L0_ffn_b2, L0_ffn_W3, L0_ffn_b3)
    x = x + _L0_attn_b_ref(_layernorm(x, axis=-1), L0_attn_b_g_ln, L0_attn_b_Wq, L0_attn_b_Wkv, L0_attn_b_Wo)
    x = x + _L0_ffn_ref(_layernorm(x, axis=-1), L0_ffn_Wg, L0_ffn_W1, L0_ffn_b1, L0_ffn_W2, L0_ffn_b2, L0_ffn_W3, L0_ffn_b3)
    x = x + _L1_attn_a_ref(_layernorm(x, axis=-1), L1_attn_a_W_in, L1_attn_a_conv_w, L1_attn_a_conv_b, L1_attn_a_W_x, L1_attn_a_W_dt, L1_attn_a_b_dt, L1_attn_a_A_log, L1_attn_a_D, L1_attn_a_W_out)
    x = x + _L1_ffn_ref(_layernorm(x, axis=-1), L1_ffn_qweights, L1_ffn_scales, L1_ffn_biases, L1_ffn_lora_a, L1_ffn_lora_b, L1_ffn_ln_gamma, L1_ffn_ln_beta)
    x = x + _L1_attn_b_ref(_layernorm(x, axis=-1), L1_attn_b_w_in, L1_attn_b_w_out)
    x = x + _L1_ffn_ref(_layernorm(x, axis=-1), L1_ffn_qweights, L1_ffn_scales, L1_ffn_biases, L1_ffn_lora_a, L1_ffn_lora_b, L1_ffn_ln_gamma, L1_ffn_ln_beta)
    return x

_drawn_inputs = setup_inputs


def setup_inputs(seed=0):
    import zlib

    import numpy as np

    out = dict(_drawn_inputs(seed))
    spreads = {'L0_attn_a_D': (1.0, 0.6),
     'L0_attn_a_norm_w': (1.0, 0.2),
     'L0_attn_a_ffn_b1': (0.0, 0.525),
     'L0_attn_a_ffn_b2': (0.0, 0.1),
     'L0_attn_a_ffn_norm_w': (1.0, 0.2),
     'L0_attn_b_g_ln': (1.0, 0.6),
     'L1_attn_a_conv_b': (0.0, 0.1),
     'L1_attn_a_D': (1.0, 0.2),
     'L1_ffn_ln_gamma': (1.0, 0.2),
     'L1_ffn_ln_beta': (0.0, 0.1)}
    factors = {'L0_attn_a_in_proj_w': 8.0,
     'L0_attn_a_conv_w': 8.0,
     'L0_attn_a_conv_b': 8.0,
     'L0_attn_a_x_proj_w': 8.0,
     'L0_attn_a_dt_proj_w': 8.0,
     'L0_attn_a_dt_proj_b': 8.0,
     'L0_attn_a_A_log': 8.0,
     'L0_attn_a_out_proj_w': 8.0,
     'L0_attn_b_Wq': 8.0,
     'L0_attn_b_Wkv': 8.0,
     'L0_attn_b_Wo': 8.0,
     'L0_ffn_b1': 7.966,
     'L0_ffn_b2': 7.692,
     'L1_attn_a_b_dt': 8.0,
     'L1_attn_b_w_in': 8.0,
     'L1_attn_b_w_out': 8.0,
     'L1_ffn_biases': 4.634,
     'L1_ffn_lora_a': 5.159,
     'L1_ffn_lora_b': 5.17}
    for name, (base, spread) in spreads.items():
        noise = np.random.default_rng([zlib.crc32(name.encode()), seed]).standard_normal(out[name].shape)
        drawn = base * np.exp(spread * noise) if base else spread * noise
        out[name] = jnp.asarray(drawn.astype(out[name].dtype))
    for name, factor in factors.items():
        out[name] = (out[name] * factor).astype(out[name].dtype)
    return out
```

```python
from contextlib import ExitStack, contextmanager

import concourse.bass as bass
import numpy as np
from concourse import mybir

F32 = mybir.dt.float32
BF16 = mybir.dt.bfloat16
I32 = mybir.dt.int32
U32 = mybir.dt.uint32
ALU = mybir.AluOpType
ACT = mybir.ActivationFunctionType
AX = mybir.AxisListType
ds = bass.ds

P = 128
TOK = 2048
NT = TOK // P
CH = 512
NC = TOK // CH
TPC = CH // P
D_IN = 256
NH2 = D_IN // P
NS = 16
RANK = 8
XDBL = RANK + 2 * NS
CONV = 4
SPL = 3
SCT = 1024
NSC = TOK // SCT
FF = 512
NF = FF // P
NE = 8
EF = 256
NEF = EF // P
HEADS = 16
DH = P // HEADS
PAIRS = SPL * SPL * DH
ALIBI = 12
NEG = -1e30
QL = 6
LORA = 32


class Memory:

    count = 0

    def __init__(self, nc, ctx, tag):
        self.nc, self.ctx, self.tag = nc, ctx, tag

    def name(self, n):
        Memory.count += 1
        return f"{self.tag}_{n}_{Memory.count}"

    def sb(self, n, shape, dt=F32):
        return self.ctx.enter_context(self.nc.sbuf_tensor(self.name(n), list(shape), dt))

    def ps(self, n, shape, dt=F32):
        return self.ctx.enter_context(self.nc.psum_tensor(self.name(n), list(shape), dt))

    def sem(self, n):
        return self.nc.alloc_semaphore(self.name(n))


@contextmanager
def fresh_semaphores(nc):
    before = nc.snapshot_sems()
    yield
    nc.clear_and_free_semaphores(nc.allocated_since(before))
    nc.all_engine_barrier()


def tile(i):
    return slice(i * P, (i + 1) * P)


def chunk(c):
    return slice(c * CH, (c + 1) * CH)


class Weights(dict):
    pass


def group(m, dram, tag, names):
    w = Weights()
    w.loaded = m.sem(tag + "_loaded")
    w.full = 16 * len(names)
    w.loads = []
    for n in names:
        src = dram[f"{tag}_{n}"]
        w[n] = m.sb(f"{tag}_{n}", src.shape, src.dtype)
        w.loads.append((w[n], src, w.loaded))
    return w


def start_loads(eng, loads):
    for dst, src, sem in loads:
        eng.dma_start(dst[tuple(slice(None) for _ in dst.shape)], src).then_inc(sem, 16)


def layer_norm(nc, g, tag, x, xn, xT, rounds=1, w=None, loads=()):
    with ExitStack() as ctx:
        m = Memory(nc, ctx, tag)
        stats = m.sb("stats", [P, NT, 6])
        mean_var = m.sb("mean_var", [P, NT, 2])
        var_eps = m.sb("var_eps", [P, NT])
        rstd = m.sb("rstd", [P, NT])
        turned = m.ps("turned", [P, NC, CH])
        stats_done = m.sem("stats_done")
        aggr_done = m.sem("aggr_done")
        var_ready = m.sem("var_ready")
        rstd_ready = m.sem("rstd_ready")
        normed = m.sem("normed")
        turned_ready = m.sem("turned_ready")
        copied = m.sem("copied")
        block = ctx.enter_context(nc.Block())

        @block.sync
        def _(sp):
            start_loads(sp, loads)

        @block.vector
        def _(dve):
            for r in range(rounds):
                src = x if r == 0 else xn
                for i in range(NT):
                    if r:
                        dve.wait_ge(normed, NT * (r - 1) + i + 1)
                    dve.bn_stats(stats[:, i, :], src[:, i, :]).then_inc(stats_done, 1)
                for i in range(NT):
                    dve.wait_ge(stats_done, NT * r + i + 1)
                    dve.bn_aggr(mean_var[:, i, :], stats[:, i, :]).then_inc(aggr_done, 1)
                dve.wait_ge(aggr_done, NT * (r + 1))
                dve.tensor_scalar(var_eps[:, :], mean_var[:, :, 1], 1e-5, None, ALU.add).then_inc(var_ready, 1)
                dve.wait_ge(rstd_ready, r + 1)
                for i in range(NT):
                    dve.tensor_scalar(xn[:, i, :], src[:, i, :], mean_var[:, i, 0:1], rstd[:, i:i + 1],
                                      ALU.subtract, ALU.mult).then_inc(normed, 1)

        @block.gpsimd
        def _(pool):
            for r in range(rounds):
                pool.wait_ge(var_ready, r + 1)
                pool.tensor_tensor(rstd[:, :], var_eps[:, :], g["minus_half"][:, :], ALU.pow).then_inc(rstd_ready, 1)

        @block.tensor
        def _(pe):
            for c in range(NC):
                for j in range(TPC):
                    pe.wait_ge(normed, NT * (rounds - 1) + TPC * c + j + 1)
                    last = pe.transpose(turned[:, c, tile(j)], xn[:, TPC * c + j, :], g["ident"][:, :])
                last.then_inc(turned_ready, 1)

        @block.scalar
        def _(act):
            if w is not None:
                act.wait_ge(w.loaded, w.full)
            for c in range(NC):
                act.wait_ge(turned_ready, c + 1)
                act.activation(xT[:, chunk(c)], turned[:, c, :], ACT.Identity,
                               scale=1.0 if w is None else w["gain"][:, 0:1]).then_inc(copied, 1)


def mamba(nc, g, w, tag, x, xn, finish):
    with ExitStack() as ctx:
        m = Memory(nc, ctx, tag)
        gate = m.sb("gate", [P, NH2, TOK])
        u = m.sb("u", [P, NH2, TOK])
        with ExitStack() as inner:
            xT = Memory(nc, inner, tag).sb("xT", [P, TOK])
            layer_norm(nc, g, tag + "ln", x, xn, xT)
            mamba_project(nc, w, tag + "in", xT, u, gate)
        with ExitStack() as inner:
            mi = Memory(nc, inner, tag)
            delta = mi.sb("delta", [P, NH2, TOK])
            du = mi.sb("du", [P, NH2, TOK])
            bc3 = mi.sb("bc3", [SPL * 2 * NS, TOK], BF16)
            neg_a = mi.sb("neg_a", [P, NH2, NS])
            diag_d = mi.sb("diag_d", [P, NH2, P])
            mamba_delta(nc, g, w, tag + "dt", u, delta, du, bc3, neg_a, diag_d)
            mamba_scan(nc, g, tag + "sc", u, delta, du, bc3, neg_a, diag_d, gate)
        finish(gate)


def mamba_project(nc, w, tag, xT, u, gate):
    with ExitStack() as ctx:
        m = Memory(nc, ctx, tag)
        raw = m.sb("raw", [P, NH2, CONV - 1 + TOK])
        acc = m.ps("acc", [P, 8, CH])
        projected = m.sem("projected")
        evacuated = m.sem("evacuated")
        padded = m.sem("padded")
        conv = m.sem("conv")
        silu_done = m.sem("silu_done")
        items = [(o, h, c) for o in range(2) for h in range(NH2) for c in range(NC)]
        block = ctx.enter_context(nc.Block())

        @block.tensor
        def _(pe):
            pe.wait_ge(w.loaded, w.full)
            for k, (o, h, c) in enumerate(items):
                if k >= 8:
                    pe.wait_ge(evacuated, k - 7)
                pe.matmul(acc[:, k % 8, :], w["in_T"][:, tile(o * NH2 + h)], xT[:, chunk(c)],
                          start=True, stop=True).then_inc(projected, 1)

        @block.scalar
        def _(act):
            for k, (o, h, c) in enumerate(items):
                act.wait_ge(projected, k + 1)
                if o == 0:
                    act.activation(raw[:, h, CONV - 1 + c * CH:CONV - 1 + (c + 1) * CH], acc[:, k % 8, :],
                                   ACT.Copy).then_inc(evacuated, 1)
                else:
                    act.activation(gate[:, h, chunk(c)], acc[:, k % 8, :], ACT.Silu).then_inc(evacuated, 1)
            for h in range(NH2):
                act.wait_ge(conv, CONV * (h + 1))
                act.activation(u[:, h, :], u[:, h, :], ACT.Silu).then_inc(silu_done, 1)

        @block.vector
        def _(dve):
            dve.wait_ge(w.loaded, w.full)
            dve.memset(raw[:, :, 0:CONV - 1], 0.0).then_inc(padded, 1)
            dve.wait_ge(padded, 1)
            for h in range(NH2):
                dve.wait_ge(evacuated, NC * (h + 1))
                dve.tensor_scalar(u[:, h, :], raw[:, h, 0:TOK], w["conv_w"][:, h, 0:1], w["conv_b"][:, h:h + 1],
                                  ALU.mult, ALU.add).then_inc(conv, 1)
                for k in range(1, CONV):
                    dve.wait_ge(conv, CONV * h + k)
                    dve.scalar_tensor_tensor(u[:, h, :], raw[:, h, k:k + TOK], w["conv_w"][:, h, k:k + 1],
                                             u[:, h, :], ALU.mult, ALU.add).then_inc(conv, 1)


def mamba_delta(nc, g, w, tag, u, delta, du, bc3, neg_a, diag_d):
    with ExitStack() as ctx:
        m = Memory(nc, ctx, tag)
        xd = m.sb("xd", [XDBL, TOK])
        rest = m.sb("rest", [XDBL, 2, CH])
        parts = m.sb("parts", [XDBL, SPL, TOK], BF16)
        e = m.sb("e", [P, NH2, TOK])
        ln = m.sb("ln", [P, TOK])
        t = du
        psx = m.ps("psx", [P, NC, CH])
        psz = m.ps("psz", [P, NC, CH])
        xd_sum = m.sem("xd_sum")
        xd_ready = m.sem("xd_ready")
        z_ready = m.sem("z_ready")
        abs_done = m.sem("abs_done")
        relu_done = m.sem("relu_done")
        exp_done = m.sem("exp_done")
        ln_done = m.sem("ln_done")
        ln_used = m.sem("ln_used")
        a_exp = m.sem("a_exp")
        chain = m.sem("chain")
        split = m.sem("split")
        stacked = m.sem("stacked")
        items = [(h, c) for h in range(NH2) for c in range(NC)]
        block = ctx.enter_context(nc.Block())

        @block.tensor
        def _(pe):
            for c in range(NC):
                for h in range(NH2):
                    last = pe.matmul(psx[0:XDBL, c, :], w["x_T"][:, h, :], u[:, h, chunk(c)],
                                     start=h == 0, stop=h == NH2 - 1)
                last.then_inc(xd_sum, 1)
            for k, (h, c) in enumerate(items):
                pe.wait_ge(xd_ready, c + 1)
                if k >= NC:
                    pe.wait_ge(abs_done, k - NC + 1)
                    pe.wait_ge(relu_done, k - NC + 1)
                pe.matmul(psz[:, c, :], w["dt_T"][:, tile(h)], xd[0:RANK, chunk(c)],
                          start=True, stop=True).then_inc(z_ready, 1)

        @block.scalar
        def _(act):
            act.activation(neg_a[:, :, :], w["a_log"][:, :, :], ACT.Exp).then_inc(a_exp, 1)
            for c in range(NC):
                act.wait_ge(xd_sum, c + 1)
                act.activation(xd[:, chunk(c)], psx[0:XDBL, c, :], ACT.Copy).then_inc(xd_ready, 1)
            for k, (h, c) in enumerate(items):
                act.wait_ge(z_ready, k + 1)
                act.activation(e[:, h, chunk(c)], psz[:, c, :], ACT.Abs, bias=w["dt_b"][:, h:h + 1]).then_inc(abs_done, 1)
                if c == NC - 1:
                    act.wait_ge(abs_done, k + 1)
                    act.activation(e[:, h, :], e[:, h, :], ACT.Exp, scale=-1.0).then_inc(exp_done, 1)
                    act.wait_ge(exp_done, h + 1)
                    if h:
                        act.wait_ge(ln_used, h)
                    act.activation(ln[:, :], e[:, h, :], ACT.Ln, bias=1.0).then_inc(ln_done, 1)

        @block.vector
        def _(dve):
            links = [0]

            def link(ins):
                links[0] += 1
                ins.then_inc(chain, 1)
                dve.wait_ge(chain, links[0])

            dve.wait_ge(a_exp, 1)
            link(dve.tensor_scalar(neg_a[:, :, :], neg_a[:, :, :], -1.0, None, ALU.mult))
            for h in range(NH2):
                link(dve.tensor_scalar(diag_d[:, h, :], g["ident"][:, :], w["d"][:, h:h + 1], None, ALU.mult))
            for k, (h, c) in enumerate(items):
                dve.wait_ge(abs_done, k + 1)
                dve.tensor_scalar(delta[:, h, chunk(c)], psz[:, c, :], w["dt_b"][:, h:h + 1], 0.0,
                                  ALU.add, ALU.max).then_inc(relu_done, 1)
            for h in range(NH2):
                dve.wait_ge(exp_done, h + 1)
                link(dve.tensor_scalar(t[:, h, :], e[:, h, :], 1.0, 1.0, ALU.add, ALU.subtract))
                link(dve.tensor_tensor(t[:, h, :], e[:, h, :], t[:, h, :], ALU.subtract))
                dve.wait_ge(ln_done, h + 1)
                dve.tensor_tensor(t[:, h, :], t[:, h, :], ln[:, :], ALU.add).then_inc(ln_used, 1)
                dve.wait_ge(ln_used, h + 1)
                dve.wait_ge(relu_done, NC * (h + 1))
                link(dve.tensor_tensor(delta[:, h, :], delta[:, h, :], t[:, h, :], ALU.add))
                link(dve.tensor_tensor(du[:, h, :], delta[:, h, :], u[:, h, :], ALU.mult))

        @block.gpsimd
        def _(pool):
            for c in range(NC):
                pool.wait_ge(xd_ready, c + 1)
                pool.tensor_copy(parts[:, 0, chunk(c)], xd[:, chunk(c)]).then_inc(split, 1)
                pool.wait_ge(split, 4 * c + 1)
                pool.tensor_tensor(rest[:, c % 2, :], xd[:, chunk(c)], parts[:, 0, chunk(c)], ALU.subtract).then_inc(split, 1)
                pool.wait_ge(split, 4 * c + 2)
                pool.tensor_copy(parts[:, 1, chunk(c)], rest[:, c % 2, :]).then_inc(split, 1)
                pool.wait_ge(split, 4 * c + 3)
                pool.tensor_tensor(parts[:, 2, chunk(c)], rest[:, c % 2, :], parts[:, 1, chunk(c)],
                                   ALU.subtract).then_inc(split, 1)

        @block.sync
        def _(sp):
            for c in range(NC):
                sp.wait_ge(split, 4 * (c + 1))
                for s in range(SPL):
                    sp.dma_start(bc3[2 * NS * s:2 * NS * (s + 1), chunk(c)],
                                 parts[RANK:XDBL, s, chunk(c)]).then_inc(stacked, 16)
            sp.wait_ge(stacked, 16 * SPL * NC)


def mamba_scan(nc, g, tag, u, delta, du, bc3, neg_a, diag_d, gate):
    with ExitStack() as ctx:
        m = Memory(nc, ctx, tag)
        decay = [m.sb(f"decay{s}", [P, NH2, SCT]) for s in range(2)]
        state = [m.sb(f"state{s}", [P, NH2, SCT]) for s in range(2)]
        read = [m.sb(f"read{s}", [P, NH2, SCT]) for s in range(2)]
        c_rows = [m.sb(f"c_rows{s}", [P, SCT]) for s in range(2)]
        drive = m.sb("drive", [P, NH2, SCT])
        carry = m.sb("carry", [P, NH2, NS])
        psy = m.ps("psy", [P, NH2, SCT])
        psb = m.ps("psb", [P, SCT])
        psc = m.ps("psc", [P, SCT])
        b_ready = m.sem("b_ready")
        c_ready = m.sem("c_ready")
        c_copied = m.sem("c_copied")
        decay_ready = m.sem("decay_ready")
        drive_ready = m.sem("drive_ready")
        scanned = m.sem("scanned")
        carried = m.sem("carried")
        read_ready = m.sem("read_ready")
        summed = m.sem("summed")
        skip_done = m.sem("skip_done")
        gated = m.sem("gated")
        cleared = m.sem("cleared")
        NB = SCT // CH
        block = ctx.enter_context(nc.Block())

        def in_pairs(eng, step):
            for k in range(NSC):
                for s in range(2):
                    step(k, NS * k + s, s, s)
                with eng.Fori(1, NS // 2) as i:
                    for s in range(2):
                        step(k, 2 * i + (NS * k + s), 2 * i + s, s)

        def at_least(eng, sem, q, value):
            if not isinstance(q, int) or value > 0:
                eng.wait_ge(sem, value)

        @block.tensor
        def _(pe):
            def sum_states(q, s, ends):
                pe.wait_ge(read_ready, q + 1)
                for h in range(NH2):
                    for b in range(NB):
                        last = pe.matmul(psy[:, h, chunk(b)], g["ident"][:, :], read[s][:, h, chunk(b)],
                                         start=False, stop=ends, skip_group_check=True)
                last.then_inc(summed, 1)

            def rows(k, q, n, s):
                at_least(pe, drive_ready, q, q)
                for b in range(NB):
                    last = pe.matmul(psb[:, chunk(b)], g["sel"][:, n, :],
                                     bc3[:, k * SCT + b * CH:k * SCT + (b + 1) * CH], start=True, stop=True)
                last.then_inc(b_ready, 1)
                at_least(pe, c_copied, q, q)
                for b in range(NB):
                    last = pe.matmul(psc[:, chunk(b)], g["sel"][:, n + NS, :],
                                     bc3[:, k * SCT + b * CH:k * SCT + (b + 1) * CH], start=True, stop=True)
                last.then_inc(c_ready, 1)

            for k in range(NSC):
                for s in range(2):
                    rows(k, NS * k + s, s, s)
                if k:
                    pe.wait_ge(gated, k)
                for h in range(NH2):
                    for b in range(NB):
                        pe.matmul(psy[:, h, chunk(b)], diag_d[:, h, :],
                                  u[:, h, k * SCT + b * CH:k * SCT + (b + 1) * CH],
                                  start=True, stop=False, skip_group_check=True)
                with pe.Fori(1, NS // 2) as i:
                    for s in range(2):
                        rows(k, 2 * i + (NS * k + s), 2 * i + s, s)
                        sum_states(2 * i + (NS * k + s - 2), s, False)
                for s in range(2):
                    sum_states(NS * (k + 1) - 2 + s, s, s == 1)

        @block.scalar
        def _(act):
            def step(k, q, n, s):
                at_least(act, scanned, q, q * NH2 - NH2)
                for h in range(NH2):
                    act.activation(decay[s][:, h, :], delta[:, h, k * SCT:(k + 1) * SCT], ACT.Exp,
                                   scale=neg_a[:, h, ds(n, 1)]).then_inc(decay_ready, 1)
                act.wait_ge(c_ready, q + 1)
                at_least(act, read_ready, q, q - 1)
                act.activation(c_rows[s][:, :], psc[:, :], ACT.Copy).then_inc(c_copied, 1)

            in_pairs(act, step)

        @block.vector
        def _(dve):
            dve.memset(carry[:, :, :], 0.0).then_inc(cleared, 1)
            dve.wait_ge(cleared, 1)

            def step(k, q, n, s):
                dve.wait_ge(b_ready, q + 1)
                at_least(dve, scanned, q, q * NH2)
                dve.tensor_tensor(drive[:, :, :], du[:, :, k * SCT:(k + 1) * SCT],
                                  psb[:, :].unsqueeze(1).broadcast_to([P, NH2, SCT]), ALU.mult).then_inc(drive_ready, 1)
                dve.wait_ge(drive_ready, q + 1)
                at_least(dve, carried, q, q - 1)
                at_least(dve, read_ready, q, q - 1)
                for h in range(NH2):
                    dve.wait_ge(decay_ready, q * NH2 + (h + 1))
                    dve.tensor_tensor_scan(state[s][:, h, :], decay[s][:, h, :], drive[:, h, :],
                                           carry[:, h, ds(n, 1)], ALU.mult, ALU.add).then_inc(scanned, 1)

            for k in range(NSC):
                for s in range(2):
                    step(k, NS * k + s, s, s)
                with dve.Fori(1, NS // 2) as i:
                    for s in range(2):
                        step(k, 2 * i + (NS * k + s), 2 * i + s, s)
                dve.wait_ge(summed, NS * (k + 1))
                dve.tensor_tensor(gate[:, :, k * SCT:(k + 1) * SCT], psy[:, :, :],
                                  gate[:, :, k * SCT:(k + 1) * SCT], ALU.mult).then_inc(gated, 1)

        @block.gpsimd
        def _(pool):
            def step(k, q, n, s):
                pool.wait_ge(scanned, q * NH2 + NH2)
                pool.tensor_copy(carry[:, :, ds(n, 1)], state[s][:, :, SCT - 1:SCT]).then_inc(carried, 1)
                pool.wait_ge(c_copied, q + 1)
                at_least(pool, summed, q, q - 1)
                pool.tensor_tensor(read[s][:, :, :], state[s][:, :, :],
                                   c_rows[s][:, :].unsqueeze(1).broadcast_to([P, NH2, SCT]),
                                   ALU.mult).then_inc(read_ready, 1)

            in_pairs(pool, step)


def mamba_out_add(nc, w, tag, x, gated):
    with ExitStack() as ctx:
        m = Memory(nc, ctx, tag)
        acc = m.ps("acc", [P, NC, CH])
        summed = m.sem("summed")
        added = m.sem("added")
        block = ctx.enter_context(nc.Block())

        @block.tensor
        def _(pe):
            for c in range(NC):
                for j in range(TPC):
                    for h in range(NH2):
                        last = pe.matmul(acc[:, c, tile(j)], gated[:, h, tile(TPC * c + j)], w["out_T"][:, h, :],
                                         start=h == 0, stop=h == NH2 - 1)
                last.then_inc(summed, 1)

        @block.vector
        def _(dve):
            for c in range(NC):
                dve.wait_ge(summed, c + 1)
                xc = x[:, TPC * c:TPC * (c + 1), :]
                dve.tensor_tensor(xc, acc[:, c, :].rearrange("p (j f) -> p j f", f=P), xc, ALU.add).then_inc(added, 1)


def mamba_out_ffn(nc, g, w, tag, x, xn, gated):
    with ExitStack() as ctx:
        m = Memory(nc, ctx, tag)
        r = m.sb("r", [P, TPC, P])
        sq = m.sb("sq", [P, TPC, P])
        ms = m.sb("ms", [P, TPC])
        rms = m.sb("rms", [P, TPC])
        hm = m.sb("hm", [P, NT, P])
        hT = m.sb("hT", [P, CH])
        act1 = m.sb("act1", [P, NF, CH])
        pso = m.ps("pso", [P, CH])
        pst = m.ps("pst", [P, CH])
        ps1 = m.ps("ps1", [P, NF, CH])
        ps2 = m.ps("ps2", [P, CH])
        o_ready = m.sem("o_ready")
        o_read = m.sem("o_read")
        h_ready = m.sem("h_ready")
        t_ready = m.sem("t_ready")
        hT_ready = m.sem("hT_ready")
        f1_ready = m.sem("f1_ready")
        gelu_done = m.sem("gelu_done")
        f2_ready = m.sem("f2_ready")
        f2_read = m.sem("f2_read")
        ms_ready = m.sem("ms_ready")
        rms_ready = m.sem("rms_ready")
        chain = m.sem("chain")
        added = m.sem("added")
        block = ctx.enter_context(nc.Block())

        @block.tensor
        def _(pe):
            def project(c):
                if c:
                    pe.wait_ge(o_read, c)
                for j in range(TPC):
                    for h in range(NH2):
                        last = pe.matmul(pso[:, tile(j)], gated[:, h, tile(TPC * c + j)], w["out_T"][:, h, :],
                                         start=h == 0, stop=h == NH2 - 1)
                last.then_inc(o_ready, 1)

            project(0)
            for c in range(NC):
                pe.wait_ge(h_ready, TPC * (c + 1))
                if c:
                    pe.wait_ge(hT_ready, c)
                for j in range(TPC):
                    last = pe.transpose(pst[:, tile(j)], hm[:, TPC * c + j, :], g["ident"][:, :])
                last.then_inc(t_ready, 1)
                pe.wait_ge(hT_ready, c + 1)
                for k in range(NF):
                    if c:
                        pe.wait_ge(gelu_done, NF * (c - 1) + k + 1)
                    pe.matmul(ps1[:, k, :], w["w1_T"][:, tile(k)], hT[:, :], start=True, stop=True).then_inc(f1_ready, 1)
                if c + 1 < NC:
                    project(c + 1)
                pe.wait_ge(gelu_done, NF * (c + 1))
                if c:
                    pe.wait_ge(f2_read, c)
                pe.matmul(ps2[:, :], g["ones_row"][:, 0:P], w["b2_rows"][:, :], start=True, stop=False, skip_group_check=True)
                for j in range(TPC):
                    for k in range(NF):
                        last = pe.matmul(ps2[:, tile(j)], act1[:, k, tile(j)], w["w2_T"][:, k, :],
                                         start=False, stop=k == NF - 1, skip_group_check=True)
                last.then_inc(f2_ready, 1)

        @block.scalar
        def _(act):
            for c in range(NC):
                act.wait_ge(t_ready, c + 1)
                if c:
                    act.wait_ge(f1_ready, NF * c)
                act.activation(hT[:, :], pst[:, :], ACT.Copy).then_inc(hT_ready, 1)
                if c:
                    act.wait_ge(f2_ready, c)
                for k in range(NF):
                    act.wait_ge(f1_ready, NF * c + k + 1)
                    act.activation(act1[:, k, :], ps1[:, k, :], ACT.Gelu, bias=w["b1"][:, k:k + 1]).then_inc(gelu_done, 1)

        @block.gpsimd
        def _(pool):
            for n in range(2 * NC):
                pool.wait_ge(ms_ready, n + 1)
                pool.tensor_tensor(rms[:, :], ms[:, :], g["minus_half"][:, 0:TPC], ALU.pow).then_inc(rms_ready, 1)

        @block.vector
        def _(dve):
            links = [0]
            norms = [0]

            def link(ins):
                links[0] += 1
                ins.then_inc(chain, 1)
                dve.wait_ge(chain, links[0])

            def rms_of_r():
                link(dve.tensor_tensor(sq[:, :, :], r[:, :, :], r[:, :, :], ALU.mult))
                link(dve.tensor_reduce(ms[:, :], sq[:, :, :], AX.X, ALU.add))
                dve.tensor_scalar(ms[:, :], ms[:, :], 1.0 / P, 1e-12, ALU.mult, ALU.add).then_inc(ms_ready, 1)
                norms[0] += 1
                dve.wait_ge(rms_ready, norms[0])

            def first(c):
                dve.wait_ge(o_ready, c + 1)
                dve.tensor_tensor(r[:, :, :], pso[:, :].rearrange("p (j f) -> p j f", f=P),
                                  xn[:, TPC * c:TPC * (c + 1), :], ALU.add).then_inc(o_read, 1)
                dve.wait_ge(o_read, c + 1)
                rms_of_r()
                for j in range(TPC):
                    dve.scalar_tensor_tensor(hm[:, TPC * c + j, :], r[:, j, :], rms[:, j:j + 1], w["norm_w"][:, :],
                                             ALU.mult, ALU.mult).then_inc(h_ready, 1)
                dve.wait_ge(h_ready, TPC * (c + 1))

            def second(c):
                dve.wait_ge(f2_ready, c + 1)
                dve.tensor_tensor(r[:, :, :], ps2[:, :].rearrange("p (j f) -> p j f", f=P),
                                  hm[:, TPC * c:TPC * (c + 1), :], ALU.add).then_inc(f2_read, 1)
                dve.wait_ge(f2_read, c + 1)
                rms_of_r()
                for j in range(TPC):
                    link(dve.scalar_tensor_tensor(r[:, j, :], r[:, j, :], rms[:, j:j + 1], w["ffn_norm_w"][:, :],
                                                  ALU.mult, ALU.mult))
                xc = x[:, TPC * c:TPC * (c + 1), :]
                dve.tensor_tensor(xc, r[:, :, :], xc, ALU.add).then_inc(added, 1)
                dve.wait_ge(added, c + 1)

            dve.wait_ge(w.loaded, w.full)
            first(0)
            for c in range(NC):
                if c + 1 < NC:
                    first(c + 1)
                second(c)


def moe(nc, g, dram, tag, x, xn):
    with ExitStack() as ctx:
        m = Memory(nc, ctx, tag)
        w = group(m, dram, "me", MOE)
        xT = m.sb("xT", [P, TOK])
        comb_T = m.sb("comb_T", [NE, TOK])
        comb3_T = m.sb("comb3_T", [SPL * NE, TOK], BF16)
        layer_norm(nc, g, tag + "ln", x, xn, xT, loads=w.loads)
        moe_gate(nc, g, w, tag + "gt", xT, comb_T, comb3_T)
        moe_experts(nc, g, w, tag + "ex", x, xT, comb_T, comb3_T)


def moe_gate(nc, g, w, tag, xT, comb_T, comb3_T):
    with ExitStack() as ctx:
        m = Memory(nc, ctx, tag)
        logits = m.sb("logits", [P, NT, NE])
        best = m.sb("best", [P, NT, 8])
        index = m.sb("index", [P, NT, 8], U32)
        index_f = m.sb("index_f", [P, NT, 2])
        gap = m.sb("gap", [P, NT, 1])
        e = m.sb("e", [P, NT, 1])
        w0 = m.sb("w0", [P, NT, 1])
        w1 = m.sb("w1", [P, NT, 1])
        is0 = m.sb("is0", [P, NT, NE])
        is1 = m.sb("is1", [P, NT, NE])
        parts = m.sb("parts", [P, NT, SPL * NE], BF16)
        psg_bank = m.ps("psg", [P, CH])
        psg = psg_bank[:, 0:NT * NE].rearrange("p (i e) -> p i e", e=NE)
        psc = m.ps("psc", [NE, NC, CH])
        psp = m.ps("psp", [SPL * NE, TOK], BF16)
        logits_ready = m.sem("logits_ready")
        maxed = m.sem("maxed")
        indexed = m.sem("indexed")
        gap_ready = m.sem("gap_ready")
        exp_done = m.sem("exp_done")
        chain = m.sem("chain")
        comb_ready = m.sem("comb_ready")
        parts_ready = m.sem("parts_ready")
        turned = m.sem("turned")
        copied = m.sem("copied")
        block = ctx.enter_context(nc.Block())

        @block.tensor
        def _(pe):
            pe.wait_ge(w.loaded, w.full)
            for i in range(NT):
                last = pe.matmul(psg[:, i, :], xT[:, tile(i)], w["g_T"][:, :], start=True, stop=True)
            last.then_inc(logits_ready, 1)
            pe.wait_ge(comb_ready, 1)
            for i in range(NT):
                last = pe.transpose(psc[:, i // TPC, tile(i % TPC)], is0[:, i, :], g["ident"][:, :])
            last.then_inc(turned, 1)
            pe.wait_ge(parts_ready, SPL)
            for i in range(NT):
                last = pe.transpose(psp[:, tile(i)], parts[:, i, :], g["ident_b"][:, :])
            last.then_inc(turned, 1)

        @block.vector
        def _(dve):
            links = [0]

            def link(ins):
                links[0] += 1
                ins.then_inc(chain, 1)
                dve.wait_ge(chain, links[0])

            def spread(col, n):
                return col.broadcast_to([P, NT, n])

            dve.wait_ge(logits_ready, 1)
            link(dve.tensor_copy(logits[:, :, :], psg[:, :, :]))
            for i in range(NT):
                dve.max(best[:, i, :], logits[:, i, :]).then_inc(maxed, 1)
            for i in range(NT):
                dve.wait_ge(maxed, i + 1)
                dve.max_index(index[:, i, :], best[:, i, :], logits[:, i, :]).then_inc(indexed, 1)
            dve.tensor_tensor(gap[:, :, :], best[:, :, 1:2], best[:, :, 0:1], ALU.subtract).then_inc(gap_ready, 1)
            dve.wait_ge(indexed, NT)
            link(dve.tensor_copy(index_f[:, :, :], index[:, :, 0:2]))
            iota = g["iota"][:, :].unsqueeze(1).broadcast_to([P, NT, NE])
            link(dve.tensor_tensor(is0[:, :, :], iota, spread(index_f[:, :, 0:1], NE), ALU.is_equal))
            link(dve.tensor_tensor(is1[:, :, :], iota, spread(index_f[:, :, 1:2], NE), ALU.is_equal))
            dve.wait_ge(exp_done, 1)
            link(dve.tensor_scalar(w1[:, :, :], e[:, :, :], 1.0, None, ALU.add))
            link(dve.reciprocal(w0[:, :, :], w1[:, :, :]))
            link(dve.tensor_tensor(w1[:, :, :], e[:, :, :], w0[:, :, :], ALU.mult))
            link(dve.tensor_tensor(is0[:, :, :], is0[:, :, :], spread(w0[:, :, :], NE), ALU.mult))
            link(dve.tensor_tensor(is1[:, :, :], is1[:, :, :], spread(w1[:, :, :], NE), ALU.mult))
            dve.tensor_tensor(is0[:, :, :], is0[:, :, :], is1[:, :, :], ALU.add).then_inc(comb_ready, 1)
            dve.wait_ge(comb_ready, 1)
            dve.tensor_copy(parts[:, :, 0:NE], is0[:, :, :]).then_inc(parts_ready, 1)
            dve.wait_ge(parts_ready, 1)
            link(dve.tensor_tensor(is1[:, :, :], is0[:, :, :], parts[:, :, 0:NE], ALU.subtract))
            dve.tensor_copy(parts[:, :, NE:2 * NE], is1[:, :, :]).then_inc(parts_ready, 1)
            dve.wait_ge(parts_ready, 2)
            dve.tensor_tensor(parts[:, :, 2 * NE:3 * NE], is1[:, :, :], parts[:, :, NE:2 * NE],
                              ALU.subtract).then_inc(parts_ready, 1)

        @block.scalar
        def _(act):
            act.wait_ge(gap_ready, 1)
            act.activation(e[:, :, :], gap[:, :, :], ACT.Exp).then_inc(exp_done, 1)
            act.wait_ge(turned, 1)
            act.activation(comb_T[:, :].rearrange("e (c t) -> e c t", t=CH), psc[:, :, :], ACT.Copy).then_inc(copied, 1)
            act.wait_ge(turned, 2)
            act.activation(comb3_T[:, :], psp[:, :], ACT.Copy).then_inc(copied, 1)


def moe_experts(nc, g, w, tag, x, xT, comb_T, comb3_T):
    with ExitStack() as ctx:
        m = Memory(nc, ctx, tag)
        SL = 4
        silu = m.sb("silu", [P, SL, CH])
        mid = m.sb("mid", [P, 2, CH])
        hid = m.sb("hid", [P, SL, CH])
        oT = m.sb("oT", [P, CH])
        psg = m.ps("psg", [P, NEF, CH])
        psv = m.ps("psv", [P, NEF, CH])
        psc = m.ps("psc", [P, CH])
        pso = m.ps("pso", [P, CH])
        pst = m.ps("pst", [P, CH])
        g_ready = m.sem("g_ready")
        v_ready = m.sem("v_ready")
        c_ready = m.sem("c_ready")
        g_free = m.sem("g_free")
        v_free = m.sem("v_free")
        hid_made = m.sem("hid_made")
        hid_free = m.sem("hid_free")
        o_free = m.sem("o_free")
        o_ready = m.sem("o_ready")
        t_ready = m.sem("t_ready")
        added = m.sem("added")
        K = NE * NEF
        x_flat = x[:, :, :].rearrange("p i f -> p (i f)")
        block = ctx.enter_context(nc.Block())

        @block.tensor
        def _(pe):
            pe.sem_inc(hid_free, SL)

            def product(c, e):
                for f in range(NEF):
                    k = NEF * e + f
                    pe.wait_ge(hid_made, c * K + (k + 2))
                    last = pe.matmul(pso[:, :], w["w3_T"][:, e, f, :], hid[:, k % SL, :], start=False,
                                     stop=k == K - 1, skip_group_check=True)
                    last.then_inc(hid_free, 1)

            def items(c, tokens, e, f):
                k = NEF * e + f
                fs = slice(f * P, (f + 1) * P)
                pe.wait_ge(g_free, c * K + (k + 1))
                pe.matmul(psg[:, f, :], w["w1_T"][:, e, fs], xT[:, tokens], start=True, stop=True).then_inc(g_ready, 1)
                pe.wait_ge(v_free, c * K + (k + 3))
                pe.matmul(psv[:, f, :], w["w2_T"][:, e, fs], xT[:, tokens], start=True, stop=True).then_inc(v_ready, 1)

            with pe.Fori(0, NC) as c:
                tokens = ds(c * CH, CH)
                for e in range(NE):
                    items(c, tokens, e, 0)
                    if e:
                        product(c, e - 1)
                    else:
                        pe.matmul(pso[:, :], w["b3"][:, :], comb_T[:, tokens], start=True, stop=False,
                                  skip_group_check=True)
                    pe.matmul(psc[:, :], g["sel_e"][:, e, :], comb3_T[:, tokens], start=True, stop=True).then_inc(c_ready, 1)
                    items(c, tokens, e, 1)
                product(c, NE - 1)
                pe.wait_ge(o_free, c + 2)
                pe.wait_ge(added, c + 1)
                for j in range(TPC):
                    last = pe.transpose(pst[:, tile(j)], oT[:, tile(j)], g["ident"][:, :])
                last.then_inc(t_ready, 1)

        @block.scalar
        def _(act):
            act.sem_inc(g_free, 2)
            act.sem_inc(o_free, 1)
            with act.Fori(0, NC) as c:
                for k in range(K):
                    e, f = divmod(k, NEF)
                    act.wait_ge(g_ready, c * K + (k + 1))
                    act.wait_ge(v_free, c * K + (k + 1))
                    act.activation(silu[:, k % SL, :], psg[:, f, :], ACT.Silu, bias=w["b1"][:, e, f:f + 1]).then_inc(g_free, 1)
                act.wait_ge(hid_free, c * K + (K + SL))
                act.wait_ge(added, c + 1)
                act.activation(oT[:, :], pso[:, :], ACT.Copy).then_inc(o_free, 1)

        @block.vector
        def _(dve):
            dve.sem_inc(v_free, SL)
            dve.sem_inc(hid_made, 1)
            dve.sem_inc(added, 1)
            with dve.Fori(0, NC) as c:
                for k in range(K):
                    e, f = divmod(k, NEF)
                    dve.wait_ge(v_ready, c * K + (k + 1))
                    dve.wait_ge(g_free, c * K + (k + 3))
                    dve.wait_ge(hid_made, c * K + (k + 1))
                    dve.scalar_tensor_tensor(mid[:, k % 2, :], psv[:, f, :], w["b2"][:, e, f:f + 1], silu[:, k % SL, :],
                                             ALU.add, ALU.mult).then_inc(v_free, 1)
                    dve.wait_ge(v_free, c * K + (k + SL + 1))
                    dve.wait_ge(c_ready, c * NE + (e + 1))
                    dve.wait_ge(hid_free, c * K + (k + 1))
                    dve.tensor_tensor(hid[:, k % SL, :], mid[:, k % 2, :], psc[:, :], ALU.mult).then_inc(hid_made, 1)
                dve.wait_ge(t_ready, c + 1)
                xc = x_flat[:, ds(c * CH, CH)]
                dve.tensor_tensor(xc, pst[:, :], xc, ALU.add).then_inc(added, 1)


def qlora_weights(nc, dram, tag, eff_all):
    with ExitStack() as ctx:
        m = Memory(nc, ctx, tag)
        w = group(m, dram, "qr", QLORA_RAW)
        psl = m.ps("psl", [P, 2, CH])
        chain = m.sem("chain")
        lora_ready = m.sem("lora_ready")
        half = QL // 2
        block = ctx.enter_context(nc.Block())

        @block.sync
        def _(sp):
            start_loads(sp, w.loads)

        @block.tensor
        def _(pe):
            pe.wait_ge(w.loaded, w.full)
            for k in range(QL):
                last = pe.matmul(psl[:, k // half, tile(k % half)], w["lora_a"][:, k, :], w["lora_b_T"][:, k, :],
                                 start=True, stop=True)
            last.then_inc(lora_ready, 1)

        @block.vector
        def _(dve):
            links = [0]

            def link(ins):
                links[0] += 1
                ins.then_inc(chain, 1)
                dve.wait_ge(chain, links[0])

            dve.wait_ge(w.loaded, w.full)
            link(dve.tensor_copy(eff_all[:, :, :], w["q_T"][:, :, :]))
            link(dve.tensor_scalar(eff_all[:, :, :], eff_all[:, :, :], 1.0 / 7.5, -1.0, ALU.mult, ALU.add))
            link(dve.tensor_tensor(eff_all[:, :, :], eff_all[:, :, :], w["scale_T"][:, :, :], ALU.mult))
            dve.wait_ge(lora_ready, 1)
            for k in range(2):
                eff = eff_all[:, half * k:half * (k + 1), :]
                link(dve.tensor_tensor(eff, psl[:, k, 0:half * P].rearrange("p (m f) -> p m f", f=P), eff, ALU.add))


def qlora_mlp(nc, g, w, tag, x, xn):
    with ExitStack() as ctx:
        m = Memory(nc, ctx, tag)
        hT = m.sb("hT", [P, TOK])
        layer_norm(nc, g, tag + "ln", x, xn, hT)
        stats = m.sb("stats", [P, TPC, 6])
        mean_var = m.sb("mean_var", [P, TPC, 2])
        var_eps = m.sb("var_eps", [P, TPC])
        rstd = m.sb("rstd", [P, TPC])
        yn = m.sb("yn", [P, 2, CH])
        act1 = m.sb("act1", [P, 2, CH])
        psy = m.ps("psy", [P, 2, CH])
        pst = m.ps("pst", [P, 2, CH])
        psz = m.ps("psz", [P, 2, CH])
        psx = m.ps("psx", [P, 2, CH])
        y_ready = m.sem("y_ready")
        stats_done = m.sem("stats_done")
        aggr_done = m.sem("aggr_done")
        var_ready = m.sem("var_ready")
        rstd_ready = m.sem("rstd_ready")
        normed = m.sem("normed")
        t_ready = m.sem("t_ready")
        gelu_done = m.sem("gelu_done")
        z_ready = m.sem("z_ready")
        h_ready = m.sem("h_ready")
        x_ready = m.sem("x_ready")
        added = m.sem("added")
        N = QL // 2 * NC
        block = ctx.enter_context(nc.Block())

        @block.tensor
        def _(pe):
            def linear(n):
                b, c = divmod(n, NC)
                if b:
                    pe.wait_ge(h_ready, n - NC + 1)
                if n >= 2:
                    pe.wait_ge(normed, TPC * (n - 1))
                pe.matmul(psy[:, n % 2, :], g["ones_row"][:, 0:P], w["bias_rows"][:, b, :], start=True, stop=False,
                          skip_group_check=True)
                for j in range(TPC):
                    last = pe.matmul(psy[:, n % 2, tile(j)], hT[:, tile(TPC * c + j)], w["eff"][:, 2 * b, :],
                                     start=False, stop=True, skip_group_check=True)
                last.then_inc(y_ready, 1)

            def turn(n):
                if n >= 2:
                    pe.wait_ge(gelu_done, n - 1)
                for j in range(TPC):
                    pe.wait_ge(normed, TPC * n + j + 1)
                    last = pe.transpose(pst[:, n % 2, tile(j)], yn[:, n % 2, tile(j)], g["ident"][:, :])
                last.then_inc(t_ready, 1)

            def linear2(n):
                pe.wait_ge(gelu_done, n + 1)
                if n >= 2:
                    pe.wait_ge(h_ready, n - 1)
                pe.matmul(psz[:, n % 2, :], w["eff"][:, 2 * (n // NC) + 1, :], act1[:, n % 2, :],
                          start=True, stop=True).then_inc(z_ready, 1)

            for n in range(N + 2):
                if n < N:
                    linear(n)
                if 1 <= n <= N:
                    turn(n - 1)
                if n >= 2:
                    linear2(n - 2)
            for c in range(NC):
                pe.wait_ge(h_ready, N - NC + c + 1)
                if c >= 2:
                    pe.wait_ge(added, c - 1)
                for j in range(TPC):
                    last = pe.transpose(psx[:, c % 2, tile(j)], hT[:, tile(TPC * c + j)], g["ident"][:, :])
                last.then_inc(x_ready, 1)

        @block.vector
        def _(dve):
            def norm(n):
                dve.wait_ge(y_ready, n + 1)
                if n:
                    dve.wait_ge(aggr_done, TPC * n)
                for j in range(TPC):
                    dve.bn_stats(stats[:, j, :], psy[:, n % 2, tile(j)]).then_inc(stats_done, 1)
                if n:
                    dve.wait_ge(normed, TPC * n)
                for j in range(TPC):
                    dve.wait_ge(stats_done, TPC * n + j + 1)
                    dve.bn_aggr(mean_var[:, j, :], stats[:, j, :]).then_inc(aggr_done, 1)
                dve.wait_ge(aggr_done, TPC * (n + 1))
                dve.tensor_scalar(var_eps[:, :], mean_var[:, :, 1], 1e-5, None, ALU.add).then_inc(var_ready, 1)
                if n >= 2:
                    dve.wait_ge(t_ready, n - 1)
                dve.wait_ge(rstd_ready, n + 1)
                for j in range(TPC):
                    dve.tensor_scalar(yn[:, n % 2, tile(j)], psy[:, n % 2, tile(j)], mean_var[:, j, 0:1],
                                      rstd[:, j:j + 1], ALU.subtract, ALU.mult).then_inc(normed, 1)

            def residual(n):
                b, c = divmod(n, NC)
                dve.wait_ge(z_ready, n + 1)
                if b:
                    dve.wait_ge(h_ready, n - NC + 1)
                dve.scalar_tensor_tensor(hT[:, chunk(c)], psz[:, n % 2, :], w["bias_cols"][:, 2 * b + 1:2 * b + 2],
                                         hT[:, chunk(c)], ALU.add, ALU.add).then_inc(h_ready, 1)

            for n in range(N + 2):
                if n < N:
                    norm(n)
                if n >= 2:
                    residual(n - 2)
            for c in range(NC):
                dve.wait_ge(x_ready, c + 1)
                xc = x[:, TPC * c:TPC * (c + 1), :]
                dve.tensor_tensor(xc, psx[:, c % 2, :].rearrange("p (j f) -> p j f", f=P), xc, ALU.add).then_inc(added, 1)

        @block.gpsimd
        def _(pool):
            for n in range(N):
                pool.wait_ge(var_ready, n + 1)
                pool.tensor_tensor(rstd[:, :], var_eps[:, :], g["minus_half"][:, 0:TPC], ALU.pow).then_inc(rstd_ready, 1)

        @block.scalar
        def _(act):
            for n in range(N):
                act.wait_ge(t_ready, n + 1)
                if n >= 2:
                    act.wait_ge(z_ready, n - 1)
                act.activation(act1[:, n % 2, :], pst[:, n % 2, :], ACT.Gelu, bias=w["beta"][:, n // NC:n // NC + 1],
                               scale=w["gamma"][:, n // NC:n // NC + 1]).then_inc(gelu_done, 1)


def attention(nc, g, w, tag, dram, x, xn, alibi):
    with ExitStack() as ctx:
        m = Memory(nc, ctx, tag)
        v = m.sb("v", [P, NT, P])
        q_dram = nc.dram_tensor(tag + "_q_parts", (SPL, P, TOK), BF16, kind="Internal").ap()
        k_dram = nc.dram_tensor(tag + "_k_parts", (HEADS, SPL * DH, TOK), BF16, kind="Internal").ap()
        o_dram = nc.dram_tensor(tag + "_outputs", (4, HEADS, DH + 1, TOK), F32, kind="Internal").ap()
        with ExitStack() as inner:
            xT = Memory(nc, inner, tag).sb("xT", [P, TOK])
            if alibi:
                layer_norm(nc, g, tag + "ln", x, xn, xT)
            else:
                layer_norm(nc, g, tag + "ln", x, xn, xT, rounds=2, w=w)
            attention_project(nc, w, tag + "pr", xT, v, q_dram, k_dram)
        attention_heads(nc, g, tag + "hd", dram, q_dram, k_dram, v, o_dram, alibi)
        attention_out(nc, g, w, tag + "ou", x, o_dram)


def attention_project(nc, w, tag, xT, v, q_dram, k_dram):
    with ExitStack() as ctx:
        m = Memory(nc, ctx, tag)
        full = [m.sb(n, [P, TOK]) for n in ("q", "k")]
        parts = [m.sb(n, [P, SPL, TOK], BF16) for n in ("q_parts", "k_parts")]
        acc = m.ps("acc", [P, 8, CH])
        projected = m.sem("projected")
        copied = m.sem("copied")
        first_part = m.sem("first_part")
        split = [m.sem("split_q"), m.sem("split_k")]
        stored = m.sem("stored")
        block = ctx.enter_context(nc.Block())

        @block.tensor
        def _(pe):
            pe.wait_ge(w.loaded, w.full)
            for n, wt in enumerate((w["wq"], w["wk"])):
                for c in range(NC):
                    pe.matmul(acc[:, NC * n + c, :], wt[:, :], xT[:, chunk(c)], start=True, stop=True).then_inc(projected, 1)
            for c in range(NC):
                pe.wait_ge(first_part, c + 1)
                for j in range(TPC):
                    last = pe.matmul(acc[:, c, tile(j)], xT[:, tile(TPC * c + j)], w["wv"][:, :], start=True, stop=True)
                last.then_inc(projected, 1)

        @block.scalar
        def _(act):
            for n in range(2 * NC):
                o, c = divmod(n, NC)
                scale = float(DH) ** -0.5 if o == 0 else 1.0
                act.wait_ge(projected, n + 1)
                act.activation(full[o][:, chunk(c)], acc[:, n, :], ACT.Copy, scale=scale).then_inc(copied, 1)
                act.activation(parts[o][:, 0, chunk(c)], acc[:, n, :], ACT.Copy, scale=scale).then_inc(first_part, 1)
            for c in range(NC):
                act.wait_ge(projected, 2 * NC + c + 1)
                act.activation(v[:, TPC * c:TPC * (c + 1), :], acc[:, c, :].rearrange("p (j f) -> p j f", f=P),
                               ACT.Copy).then_inc(copied, 1)

        def split_parts(eng, o):
            for c in range(NC):
                r = full[o][:, chunk(c)]
                eng.wait_ge(copied, NC * o + c + 1)
                eng.wait_ge(first_part, NC * o + c + 1)
                eng.tensor_tensor(r, r, parts[o][:, 0, chunk(c)], ALU.subtract).then_inc(split[o], 1)
                eng.wait_ge(split[o], 3 * c + 1)
                eng.tensor_copy(parts[o][:, 1, chunk(c)], r).then_inc(split[o], 1)
                eng.wait_ge(split[o], 3 * c + 2)
                eng.tensor_tensor(parts[o][:, 2, chunk(c)], r, parts[o][:, 1, chunk(c)], ALU.subtract).then_inc(split[o], 1)

        @block.gpsimd
        def _(pool):
            split_parts(pool, 0)

        @block.vector
        def _(dve):
            split_parts(dve, 1)

        @block.sync
        def _(sp):
            for c in range(NC):
                sp.wait_ge(split[1], 3 * (c + 1))
                for s in range(SPL):
                    sp.dma_start(k_dram[:, s * DH:(s + 1) * DH, chunk(c)], parts[1][:, s, chunk(c)]).then_inc(stored, 16)
                sp.wait_ge(split[0], 3 * (c + 1))
                sp.dma_start(q_dram[:, :, chunk(c)].rearrange("s p t -> p s t"), parts[0][:, :, chunk(c)]).then_inc(stored, 16)
            sp.wait_ge(stored, 16 * (SPL + 1) * NC)


def attention_heads(nc, g, tag, dram, q_dram, k_dram, v, o_dram, alibi):
    with ExitStack() as ctx:
        m = Memory(nc, ctx, tag)
        NR = PAIRS + (ALIBI if alibi else 0)
        NR_MAX = NR + SPL
        SLOT = 4
        PSLOT = 4
        LEAD = 16
        TURN = 4
        q_op = [m.sb(f"q_op{s}", [NR_MAX, TOK], BF16) for s in range(SLOT)]
        k_op = [m.sb(f"k_op{s}", [NR_MAX, TOK], BF16) for s in range(SLOT)]
        vh = [m.sb(f"vh{s}", [P, NT, 32]) for s in range(SLOT)]
        probs = m.sb("probs", [P, PSLOT, 2 * CH])
        maxes = m.sb("maxes", [P, NT, NC])
        neg_max = m.sb("neg_max", [P, NT])
        max_parts = m.sb("max_parts", [P, P], BF16)
        max_T = m.sb("max_T", [SPL * NT, P], BF16)
        o_sb = m.sb("o_sb", [P, 2, CH])
        ps_k = m.ps("ps_k", [P, 2, 2 * CH])
        ps_q = m.ps("ps_q", [P, 2, CH])
        ps_o = m.ps("ps_o", [P, 2, CH])
        op_loaded = [m.sem(f"op_loaded{s}") for s in range(SLOT)]
        max_loaded = [m.sem(f"max_loaded{s}") for s in range(SLOT)]
        ones_loaded = m.sem("ones_loaded")
        v_set = m.sem("v_set")
        v_ready = m.sem("v_ready")
        q_ready = m.sem("q_ready")
        q_read = m.sem("q_read")
        max_set = m.sem("max_set")
        max_ready = m.sem("max_ready")
        chain = m.sem("chain")
        k_ready = m.sem("k_ready")
        exp_done = m.sem("exp_done")
        pv_done = m.sem("pv_done")
        o_read = m.sem("o_read")
        o_stored = [m.sem(f"o_stored{s}") for s in range(2)]
        OPS = SPL + 1 + (2 if alibi else 0)
        STORES = 4

        q_items = [(t, kc) for t in range(NT) for kc in range(t // TPC + 1)]
        NQ = len(q_items)

        groups = []
        for c in range(NC):
            rows = [(j, 0, CH) for j in range(TPC * c)]
            rows += [(TPC * c + d, d * P if c else 0, CH - d * P if c else CH) for d in range(TPC)]
            groups += [(c, rows[i:i + 2]) for i in range(0, len(rows), 2)]
        NG = len(groups)
        ends = [max(i for i, (cc, _) in enumerate(groups) if cc == c) for c in range(NC)]
        assert NG % 4 == 0 and 2 * NG == NQ and ends[0] == 1

        def number(i, k):
            return i * SLOT + k

        def use(i, k):
            return i + (k // SLOT + 1)

        def beyond(i, k, n=HEADS):
            return isinstance(i, int) and number(i, k) >= n

        def q_index(i, k, n):
            if isinstance(i, int) and number(i, k) == 0:
                return n
            return number(i, k) * (NQ + 1) + (n + (n >= TURN) - 1)

        def turn_index(i, k):
            if beyond(i, k, HEADS - 1):
                return HEADS * (NQ + 1) - 1
            return number(i, k) * (NQ + 1) + (NQ + TURN)

        def stream(turn, item, i, k, p):
            k, n = k + 1 + p // NQ, p % NQ
            if n == TURN and not beyond(i, k, HEADS + 1):
                turn(i, k - 1)
            if not beyond(i, k):
                item(i, k, n)

        def prologue(turn, item):
            for n in range(NQ):
                item(0, 0, n)
            for p in range(LEAD):
                stream(turn, item, 0, 0, p)

        def heads(eng, body):
            with eng.Fori(0, HEADS // SLOT - 1) as i:
                for k in range(SLOT):
                    body(i, k)
            for k in range(SLOT):
                body(HEADS // SLOT - 1, k)

        def turned_bank(k):
            par = turn_index(0, k) % 2
            return ps_q[:, par, 0:P // 2].bitcast(BF16)

        block = ctx.enter_context(nc.Block())

        @block.tensor
        def _(pe):
            pe.sem_inc(pv_done, PSLOT)

            def turn(i, k):
                pe.wait_ge(max_ready, number(i, k) + 1)
                pe.wait_ge(q_read, turn_index(i, k) - 1)
                pe.transpose(turned_bank(k), max_parts[:, :], g["ident_b"][:, :]).then_inc(q_ready, 1)

            def item(i, k, n):
                t, kc = q_items[n]
                place = q_index(i, k, n)
                par = q_index(0, k, n) % 2
                width = min(CH, (t + 1) * P - kc * CH)
                if n == 0:
                    pe.wait_ge(op_loaded[k % SLOT], use(i, k) * (16 * OPS))
                if not isinstance(place, int) or place >= 2:
                    pe.wait_ge(q_read, place - 1)
                diagonal = kc == t // TPC
                last = pe.matmul(ps_q[:, par, 0:width], q_op[k % SLOT][0:NR, tile(t)],
                                 k_op[k % SLOT][0:NR, kc * CH:kc * CH + width], start=True, stop=not diagonal,
                                 skip_group_check=True)
                if diagonal:
                    last = pe.matmul(ps_q[:, par, width - P:width], g["ident_b"][:, :], g["mask_q"][:, :],
                                     start=False, stop=True, skip_group_check=True)
                last.then_inc(q_ready, 1)

            def scores(i, k, gi):
                c, rows = groups[gi]
                if gi == 0:
                    pe.wait_ge(max_loaded[k % SLOT], use(i, k) * 16)
                pe.wait_ge(exp_done, number(i, k) * NG + (gi + 1))
                at = 0
                for j, first, width in rows:
                    d = j - TPC * c
                    last = pe.matmul(ps_k[:, gi % 2, at:at + width], k_op[k % SLOT][:, tile(j)],
                                     q_op[k % SLOT][:, c * CH + first:c * CH + first + width], start=True, stop=d < 0,
                                     skip_group_check=True)
                    if d >= 0:
                        m0 = ((TPC - 1 - d) if c == 0 else (TPC - 1)) * P
                        last = pe.matmul(ps_k[:, gi % 2, at:at + TPC * P - m0], g["ident_b"][:, :],
                                         g["mask_k"][:, m0:TPC * P], start=False, stop=True, skip_group_check=True)
                    at += width
                last.then_inc(k_ready, 1)

            def times_v(i, k, gi):
                c, rows = groups[gi]
                if gi == 0:
                    pe.wait_ge(v_ready, number(i, k) + 1)
                if gi == 0 or gi - 1 in ends:
                    pe.wait_ge(o_read, number(i, k) * NC + (c + 1))
                pe.wait_ge(exp_done, number(i, k) * NG + (gi + 3))
                at = 0
                for j, first, width in rows:
                    r = 32 * (j % 4)
                    last = pe.matmul(ps_o[r:r + 32, c % 2, first:first + width], vh[k % SLOT][:, j, :],
                                     probs[:, gi % PSLOT, at:at + width], start=j < 4, stop=j >= TPC * c,
                                     skip_group_check=True)
                    at += width
                last.then_inc(pv_done, 1)

            def body(i, k):
                for gi in range(NG):
                    if gi + 2 < NG:
                        scores(i, k, gi + 2)
                    elif not beyond(i, k + 1):
                        scores(i, k + 1, gi + 2 - NG)
                    times_v(i, k, gi)
                    for p in (2 * gi + LEAD, 2 * gi + LEAD + 1):
                        stream(turn, item, i, k, p)

            prologue(turn, item)
            scores(0, 0, 0)
            scores(0, 0, 1)
            heads(pe, body)

        @block.vector
        def _(dve):
            dve.memset(max_parts[:, :], 0.0).then_inc(max_set, 1)
            dve.memset(maxes[:, :, :], -3e38).then_inc(max_set, 1)
            dve.wait_ge(max_set, 2)

            def turn(i, k):
                dve.wait_ge(q_ready, turn_index(i, k) + 1)
                dve.tensor_copy(max_T[:, :], turned_bank(k)[0:SPL * NT, :]).then_inc(q_read, 1)

            def item(i, k, n):
                t, kc = q_items[n]
                par = q_index(0, k, n) % 2
                width = min(CH, (t + 1) * P - kc * CH)
                dve.wait_ge(q_ready, q_index(i, k, n) + 1)
                dve.tensor_reduce(maxes[:, t, kc:kc + 1], ps_q[:, par, 0:width], AX.X, ALU.max).then_inc(q_read, 1)
                if n == NQ - 1:
                    maxima(i, k)

            def maxima(i, k):
                def part(s):
                    return max_parts[:, s * NT:(s + 1) * NT]

                done = number(i, k) * 5
                dve.wait_ge(q_read, q_index(i, k, NQ - 1) + 1)
                dve.tensor_reduce(neg_max[:, :], maxes[:, :, :], AX.X, ALU.max, negate=True).then_inc(chain, 1)
                dve.wait_ge(chain, done + 1)
                dve.tensor_copy(part(0), neg_max[:, :]).then_inc(chain, 1)
                dve.wait_ge(chain, done + 2)
                dve.tensor_tensor(neg_max[:, :], neg_max[:, :], part(0), ALU.subtract).then_inc(chain, 1)
                dve.wait_ge(chain, done + 3)
                dve.tensor_copy(part(1), neg_max[:, :]).then_inc(chain, 1)
                dve.wait_ge(chain, done + 4)
                dve.tensor_tensor(neg_max[:, :], neg_max[:, :], part(1), ALU.subtract).then_inc(chain, 1)
                dve.wait_ge(chain, done + 5)
                dve.tensor_copy(part(2), neg_max[:, :]).then_inc(max_ready, 1)
                dve.wait_ge(max_ready, number(i, k) + 1)

            def body(i, k):
                for gi in range(NG):
                    for p in (2 * gi + LEAD, 2 * gi + LEAD + 1):
                        stream(turn, item, i, k, p)

            prologue(turn, item)
            heads(dve, body)

        @block.scalar
        def _(act):
            act.sem_inc(exp_done, 2)
            act.sem_inc(o_read, 2)
            AHEAD = 3

            def exps(i, k, gi):
                c, rows = groups[gi]
                width = sum(r[2] for r in rows)
                act.wait_ge(k_ready, number(i, k) * NG + (gi + 1))
                act.wait_ge(pv_done, number(i, k) * NG + (gi + 1))
                act.activation(probs[:, gi % PSLOT, 0:width], ps_k[:, gi % 2, 0:width], ACT.Exp).then_inc(exp_done, 1)

            def output(i, k, c):
                act.wait_ge(pv_done, number(i, k) * NG + (ends[c] + 1 + PSLOT))
                act.wait_ge(o_stored[c % 2], number(i, k) * (2 * 16 * STORES) + (c // 2 * 16 * STORES + 16))
                act.activation(o_sb[:, c % 2, :], ps_o[:, c % 2, :], ACT.Copy).then_inc(o_read, 1)

            def body(i, k):
                for gi in range(AHEAD, NG):
                    exps(i, k, gi)
                    if gi - AHEAD in ends:
                        output(i, k, ends.index(gi - AHEAD))
                if not beyond(i, k + 1):
                    for gi in range(AHEAD):
                        exps(i, k + 1, gi)
                output(i, k, NC - 1)

            for gi in range(AHEAD):
                exps(0, 0, gi)
            heads(act, body)

        @block.gpsimd
        def _(pool):
            for s in range(SLOT):
                pool.memset(vh[s][:, :, :], 0.0).then_inc(v_set, 1)
            pool.wait_ge(v_set, SLOT)
            for s in range(SLOT):
                pool.memset(vh[s][:, :, DH:DH + 1], 1.0).then_inc(v_set, 1)
            pool.wait_ge(v_set, 2 * SLOT)

            def place(i, k):
                pool.tensor_copy(vh[k][:, :, 0:DH], v[:, :, ds(number(i, k) * DH, DH)]).then_inc(v_ready, 1)

            for k in range(SLOT):
                place(0, k)
            with pool.Fori(1, HEADS // SLOT) as i:
                for k in range(SLOT):
                    pool.wait_ge(pv_done, number(i, k - 3) * NG + PSLOT)
                    place(i, k)

        @block.sync
        def _(sp):
            for s in range(2):
                sp.sem_inc(o_stored[s], 16)

            def load(i, k):
                h = number(i, k)
                s = k % SLOT
                PER = SPL * DH
                for a in range(SPL):
                    sp.dma_start(q_op[s][a * PER:(a + 1) * PER, :],
                                 q_dram[a, ds(h * DH, DH), :].unsqueeze(0).broadcast_to([SPL, DH, TOK])).then_inc(op_loaded[s], 16)
                sp.dma_start(k_op[s][0:PAIRS, :],
                             k_dram[ds(h, 1), :, :].broadcast_to([SPL, PER, TOK])).then_inc(op_loaded[s], 16)
                if alibi:
                    sp.dma_start(q_op[s][PAIRS:NR, :], dram["alibi_q"][ds(h, 1), :, :].rearrange("o r t -> (o r) t")).then_inc(op_loaded[s], 16)
                    sp.dma_start(k_op[s][PAIRS:NR, :], dram["alibi_k"][ds(h, 1), :, :].rearrange("o r t -> (o r) t")).then_inc(op_loaded[s], 16)

            def load_maxima(i, k):
                sp.wait_ge(q_read, turn_index(i, k) + 1)
                sp.dma_start(q_op[k % SLOT][NR:NR_MAX, :].rearrange("s (t p) -> s t p", p=P),
                             max_T[:, :]).then_inc(max_loaded[k % SLOT], 16)

            def store(i, k, c):
                h = number(i, k)
                sp.wait_ge(o_read, h * NC + (c + 3))
                for r in range(4):
                    sp.dma_start(o_dram[r, ds(h, 1), :, chunk(c)], o_sb[32 * r:32 * r + DH + 1, c % 2, :]).then_inc(o_stored[c % 2], 16)

            for k in range(SLOT):
                sp.dma_start(k_op[k][NR:NR_MAX, :], dram["ones_b"]).then_inc(ones_loaded, 16)
            sp.wait_ge(ones_loaded, 16 * SLOT)
            for k in range(SLOT):
                load(0, k)
            load_maxima(0, 0)

            def body(i, k):
                for c in range(NC - 1):
                    store(i, k, c)
                if not beyond(i, k + 1):
                    load_maxima(i, k + 1)
                if not beyond(i, k + SLOT):
                    sp.wait_ge(k_ready, number(i, k + 1) * NG)
                    load(i, k + SLOT)
                store(i, k, NC - 1)

            heads(sp, body)
            for s in range(2):
                sp.wait_ge(o_stored[s], 16 + HEADS * 2 * 16 * STORES)


def attention_out(nc, g, w, tag, x, o_dram):
    with ExitStack() as ctx:
        m = Memory(nc, ctx, tag)
        oT = m.sb("oT", [P, 4, TOK])
        sums = m.sb("sums", [4 * HEADS, TOK])
        inv = m.sb("inv", [P, 2, CH])
        total = m.sb("total", [P, 2, CH])
        upper = m.sb("upper", [P, 2, CH])
        ps_s = m.ps("ps_s", [P, 2, CH])
        ps_y = m.ps("ps_y", [P, 2, CH])
        sums_loaded = m.sem("sums_loaded")
        o_loaded = [m.sem(f"o_loaded{c}") for c in range(NC)]
        sum_ready = m.sem("sum_ready")
        inverted = m.sem("inverted")
        upper_ready = m.sem("upper_ready")
        lower_ready = m.sem("lower_ready")
        total_ready = m.sem("total_ready")
        normed = m.sem("normed")
        y_ready = m.sem("y_ready")
        added = m.sem("added")
        block = ctx.enter_context(nc.Block())

        @block.tensor
        def _(pe):
            pe.wait_ge(sums_loaded, 16)

            def spread(c):
                if c >= 2:
                    pe.wait_ge(inverted, c - 1)
                pe.matmul(ps_s[:, c % 2, :], g["sel_sum"][:, :], sums[:, chunk(c)], start=True, stop=True).then_inc(sum_ready, 1)

            spread(0)
            for c in range(NC):
                if c + 1 < NC:
                    spread(c + 1)
                pe.wait_ge(normed, c + 1)
                if c >= 2:
                    pe.wait_ge(added, c - 1)
                for j in range(TPC):
                    last = pe.matmul(ps_y[:, c % 2, tile(j)], total[:, c % 2, tile(j)], w["wo"][:, :], start=True, stop=True)
                last.then_inc(y_ready, 1)

        @block.sync
        def _(sp):
            sp.dma_start(sums[:, :], o_dram[:, :, DH, :]).then_inc(sums_loaded, 16)
            for c in range(NC):
                for r in range(4):
                    sp.dma_start(oT[:, r, chunk(c)], o_dram[r, :, 0:DH, chunk(c)]).then_inc(o_loaded[c], 16)

        @block.gpsimd
        def _(pool):
            for c in range(NC):
                pool.wait_ge(o_loaded[c], 16 * 4)
                if c >= 2:
                    pool.wait_ge(total_ready, c - 1)
                pool.tensor_tensor(upper[:, c % 2, :], oT[:, 2, chunk(c)], oT[:, 3, chunk(c)], ALU.add).then_inc(upper_ready, 1)

        @block.vector
        def _(dve):
            def add(c):
                dve.wait_ge(y_ready, c + 1)
                xc = x[:, TPC * c:TPC * (c + 1), :]
                dve.tensor_tensor(xc, ps_y[:, c % 2, :].rearrange("p (j f) -> p j f", f=P), xc, ALU.add).then_inc(added, 1)

            for c in range(NC):
                s = c % 2
                dve.wait_ge(sum_ready, c + 1)
                if c >= 2:
                    dve.wait_ge(normed, c - 1)
                    dve.wait_ge(y_ready, c - 1)
                dve.reciprocal(inv[:, s, :], ps_s[:, s, :]).then_inc(inverted, 1)
                dve.wait_ge(o_loaded[c], 16 * 4)
                dve.tensor_tensor(total[:, s, :], oT[:, 0, chunk(c)], oT[:, 1, chunk(c)], ALU.add).then_inc(lower_ready, 1)
                dve.wait_ge(lower_ready, c + 1)
                dve.wait_ge(upper_ready, c + 1)
                dve.tensor_tensor(total[:, s, :], total[:, s, :], upper[:, s, :], ALU.add).then_inc(total_ready, 1)
                dve.wait_ge(total_ready, c + 1)
                dve.wait_ge(inverted, c + 1)
                dve.tensor_tensor(total[:, s, :], total[:, s, :], inv[:, s, :], ALU.mult).then_inc(normed, 1)
                if c:
                    add(c - 1)
            add(NC - 1)


MAMBA = ["in_T", "conv_w", "conv_b", "x_T", "dt_T", "dt_b", "a_log", "d", "out_T"]
MAMBA_FFN = ["w1_T", "b1", "w2_T", "b2_rows", "norm_w", "ffn_norm_w"]
MOE = ["g_T", "b1", "b2", "b3", "w1_T", "w2_T", "w3_T"]
QLORA = ["bias_rows", "bias_cols", "gamma", "beta"]
QLORA_RAW = ["q_T", "scale_T", "lora_a", "lora_b_T"]
ATT0 = ["wq", "wk", "wv", "wo", "gain"]
ATT1 = ["wq", "wk", "wv", "wo"]
CONST = ["ident", "ident_b", "ones_row", "sel", "sel_e", "iota", "minus_half", "mask_q", "mask_k", "sel_sum"]


def build(nc, dram, out, steps=8):
    Memory.count = 0
    with ExitStack() as ctx:
        m = Memory(nc, ctx, "all")
        x = m.sb("x", [P, NT, P])
        xn = m.sb("xn", [P, NT, P])
        x_loaded = m.sem("x_loaded")
        stored = m.sem("stored")
        g = group(m, dram, "c", CONST)
        m0 = group(m, dram, "m0", MAMBA + MAMBA_FFN)
        a0 = group(m, dram, "a0", ATT0)
        m1 = group(m, dram, "m1", MAMBA)
        ql = group(m, dram, "ql", QLORA)
        a1 = group(m, dram, "a1", ATT1)
        ql["eff"] = m.sb("ql_eff", [P, QL, P])

        with nc.Block() as block:
            @block.sync
            def _(sp):
                start_loads(sp, [(x, dram["x"], x_loaded)] + g.loads + m0.loads + a0.loads + m1.loads + ql.loads + a1.loads)
                sp.wait_ge(x_loaded, 16)
                sp.wait_ge(g.loaded, g.full)

        plan = [
            lambda: mamba(nc, g, m0, "m0", x, xn, lambda gated: mamba_out_ffn(nc, g, m0, "m0o", x, xn, gated)),
            lambda: moe(nc, g, dram, "e0", x, xn),
            lambda: attention(nc, g, a0, "a0", dram, x, xn, False),
            lambda: moe(nc, g, dram, "e1", x, xn),
            lambda: mamba(nc, g, m1, "m1", x, xn, lambda gated: mamba_out_add(nc, m1, "m1o", x, gated)),
            lambda: (qlora_weights(nc, dram, "qw", ql["eff"]), qlora_mlp(nc, g, ql, "q0", x, xn)),
            lambda: attention(nc, g, a1, "a1", dram, x, xn, True),
            lambda: qlora_mlp(nc, g, ql, "q1", x, xn),
        ]
        for n in (range(steps) if isinstance(steps, int) else steps):
            with fresh_semaphores(nc):
                plan[n]()
        with nc.Block() as block:
            @block.sync
            def _(sp):
                sp.dma_start(out, x[:, :, :]).then_inc(stored, 16)
                for w in (m0, a0, m1, ql, a1):
                    sp.wait_ge(w.loaded, w.full)
                sp.wait_ge(stored, 16)


def constants():
    bf = mybir.dt.np(BF16)
    k, q = np.arange(P)[:, None], np.arange(P)[None, :]
    sel = np.zeros((SPL, 2 * NS, 2 * NS, P), np.float32)
    for n in range(2 * NS):
        sel[:, n, n] = 1
    sel_e = np.zeros((SPL, NE, NE, P), np.float32)
    for n in range(NE):
        sel_e[:, n, n] = 1
    sel_sum = np.zeros((4, HEADS, HEADS, DH), np.float32)
    for h in range(HEADS):
        sel_sum[:, h, h] = 1
    slopes = (2.0 ** (-8.0 / HEADS * (np.arange(HEADS, dtype=np.float32) + 1.0))).astype(np.float32)
    pos = np.arange(TOK)
    hi, lo = (pos // P * P).astype(np.float32), (pos % P).astype(np.float32)
    qa, ka = np.zeros((HEADS, ALIBI, TOK), np.float32), np.zeros((HEADS, ALIBI, TOK), np.float32)
    rest = slopes.copy()
    for s in range(SPL):
        part = rest.astype(bf).astype(np.float32)
        rest = rest - part
        for r, p in enumerate((hi, lo)):
            row = 4 * s + 2 * r
            qa[:, row], ka[:, row] = part[:, None], p
            qa[:, row + 1], ka[:, row + 1] = p, -part[:, None]
    return {
        "c_ident": np.eye(P, dtype=np.float32),
        "c_ident_b": np.eye(P, dtype=np.float32).astype(bf),
        "c_ones_row": np.ones((1, P), np.float32),
        "c_sel": sel.reshape(SPL * 2 * NS, 2 * NS, P).astype(bf),
        "c_sel_e": sel_e.reshape(SPL * NE, NE, P).astype(bf),
        "c_iota": np.tile(np.arange(NE, dtype=np.float32), (P, 1)),
        "c_minus_half": np.full((P, NT), -0.5, np.float32),
        "c_mask_q": np.where(q > k, NEG, 0.0).astype(bf),
        "c_mask_k": np.concatenate([np.full((P, 3 * P), NEG), np.where(k > q, NEG, 0.0)], 1).astype(bf),
        "c_sel_sum": sel_sum.reshape(4 * HEADS, P),
        "alibi_q": qa.astype(bf),
        "alibi_k": ka.astype(bf),
        "ones_b": np.ones((SPL, TOK), np.float32).astype(bf),
    }


def layouts(i):
    def halves(a):
        return a.reshape((a.shape[0] // P, P) + a.shape[1:]).swapaxes(0, 1)

    def rows(a):
        return np.broadcast_to(a, (P, P))

    r = {"x": i["L0_attn_a_input_tensor"][0].reshape(NT, P, P).swapaxes(0, 1)}
    a = {k[len("L0_attn_a_"):]: v for k, v in i.items() if k.startswith("L0_attn_a_")}
    r.update({
        "m0_in_T": a["in_proj_w"].T, "m0_conv_w": halves(a["conv_w"]), "m0_conv_b": halves(a["conv_b"]),
        "m0_x_T": halves(a["x_proj_w"].T), "m0_dt_T": a["dt_proj_w"].T, "m0_dt_b": halves(a["dt_proj_b"]),
        "m0_a_log": halves(a["A_log"]), "m0_d": halves(a["D"]), "m0_out_T": halves(a["out_proj_w"].T),
        "m0_w1_T": a["ffn_w1"].T, "m0_b1": halves(a["ffn_b1"]), "m0_w2_T": halves(a["ffn_w2"].T),
        "m0_b2_rows": np.tile(a["ffn_b2"], TPC)[None], "m0_norm_w": rows(a["norm_w"]),
        "m0_ffn_norm_w": rows(a["ffn_norm_w"]),
    })
    a = {k[len("L1_attn_a_"):]: v for k, v in i.items() if k.startswith("L1_attn_a_")}
    r.update({
        "m1_in_T": a["W_in"], "m1_conv_w": halves(a["conv_w"]), "m1_conv_b": halves(a["conv_b"]),
        "m1_x_T": halves(a["W_x"]), "m1_dt_T": a["W_dt"], "m1_dt_b": halves(a["b_dt"]),
        "m1_a_log": halves(a["A_log"]), "m1_d": halves(a["D"]), "m1_out_T": halves(a["W_out"]),
    })
    a = {k[len("L0_ffn_"):]: v for k, v in i.items() if k.startswith("L0_ffn_")}
    r.update({
        "me_g_T": a["Wg"].T, "me_w1_T": a["W1"].transpose(2, 0, 1), "me_w2_T": a["W2"].transpose(2, 0, 1),
        "me_w3_T": halves(a["W3"].transpose(2, 0, 1)).transpose(0, 2, 1, 3),
        "me_b1": halves(a["b1"].T).transpose(0, 2, 1), "me_b2": halves(a["b2"].T).transpose(0, 2, 1), "me_b3": a["b3"],
    })
    wkv = i["L0_attn_b_Wkv"]
    r.update({"a0_wq": i["L0_attn_b_Wq"], "a0_wk": wkv[:, :P], "a0_wv": wkv[:, P:], "a0_wo": i["L0_attn_b_Wo"],
              "a0_gain": i["L0_attn_b_g_ln"][:, None]})
    w_in = i["L1_attn_b_w_in"]
    r.update({"a1_wq": w_in[:P].T, "a1_wk": w_in[P:2 * P].T, "a1_wv": w_in[2 * P:].T, "a1_wo": i["L1_attn_b_w_out"].T})
    a = {k[len("L1_ffn_"):]: v for k, v in i.items() if k.startswith("L1_ffn_")}
    r.update({
        "qr_q_T": a["qweights"].transpose(2, 0, 1),
        "qr_scale_T": np.repeat(a["scales"], P // a["scales"].shape[2], axis=2).transpose(2, 0, 1),
        "ql_bias_rows": np.tile(a["biases"][0::2], (1, TPC))[None], "ql_bias_cols": a["biases"].T,
        "qr_lora_a": a["lora_a"].swapaxes(0, 1), "qr_lora_b_T": a["lora_b"].transpose(2, 0, 1),
        "ql_gamma": a["ln_gamma"].T, "ql_beta": a["ln_beta"].T,
    })
    return r


def kernel(**inputs):
    import concourse.bacc as bacc
    from concourse.bass_utils import run_bass_kernel_spmd

    nc = bacc.Bacc("TRN2", target_bir_lowering=False, num_devices=1)
    arrays, dram = {}, {}
    laid = layouts({k: np.asarray(v) for k, v in inputs.items()})
    for name, a in {**laid, **constants()}.items():
        a = np.ascontiguousarray(a)
        arrays[f"in_{name}"] = a
        dram[name] = nc.dram_tensor(f"in_{name}", a.shape, mybir.dt.from_np(a.dtype), kind="ExternalInput").ap()
    out = nc.dram_tensor("out_x", (P, NT, P), F32, kind="ExternalOutput").ap()
    build(nc, dram, out)
    r = run_bass_kernel_spmd(nc, [arrays], core_ids=[0])
    got = r.results[0]["out_x"].reshape(P, NT, P).swapaxes(0, 1).reshape(1, TOK, P)
    return np.ascontiguousarray(got)
```

```python
from contextlib import ExitStack, contextmanager

import concourse.bass as bass
import numpy as np
from concourse import mybir

F32 = mybir.dt.float32
BF16 = mybir.dt.bfloat16
I32 = mybir.dt.int32
U32 = mybir.dt.uint32
ALU = mybir.AluOpType
ACT = mybir.ActivationFunctionType
AX = mybir.AxisListType
ds = bass.ds

P = 128
TOK = 2048
NT = TOK // P
CH = 512
NC = TOK // CH
TPC = CH // P
D_IN = 256
NH2 = D_IN // P
NS = 16
RANK = 8
XDBL = RANK + 2 * NS
CONV = 4
SPL = 3
SCT = 1024
NSC = TOK // SCT
FF = 512
NF = FF // P
NE = 8
EF = 256
NEF = EF // P
HEADS = 16
DH = P // HEADS
PAIRS = SPL * SPL * DH
ALIBI = 12
NEG = -1e30
QL = 6
LORA = 32
SB = P // HEADS


class Memory:

    count = 0

    def __init__(self, nc, ctx, tag):
        self.nc, self.ctx, self.tag = nc, ctx, tag

    def name(self, n):
        Memory.count += 1
        return f"{self.tag}_{n}_{Memory.count}"

    def sb(self, n, shape, dt=F32):
        return self.ctx.enter_context(self.nc.sbuf_tensor(self.name(n), list(shape), dt))

    def ps(self, n, shape, dt=F32):
        return self.ctx.enter_context(self.nc.psum_tensor(self.name(n), list(shape), dt))

    def sem(self, n):
        return self.nc.alloc_semaphore(self.name(n))


@contextmanager
def fresh_semaphores(nc):
    before = nc.snapshot_sems()
    yield
    nc.clear_and_free_semaphores(nc.allocated_since(before))
    nc.all_engine_barrier()


def tile(i):
    return slice(i * P, (i + 1) * P)


def chunk(c):
    return slice(c * CH, (c + 1) * CH)


class Weights(dict):
    pass


def group(m, dram, tag, names):
    w = Weights()
    w.loaded = m.sem(tag + "_loaded")
    w.full = 16 * len(names)
    w.loads = []
    for n in names:
        src = dram[f"{tag}_{n}"]
        w[n] = m.sb(f"{tag}_{n}", src.shape, src.dtype)
        w.loads.append((w[n], src, w.loaded))
    return w


def start_loads(eng, loads):
    for dst, src, sem in loads:
        eng.dma_start(dst[tuple(slice(None) for _ in dst.shape)], src).then_inc(sem, 16)


class LayerNorm:

    def __init__(self, m, g, x, xn, xT, turned, rounds=1, w=None):
        self.g, self.x, self.xn, self.xT, self.turned, self.rounds, self.w = g, x, xn, xT, turned, rounds, w
        self.bn = m.sb("bn_stats", [P, NT, 6])
        self.mean_var = m.sb("mean_var", [P, NT, 2])
        self.var_eps = m.sb("var_eps", [P, NT])
        self.rstd = m.sb("rstd", [P, NT])
        self.stats_done = m.sem("stats_done")
        self.aggr_done = m.sem("aggr_done")
        self.var_ready = m.sem("var_ready")
        self.rstd_ready = m.sem("rstd_ready")
        self.normed = m.sem("normed")
        self.turned_ready = m.sem("turned_ready")
        self.copied = m.sem("copied")

    def stats(self, dve, c, r=0):
        src = self.x if r == 0 else self.xn
        done = NT * r + TPC * c
        if r:
            dve.wait_ge(self.normed, NT * (r - 1) + TPC * (c + 1))
        for j in range(TPC):
            dve.bn_stats(self.bn[:, TPC * c + j, :], src[:, TPC * c + j, :]).then_inc(self.stats_done, 1)
        for j in range(TPC):
            dve.wait_ge(self.stats_done, done + j + 1)
            dve.bn_aggr(self.mean_var[:, TPC * c + j, :], self.bn[:, TPC * c + j, :]).then_inc(self.aggr_done, 1)
        dve.wait_ge(self.aggr_done, done + TPC)
        tiles = slice(TPC * c, TPC * (c + 1))
        dve.tensor_scalar(self.var_eps[:, tiles], self.mean_var[:, tiles, 1], 1e-5, None, ALU.add).then_inc(self.var_ready, 1)

    def power(self, pool, c, r=0):
        pool.wait_ge(self.var_ready, NC * r + c + 1)
        tiles = slice(TPC * c, TPC * (c + 1))
        pool.tensor_tensor(self.rstd[:, tiles], self.var_eps[:, tiles], self.g["minus_half"][:, 0:TPC],
                           ALU.pow).then_inc(self.rstd_ready, 1)

    def normalise(self, dve, c, r=0):
        src = self.x if r == 0 else self.xn
        dve.wait_ge(self.rstd_ready, NC * r + c + 1)
        for i in range(TPC * c, TPC * (c + 1)):
            dve.tensor_scalar(self.xn[:, i, :], src[:, i, :], self.mean_var[:, i, 0:1], self.rstd[:, i:i + 1],
                              ALU.subtract, ALU.mult).then_inc(self.normed, 1)

    def turn(self, pe, c):
        if c >= 2:
            pe.wait_ge(self.copied, c - 1)
        for j in range(TPC):
            pe.wait_ge(self.normed, NT * (self.rounds - 1) + TPC * c + j + 1)
            last = pe.transpose(self.turned[:, c % 2, tile(j)], self.xn[:, TPC * c + j, :], self.g["ident"][:, :])
        last.then_inc(self.turned_ready, 1)

    def copy(self, act, c):
        if self.w is not None and c == 0:
            act.wait_ge(self.w.loaded, self.w.full)
        act.wait_ge(self.turned_ready, c + 1)
        act.activation(self.xT[:, chunk(c)], self.turned[:, c % 2, :], ACT.Identity,
                       scale=1.0 if self.w is None else self.w["gain"][:, 0:1]).then_inc(self.copied, 1)


def mamba(nc, g, w, tag, x, xn, finish, loads=()):
    with ExitStack() as ctx:
        m = Memory(nc, ctx, tag)
        gate = m.sb("gate", [P, NH2, TOK])
        u = m.sb("u", [P, NH2, TOK])
        with ExitStack() as inner:
            mi = Memory(nc, inner, tag)
            delta = mi.sb("delta", [P, NH2, TOK])
            du = mi.sb("du", [P, NH2, TOK])
            bc3 = mi.sb("bc3", [SPL * 2 * NS, TOK], BF16)
            neg_a = mi.sb("neg_a", [P, NH2, NS])
            diag_d = mi.sb("diag_d", [P, NH2, P])
            mamba_inputs(nc, g, w, tag + "in", x, xn, u, gate, delta, du, bc3, neg_a, diag_d, loads)
            mamba_scan(nc, g, tag + "sc", u, delta, du, bc3, neg_a, diag_d, gate)
        finish(gate)


def mamba_inputs(nc, g, w, tag, x, xn, u, gate, delta, du, bc3, neg_a, diag_d, loads):
    with ExitStack() as ctx:
        m = Memory(nc, ctx, tag)
        xT = m.sb("xT", [P, TOK])
        raw = m.sb("raw", [P, NH2, CONV - 1 + TOK])
        xd = m.sb("xd", [XDBL, TOK])
        rest = m.sb("rest", [XDBL, 2, CH])
        parts = m.sb("parts", [XDBL, SPL, TOK], BF16)
        e = m.sb("e", [P, NH2, TOK])
        halves = (slice(0, TOK // 2), slice(TOK // 2, TOK))
        ln = raw[:, :, 0:TOK]
        t = du
        turned = m.ps("turned", [P, 2, CH])
        RING = 6
        acc = m.ps("acc", [P, RING, CH])
        norm = LayerNorm(m, g, x, xn, xT, turned)
        made = m.sem("made")
        raw_copied = m.sem("raw_copied")
        padded = m.sem("padded")
        conv = m.sem("conv")
        u_ready = m.sem("u_ready")
        xd_ready = m.sem("xd_ready")
        abs_done = m.sem("abs_done")
        relu_done = m.sem("relu_done")
        gate_ready = m.sem("gate_ready")
        exp_done = m.sem("exp_done")
        ln_done = m.sem("ln_done")
        rounded = m.sem("rounded")
        lost = [m.sem(f"lost{n}") for n in range(2)]
        a_exp = m.sem("a_exp")
        chain = m.sem("chain")
        split_0 = m.sem("split_0")
        split_1 = m.sem("split_1")
        split_2 = m.sem("split_2")
        rest_ready = m.sem("rest_ready")
        stacked = m.sem("stacked")
        block = ctx.enter_context(nc.Block())

        STEPS = NC + 3
        items = []
        for s in range(STEPS):
            items += [("u", s, h) for h in range(NH2) if s < NC]
            items += [("dt", s - 3, h) for h in range(NH2) if s >= 3]
            items += [("xd", s - 2, 0)] if 2 <= s < NC + 2 else []
            items += [("gate", s - 1, h) for h in range(NH2) if 1 <= s <= NC]
        late = {"u": 0, "gate": 1, "xd": 2, "dt": 3}
        reader = {"u": raw_copied, "xd": xd_ready, "dt": relu_done, "gate": gate_ready}

        def bank(what, c, h=0):
            return acc[:, items.index((what, c, h)) % RING, :]

        def tap(c, k, h):
            return NH2 * (CONV * c + k) + h + 1

        def product_made(what, c, h=0):
            return items.index((what, c, h)) + 1

        @block.tensor
        def _(pe):
            pe.wait_ge(w.loaded, w.full)
            for s in range(STEPS):
                if s < NC:
                    norm.turn(pe, s)
                for k, (what, c, h) in enumerate(items):
                    if c + late[what] != s:
                        continue
                    if k >= RING:
                        what0, c0, h0 = items[k - RING]
                        pe.wait_ge(reader[what0], c0 + 1 if what0 == "xd" else NH2 * c0 + h0 + 1)
                    if what == "u" or what == "gate":
                        if h == 0:
                            pe.wait_ge(norm.copied, c + 1)
                        wt = w["in_T"][:, tile((what == "gate") * NH2 + h)]
                        pe.matmul(bank(what, c, h), wt, xT[:, chunk(c)], start=True, stop=True).then_inc(made, 1)
                    elif what == "xd":
                        pe.wait_ge(u_ready, NH2 * (c + 1))
                        for half in range(NH2):
                            last = pe.matmul(bank("xd", c)[0:XDBL, :], w["x_T"][:, half, :], u[:, half, chunk(c)],
                                             start=half == 0, stop=half == NH2 - 1)
                        last.then_inc(made, 1)
                    else:
                        pe.wait_ge(xd_ready, c + 1)
                        pe.matmul(bank("dt", c, h), w["dt_T"][:, tile(h)], xd[0:RANK, chunk(c)],
                                  start=True, stop=True).then_inc(made, 1)

        @block.scalar
        def _(act):
            act.wait_ge(w.loaded, w.full)
            for s in range(STEPS):
                if 2 <= s < NC + 2:
                    c = s - 2
                    for h in range(NH2):
                        act.wait_ge(conv, tap(c, CONV - 1, h))
                        act.activation(u[:, h, chunk(c)], u[:, h, chunk(c)], ACT.Silu).then_inc(u_ready, 1)
                if s < NC:
                    norm.copy(act, s)
                    for h in range(NH2):
                        act.wait_ge(made, product_made("u", s, h))
                        act.activation(raw[:, h, CONV - 1 + s * CH:CONV - 1 + (s + 1) * CH], bank("u", s, h),
                                       ACT.Copy).then_inc(raw_copied, 1)
                if s >= 3:
                    c = s - 3
                    for h in range(NH2):
                        act.wait_ge(made, product_made("dt", c, h))
                        act.activation(e[:, h, chunk(c)], bank("dt", c, h), ACT.Abs,
                                       bias=w["dt_b"][:, h:h + 1]).then_inc(abs_done, 1)
                    act.wait_ge(rest_ready, c + 1)
                    act.activation(parts[:, 1, chunk(c)], rest[:, c % 2, :], ACT.Copy).then_inc(split_1, 1)
                if 2 <= s < NC + 2:
                    c = s - 2
                    act.wait_ge(made, product_made("xd", c))
                    act.activation(xd[:, chunk(c)], bank("xd", c)[0:XDBL, :], ACT.Copy).then_inc(xd_ready, 1)
                    act.wait_ge(xd_ready, c + 1)
                    act.activation(parts[:, 0, chunk(c)], xd[:, chunk(c)], ACT.Copy).then_inc(split_0, 1)
                if 1 <= s <= NC:
                    c = s - 1
                    for h in range(NH2):
                        act.wait_ge(made, product_made("gate", c, h))
                        act.activation(gate[:, h, chunk(c)], bank("gate", c, h), ACT.Silu).then_inc(gate_ready, 1)
                if s == NC + 1:
                    act.wait_ge(abs_done, NC)
                    act.activation(neg_a[:, :, :], w["a_log"][:, :, :], ACT.Exp).then_inc(a_exp, 1)
                    act.activation(e[:, :, halves[0]], e[:, :, halves[0]], ACT.Exp, scale=-1.0).then_inc(exp_done, 1)
            act.wait_ge(abs_done, NH2 * NC)
            act.activation(e[:, :, halves[1]], e[:, :, halves[1]], ACT.Exp, scale=-1.0).then_inc(exp_done, 1)
            act.wait_ge(conv, CONV * NH2 * NC)
            for n, half in enumerate(halves):
                act.wait_ge(exp_done, n + 1)
                act.activation(ln[:, :, half], e[:, :, half], ACT.Ln, bias=1.0).then_inc(ln_done, 1)
        def lost_in_rounding(eng, n):
            half = halves[n]
            eng.wait_ge(rounded, n + 1)
            eng.tensor_tensor(t[:, :, half], e[:, :, half], t[:, :, half], ALU.subtract).then_inc(lost[n], 1)
            eng.wait_ge(lost[n], 1)
            eng.wait_ge(relu_done, NC * (n + 1))
            eng.tensor_tensor(delta[:, :, half], delta[:, :, half], t[:, :, half], ALU.add).then_inc(lost[n], 1)

        def round_sum(dve, n):
            half = halves[n]
            dve.wait_ge(exp_done, n + 1)
            dve.tensor_scalar(t[:, :, half], e[:, :, half], 1.0, 1.0, ALU.add, ALU.subtract).then_inc(rounded, 1)

        @block.vector
        def _(dve):
            links = [0]

            def link(ins):
                links[0] += 1
                ins.then_inc(chain, 1)
                dve.wait_ge(chain, links[0])

            dve.memset(raw[:, :, 0:CONV - 1], 0.0).then_inc(padded, 1)
            norm.stats(dve, 0)
            for s in range(STEPS):
                if s + 1 < NC:
                    norm.stats(dve, s + 1)
                if s < NC:
                    norm.normalise(dve, s)
                if s == 0:
                    dve.wait_ge(padded, 1)
                    dve.wait_ge(w.loaded, w.full)
                if 1 <= s <= NC:
                    c = s - 1
                    for h in range(NH2):
                        dve.wait_ge(raw_copied, NH2 * c + h + 1)
                        dve.tensor_scalar(u[:, h, chunk(c)], raw[:, h, chunk(c)], w["conv_w"][:, h, 0:1],
                                          w["conv_b"][:, h:h + 1], ALU.mult, ALU.add).then_inc(conv, 1)
                    for k in range(1, CONV):
                        for h in range(NH2):
                            dve.wait_ge(conv, tap(c, k - 1, h))
                            dve.scalar_tensor_tensor(u[:, h, chunk(c)], raw[:, h, k + c * CH:k + (c + 1) * CH],
                                                     w["conv_w"][:, h, k:k + 1], u[:, h, chunk(c)],
                                                     ALU.mult, ALU.add).then_inc(conv, 1)
                if s >= 3:
                    c = s - 3
                    for h in range(NH2):
                        dve.wait_ge(abs_done, NH2 * c + h + 1)
                        dve.tensor_scalar(delta[:, h, chunk(c)], bank("dt", c, h), w["dt_b"][:, h:h + 1], 0.0,
                                          ALU.add, ALU.max).then_inc(relu_done, 1)
                if s == NC + 1:
                    round_sum(dve, 0)
            dve.wait_ge(a_exp, 1)
            link(dve.tensor_scalar(neg_a[:, :, :], neg_a[:, :, :], -1.0, None, ALU.mult))
            for h in range(NH2):
                link(dve.tensor_scalar(diag_d[:, h, :], g["ident"][:, :], w["d"][:, h:h + 1], None, ALU.mult))
            round_sum(dve, 1)
            lost_in_rounding(dve, 1)
            for n, half in enumerate(halves):
                dve.wait_ge(ln_done, n + 1)
                dve.wait_ge(lost[n], 2)
                link(dve.tensor_tensor(delta[:, :, half], delta[:, :, half], ln[:, :, half], ALU.add))
                link(dve.tensor_tensor(du[:, :, half], delta[:, :, half], u[:, :, half], ALU.mult))

        @block.gpsimd
        def _(pool):
            norm.power(pool, 0)
            for s in range(STEPS):
                if s + 1 < NC:
                    norm.power(pool, s + 1)
                if s >= 3:
                    c = s - 3
                    pool.wait_ge(split_1, c + 1)
                    pool.tensor_tensor(parts[:, 2, chunk(c)], rest[:, c % 2, :], parts[:, 1, chunk(c)],
                                       ALU.subtract).then_inc(split_2, 1)
                if 2 <= s < NC + 2:
                    c = s - 2
                    pool.wait_ge(split_0, c + 1)
                    if c >= 2:
                        pool.wait_ge(split_2, c - 1)
                    pool.tensor_tensor(rest[:, c % 2, :], xd[:, chunk(c)], parts[:, 0, chunk(c)], ALU.subtract).then_inc(rest_ready, 1)
                if s == NC + 1:
                    lost_in_rounding(pool, 0)

        @block.sync
        def _(sp):
            start_loads(sp, loads)
            for c in range(NC):
                sp.wait_ge(split_2, c + 1)
                for s in range(SPL):
                    sp.dma_start(bc3[2 * NS * s:2 * NS * (s + 1), chunk(c)],
                                 parts[RANK:XDBL, s, chunk(c)]).then_inc(stacked, 16)
            sp.wait_ge(stacked, 16 * SPL * NC)
            sp.wait_ge(g.late.loaded, g.late.full)


def mamba_scan(nc, g, tag, u, delta, du, bc3, neg_a, diag_d, gate):
    with ExitStack() as ctx:
        m = Memory(nc, ctx, tag)
        decay = [m.sb(f"decay{s}", [P, NH2, SCT]) for s in range(2)]
        state = [m.sb(f"state{s}", [P, NH2, SCT]) for s in range(2)]
        read = [m.sb(f"read{s}", [P, NH2, SCT]) for s in range(2)]
        c_rows = [m.sb(f"c_rows{s}", [P, SCT]) for s in range(2)]
        drive = m.sb("drive", [P, NH2, SCT])
        carry = m.sb("carry", [P, NH2, NS])
        psy = m.ps("psy", [P, NH2, SCT])
        psb = m.ps("psb", [P, SCT])
        psc = m.ps("psc", [P, SCT])
        b_ready = m.sem("b_ready")
        c_ready = m.sem("c_ready")
        c_copied = m.sem("c_copied")
        decay_ready = m.sem("decay_ready")
        drive_ready = m.sem("drive_ready")
        scanned = m.sem("scanned")
        carried = m.sem("carried")
        read_ready = m.sem("read_ready")
        summed = m.sem("summed")
        skip_done = m.sem("skip_done")
        gated = m.sem("gated")
        cleared = m.sem("cleared")
        NB = SCT // CH
        block = ctx.enter_context(nc.Block())

        def in_pairs(eng, step):
            for k in range(NSC):
                for s in range(2):
                    step(k, NS * k + s, s, s)
                with eng.Fori(1, NS // 2) as i:
                    for s in range(2):
                        step(k, 2 * i + (NS * k + s), 2 * i + s, s)

        def at_least(eng, sem, q, value):
            if not isinstance(q, int) or value > 0:
                eng.wait_ge(sem, value)

        @block.tensor
        def _(pe):
            def sum_states(q, s, ends):
                pe.wait_ge(read_ready, q + 1)
                for h in range(NH2):
                    for b in range(NB):
                        last = pe.matmul(psy[:, h, chunk(b)], g["ident"][:, :], read[s][:, h, chunk(b)],
                                         start=False, stop=ends, skip_group_check=True)
                last.then_inc(summed, 1)

            def rows(k, q, n, s):
                at_least(pe, drive_ready, q, q)
                for b in range(NB):
                    last = pe.matmul(psb[:, chunk(b)], g["sel"][:, n, :],
                                     bc3[:, k * SCT + b * CH:k * SCT + (b + 1) * CH], start=True, stop=True)
                last.then_inc(b_ready, 1)
                at_least(pe, c_copied, q, q)
                for b in range(NB):
                    last = pe.matmul(psc[:, chunk(b)], g["sel"][:, n + NS, :],
                                     bc3[:, k * SCT + b * CH:k * SCT + (b + 1) * CH], start=True, stop=True)
                last.then_inc(c_ready, 1)

            for k in range(NSC):
                for s in range(2):
                    rows(k, NS * k + s, s, s)
                if k:
                    pe.wait_ge(gated, k)
                for h in range(NH2):
                    for b in range(NB):
                        pe.matmul(psy[:, h, chunk(b)], diag_d[:, h, :],
                                  u[:, h, k * SCT + b * CH:k * SCT + (b + 1) * CH],
                                  start=True, stop=False, skip_group_check=True)
                with pe.Fori(1, NS // 2) as i:
                    for s in range(2):
                        rows(k, 2 * i + (NS * k + s), 2 * i + s, s)
                        sum_states(2 * i + (NS * k + s - 2), s, False)
                for s in range(2):
                    sum_states(NS * (k + 1) - 2 + s, s, s == 1)

        @block.scalar
        def _(act):
            def step(k, q, n, s):
                at_least(act, scanned, q, q * NH2 - NH2)
                for h in range(NH2):
                    act.activation(decay[s][:, h, :], delta[:, h, k * SCT:(k + 1) * SCT], ACT.Exp,
                                   scale=neg_a[:, h, ds(n, 1)]).then_inc(decay_ready, 1)
                act.wait_ge(c_ready, q + 1)
                at_least(act, read_ready, q, q - 1)
                act.activation(c_rows[s][:, :], psc[:, :], ACT.Copy).then_inc(c_copied, 1)

            in_pairs(act, step)

        @block.vector
        def _(dve):
            dve.memset(carry[:, :, :], 0.0).then_inc(cleared, 1)
            dve.wait_ge(cleared, 1)

            def step(k, q, n, s):
                dve.wait_ge(b_ready, q + 1)
                at_least(dve, scanned, q, q * NH2)
                dve.tensor_tensor(drive[:, :, :], du[:, :, k * SCT:(k + 1) * SCT],
                                  psb[:, :].unsqueeze(1).broadcast_to([P, NH2, SCT]), ALU.mult).then_inc(drive_ready, 1)
                dve.wait_ge(drive_ready, q + 1)
                at_least(dve, carried, q, q - 1)
                at_least(dve, read_ready, q, q - 1)
                for h in range(NH2):
                    dve.wait_ge(decay_ready, q * NH2 + (h + 1))
                    dve.tensor_tensor_scan(state[s][:, h, :], decay[s][:, h, :], drive[:, h, :],
                                           carry[:, h, ds(n, 1)], ALU.mult, ALU.add).then_inc(scanned, 1)

            for k in range(NSC):
                for s in range(2):
                    step(k, NS * k + s, s, s)
                with dve.Fori(1, NS // 2) as i:
                    for s in range(2):
                        step(k, 2 * i + (NS * k + s), 2 * i + s, s)
                dve.wait_ge(summed, NS * (k + 1))
                dve.tensor_tensor(gate[:, :, k * SCT:(k + 1) * SCT], psy[:, :, :],
                                  gate[:, :, k * SCT:(k + 1) * SCT], ALU.mult).then_inc(gated, 1)

        @block.gpsimd
        def _(pool):
            def step(k, q, n, s):
                pool.wait_ge(scanned, q * NH2 + NH2)
                pool.tensor_copy(carry[:, :, ds(n, 1)], state[s][:, :, SCT - 1:SCT]).then_inc(carried, 1)
                pool.wait_ge(c_copied, q + 1)
                at_least(pool, summed, q, q - 1)
                pool.tensor_tensor(read[s][:, :, :], state[s][:, :, :],
                                   c_rows[s][:, :].unsqueeze(1).broadcast_to([P, NH2, SCT]),
                                   ALU.mult).then_inc(read_ready, 1)

            in_pairs(pool, step)


def mamba_out_add(nc, w, tag, x, gated):
    with ExitStack() as ctx:
        m = Memory(nc, ctx, tag)
        acc = m.ps("acc", [P, NC, CH])
        summed = m.sem("summed")
        added = m.sem("added")
        block = ctx.enter_context(nc.Block())

        @block.tensor
        def _(pe):
            for c in range(NC):
                for j in range(TPC):
                    for h in range(NH2):
                        last = pe.matmul(acc[:, c, tile(j)], gated[:, h, tile(TPC * c + j)], w["out_T"][:, h, :],
                                         start=h == 0, stop=h == NH2 - 1)
                last.then_inc(summed, 1)

        @block.vector
        def _(dve):
            for c in range(NC):
                dve.wait_ge(summed, c + 1)
                xc = x[:, TPC * c:TPC * (c + 1), :]
                dve.tensor_tensor(xc, acc[:, c, :].rearrange("p (j f) -> p j f", f=P), xc, ALU.add).then_inc(added, 1)


def mamba_out_ffn(nc, g, w_out, w, tag, x, xn, gated):
    with ExitStack() as ctx:
        m = Memory(nc, ctx, tag)
        r = m.sb("r", [P, TPC, P])
        sq = m.sb("sq", [P, TPC, P])
        ms = m.sb("ms", [P, TPC])
        rms = m.sb("rms", [P, TPC])
        hm = m.sb("hm", [P, NT, P])
        hT = m.sb("hT", [P, CH])
        act1 = m.sb("act1", [P, NF, CH])
        pso = m.ps("pso", [P, CH])
        pst = m.ps("pst", [P, CH])
        ps1 = m.ps("ps1", [P, NF, CH])
        ps2 = m.ps("ps2", [P, CH])
        o_ready = m.sem("o_ready")
        o_read = m.sem("o_read")
        h_ready = m.sem("h_ready")
        t_ready = m.sem("t_ready")
        hT_ready = m.sem("hT_ready")
        f1_ready = m.sem("f1_ready")
        gelu_done = m.sem("gelu_done")
        f2_ready = m.sem("f2_ready")
        f2_read = m.sem("f2_read")
        ms_ready = m.sem("ms_ready")
        rms_ready = m.sem("rms_ready")
        chain = m.sem("chain")
        added = m.sem("added")
        block = ctx.enter_context(nc.Block())

        @block.tensor
        def _(pe):
            def project(c):
                if c:
                    pe.wait_ge(o_read, c)
                for j in range(TPC):
                    for h in range(NH2):
                        last = pe.matmul(pso[:, tile(j)], gated[:, h, tile(TPC * c + j)], w_out["out_T"][:, h, :],
                                         start=h == 0, stop=h == NH2 - 1)
                last.then_inc(o_ready, 1)

            project(0)
            pe.wait_ge(w.loaded, w.full)
            for c in range(NC):
                pe.wait_ge(h_ready, TPC * (c + 1))
                if c:
                    pe.wait_ge(hT_ready, c)
                for j in range(TPC):
                    last = pe.transpose(pst[:, tile(j)], hm[:, TPC * c + j, :], g["ident"][:, :])
                last.then_inc(t_ready, 1)
                pe.wait_ge(hT_ready, c + 1)
                for k in range(NF):
                    if c:
                        pe.wait_ge(gelu_done, NF * (c - 1) + k + 1)
                    pe.matmul(ps1[:, k, :], w["w1_T"][:, tile(k)], hT[:, :], start=True, stop=True).then_inc(f1_ready, 1)
                if c + 1 < NC:
                    project(c + 1)
                pe.wait_ge(gelu_done, NF * (c + 1))
                if c:
                    pe.wait_ge(f2_read, c)
                pe.matmul(ps2[:, :], g["ones_row"][:, 0:P], w["b2_rows"][:, :], start=True, stop=False, skip_group_check=True)
                for j in range(TPC):
                    for k in range(NF):
                        last = pe.matmul(ps2[:, tile(j)], act1[:, k, tile(j)], w["w2_T"][:, k, :],
                                         start=False, stop=k == NF - 1, skip_group_check=True)
                last.then_inc(f2_ready, 1)

        @block.scalar
        def _(act):
            act.wait_ge(w.loaded, w.full)
            for c in range(NC):
                act.wait_ge(t_ready, c + 1)
                if c:
                    act.wait_ge(f1_ready, NF * c)
                act.activation(hT[:, :], pst[:, :], ACT.Copy).then_inc(hT_ready, 1)
                if c:
                    act.wait_ge(f2_ready, c)
                for k in range(NF):
                    act.wait_ge(f1_ready, NF * c + k + 1)
                    act.activation(act1[:, k, :], ps1[:, k, :], ACT.Gelu, bias=w["b1"][:, k:k + 1]).then_inc(gelu_done, 1)

        @block.gpsimd
        def _(pool):
            for n in range(2 * NC):
                pool.wait_ge(ms_ready, n + 1)
                pool.tensor_tensor(rms[:, :], ms[:, :], g["minus_half"][:, 0:TPC], ALU.pow).then_inc(rms_ready, 1)

        @block.vector
        def _(dve):
            links = [0]
            norms = [0]

            def link(ins):
                links[0] += 1
                ins.then_inc(chain, 1)
                dve.wait_ge(chain, links[0])

            def rms_of_r():
                link(dve.tensor_tensor(sq[:, :, :], r[:, :, :], r[:, :, :], ALU.mult))
                link(dve.tensor_reduce(ms[:, :], sq[:, :, :], AX.X, ALU.add))
                dve.tensor_scalar(ms[:, :], ms[:, :], 1.0 / P, 1e-12, ALU.mult, ALU.add).then_inc(ms_ready, 1)
                norms[0] += 1
                dve.wait_ge(rms_ready, norms[0])

            def first(c):
                dve.wait_ge(o_ready, c + 1)
                dve.tensor_tensor(r[:, :, :], pso[:, :].rearrange("p (j f) -> p j f", f=P),
                                  xn[:, TPC * c:TPC * (c + 1), :], ALU.add).then_inc(o_read, 1)
                dve.wait_ge(o_read, c + 1)
                rms_of_r()
                for j in range(TPC):
                    dve.scalar_tensor_tensor(hm[:, TPC * c + j, :], r[:, j, :], rms[:, j:j + 1], w["norm_w"][:, :],
                                             ALU.mult, ALU.mult).then_inc(h_ready, 1)
                dve.wait_ge(h_ready, TPC * (c + 1))

            def second(c):
                dve.wait_ge(f2_ready, c + 1)
                dve.tensor_tensor(r[:, :, :], ps2[:, :].rearrange("p (j f) -> p j f", f=P),
                                  hm[:, TPC * c:TPC * (c + 1), :], ALU.add).then_inc(f2_read, 1)
                dve.wait_ge(f2_read, c + 1)
                rms_of_r()
                for j in range(TPC):
                    link(dve.scalar_tensor_tensor(r[:, j, :], r[:, j, :], rms[:, j:j + 1], w["ffn_norm_w"][:, :],
                                                  ALU.mult, ALU.mult))
                xc = x[:, TPC * c:TPC * (c + 1), :]
                dve.tensor_tensor(xc, r[:, :, :], xc, ALU.add).then_inc(added, 1)
                dve.wait_ge(added, c + 1)

            dve.wait_ge(w.loaded, w.full)
            first(0)
            for c in range(NC):
                if c + 1 < NC:
                    first(c + 1)
                second(c)


def moe(nc, g, dram, tag, x, xn):
    with ExitStack() as ctx:
        m = Memory(nc, ctx, tag)
        wg = group(m, dram, "me", ["g_T"])
        w = group(m, dram, "me", MOE)
        xT = m.sb("xT", [P, TOK])
        comb_T = m.sb("comb_T", [NE, TOK])
        comb3_T = m.sb("comb3_T", [SPL * NE, TOK], BF16)
        moe_gate(nc, g, wg, w.loads, tag + "gt", x, xn, xT, comb_T, comb3_T)
        moe_experts(nc, g, w, tag + "ex", x, xT, comb_T, comb3_T)


def moe_gate(nc, g, w, loads, tag, x, xn, xT, comb_T, comb3_T):
    with ExitStack() as ctx:
        m = Memory(nc, ctx, tag)
        logits = m.sb("logits", [P, NT, NE])
        best = m.sb("best", [P, NT, 8])
        index = m.sb("index", [P, NT, 8], U32)
        index_f = m.sb("index_f", [P, NT, 2])
        gap = m.sb("gap", [P, NT, 1])
        e = m.sb("e", [P, NT, 1])
        w0 = m.sb("w0", [P, NT, 1])
        w1 = m.sb("w1", [P, NT, 1])
        is0 = m.sb("is0", [P, NT, NE])
        is1 = m.sb("is1", [P, NT, NE])
        parts = m.sb("parts", [P, NT, SPL * NE], BF16)
        turned = m.ps("turned", [P, 2, CH])
        norm = LayerNorm(m, g, x, xn, xT, turned)
        psg_bank = m.ps("psg", [P, CH])
        psg = psg_bank[:, 0:NT * NE].rearrange("p (i e) -> p i e", e=NE)
        psc = m.ps("psc", [NE, 2, CH])
        psp = m.ps("psp", [SPL * NE, TOK], BF16)
        logits_ready = m.sem("logits_ready")
        maxed = m.sem("maxed")
        indexed = m.sem("indexed")
        gap_ready = m.sem("gap_ready")
        exp_done = m.sem("exp_done")
        chain = m.sem("chain")
        comb_ready = m.sem("comb_ready")
        parts_ready = m.sem("parts_ready")
        comb_turned = m.sem("comb_turned")
        comb_copied = m.sem("comb_copied")
        parts_turned = m.sem("parts_turned")
        parts_copied = m.sem("parts_copied")
        block = ctx.enter_context(nc.Block())

        @block.sync
        def _(sp):
            start_loads(sp, w.loads + loads)

        @block.tensor
        def _(pe):
            for c in range(NC):
                norm.turn(pe, c)
                pe.wait_ge(norm.copied, c + 1)
                if c == 0:
                    pe.wait_ge(w.loaded, w.full)
                for i in range(TPC * c, TPC * (c + 1)):
                    last = pe.matmul(psg[:, i, :], xT[:, tile(i)], w["g_T"][:, :], start=True, stop=True)
            last.then_inc(logits_ready, 1)
            pe.wait_ge(comb_ready, 1)
            for c in range(NC):
                if c >= 2:
                    pe.wait_ge(comb_copied, c - 1)
                for j in range(TPC):
                    last = pe.transpose(psc[:, c % 2, tile(j)], is0[:, TPC * c + j, :], g["ident"][:, :])
                last.then_inc(comb_turned, 1)
            pe.wait_ge(parts_ready, SPL)
            for i in range(NT):
                last = pe.transpose(psp[:, tile(i)], parts[:, i, :], g["ident_b"][:, :])
            last.then_inc(parts_turned, 1)

        @block.vector
        def _(dve):
            links = [0]

            def link(ins):
                links[0] += 1
                ins.then_inc(chain, 1)
                dve.wait_ge(chain, links[0])

            def spread(col, n):
                return col.broadcast_to([P, NT, n])

            norm.stats(dve, 0)
            for c in range(NC):
                if c + 1 < NC:
                    norm.stats(dve, c + 1)
                norm.normalise(dve, c)
            dve.wait_ge(logits_ready, 1)
            link(dve.tensor_copy(logits[:, :, :], psg[:, :, :]))
            for i in range(NT):
                dve.max(best[:, i, :], logits[:, i, :]).then_inc(maxed, 1)
            for i in range(NT):
                dve.wait_ge(maxed, i + 1)
                dve.max_index(index[:, i, :], best[:, i, :], logits[:, i, :]).then_inc(indexed, 1)
            dve.tensor_tensor(gap[:, :, :], best[:, :, 1:2], best[:, :, 0:1], ALU.subtract).then_inc(gap_ready, 1)
            dve.wait_ge(indexed, NT)
            link(dve.tensor_copy(index_f[:, :, :], index[:, :, 0:2]))
            iota = g["iota"][:, :].unsqueeze(1).broadcast_to([P, NT, NE])
            link(dve.tensor_tensor(is0[:, :, :], iota, spread(index_f[:, :, 0:1], NE), ALU.is_equal))
            link(dve.tensor_tensor(is1[:, :, :], iota, spread(index_f[:, :, 1:2], NE), ALU.is_equal))
            dve.wait_ge(exp_done, 1)
            link(dve.tensor_scalar(w1[:, :, :], e[:, :, :], 1.0, None, ALU.add))
            link(dve.reciprocal(w0[:, :, :], w1[:, :, :]))
            link(dve.tensor_tensor(w1[:, :, :], e[:, :, :], w0[:, :, :], ALU.mult))
            link(dve.tensor_tensor(is0[:, :, :], is0[:, :, :], spread(w0[:, :, :], NE), ALU.mult))
            link(dve.tensor_tensor(is1[:, :, :], is1[:, :, :], spread(w1[:, :, :], NE), ALU.mult))
            dve.tensor_tensor(is0[:, :, :], is0[:, :, :], is1[:, :, :], ALU.add).then_inc(comb_ready, 1)
            dve.wait_ge(comb_ready, 1)
            dve.tensor_copy(parts[:, :, 0:NE], is0[:, :, :]).then_inc(parts_ready, 1)
            dve.wait_ge(parts_ready, 1)
            link(dve.tensor_tensor(is1[:, :, :], is0[:, :, :], parts[:, :, 0:NE], ALU.subtract))
            dve.tensor_copy(parts[:, :, NE:2 * NE], is1[:, :, :]).then_inc(parts_ready, 1)
            dve.wait_ge(parts_ready, 2)
            dve.tensor_tensor(parts[:, :, 2 * NE:3 * NE], is1[:, :, :], parts[:, :, NE:2 * NE],
                              ALU.subtract).then_inc(parts_ready, 1)

        @block.scalar
        def _(act):
            for c in range(NC):
                norm.copy(act, c)
            act.wait_ge(gap_ready, 1)
            act.activation(e[:, :, :], gap[:, :, :], ACT.Exp).then_inc(exp_done, 1)
            for c in range(NC):
                act.wait_ge(comb_turned, c + 1)
                act.activation(comb_T[:, chunk(c)], psc[:, c % 2, :], ACT.Copy).then_inc(comb_copied, 1)
            act.wait_ge(parts_turned, 1)
            act.activation(comb3_T[:, :], psp[:, :], ACT.Copy).then_inc(parts_copied, 1)

        @block.gpsimd
        def _(pool):
            for c in range(NC):
                norm.power(pool, c)


def moe_experts(nc, g, w, tag, x, xT, comb_T, comb3_T):
    with ExitStack() as ctx:
        m = Memory(nc, ctx, tag)
        SL = 4
        silu = m.sb("silu", [P, SL, CH])
        mid = m.sb("mid", [P, 2, CH])
        hid = m.sb("hid", [P, SL, CH])
        oT = m.sb("oT", [P, CH])
        psg = m.ps("psg", [P, NEF, CH])
        psv = m.ps("psv", [P, NEF, CH])
        psc = m.ps("psc", [P, CH])
        pso = m.ps("pso", [P, CH])
        pst = m.ps("pst", [P, CH])
        g_ready = m.sem("g_ready")
        v_ready = m.sem("v_ready")
        c_ready = m.sem("c_ready")
        g_free = m.sem("g_free")
        v_free = m.sem("v_free")
        hid_made = m.sem("hid_made")
        hid_free = m.sem("hid_free")
        o_free = m.sem("o_free")
        o_ready = m.sem("o_ready")
        t_ready = m.sem("t_ready")
        added = m.sem("added")
        K = NE * NEF
        x_flat = x[:, :, :].rearrange("p i f -> p (i f)")
        block = ctx.enter_context(nc.Block())

        @block.tensor
        def _(pe):
            pe.wait_ge(w.loaded, w.full)
            pe.sem_inc(hid_free, SL)

            def product(c, e):
                for f in range(NEF):
                    k = NEF * e + f
                    pe.wait_ge(hid_made, c * K + (k + 2))
                    last = pe.matmul(pso[:, :], w["w3_T"][:, e, f, :], hid[:, k % SL, :], start=False,
                                     stop=k == K - 1, skip_group_check=True)
                    last.then_inc(hid_free, 1)

            def items(c, tokens, e, f):
                k = NEF * e + f
                fs = slice(f * P, (f + 1) * P)
                pe.wait_ge(g_free, c * K + (k + 1))
                pe.matmul(psg[:, f, :], w["w1_T"][:, e, fs], xT[:, tokens], start=True, stop=True).then_inc(g_ready, 1)
                pe.wait_ge(v_free, c * K + (k + 3))
                pe.matmul(psv[:, f, :], w["w2_T"][:, e, fs], xT[:, tokens], start=True, stop=True).then_inc(v_ready, 1)

            with pe.Fori(0, NC) as c:
                tokens = ds(c * CH, CH)
                for e in range(NE):
                    items(c, tokens, e, 0)
                    if e:
                        product(c, e - 1)
                    else:
                        pe.matmul(pso[:, :], w["b3"][:, :], comb_T[:, tokens], start=True, stop=False,
                                  skip_group_check=True)
                    pe.matmul(psc[:, :], g["sel_e"][:, e, :], comb3_T[:, tokens], start=True, stop=True).then_inc(c_ready, 1)
                    items(c, tokens, e, 1)
                product(c, NE - 1)
                pe.wait_ge(o_free, c + 2)
                pe.wait_ge(added, c + 1)
                for j in range(TPC):
                    last = pe.transpose(pst[:, tile(j)], oT[:, tile(j)], g["ident"][:, :])
                last.then_inc(t_ready, 1)

        @block.scalar
        def _(act):
            act.sem_inc(g_free, 2)
            act.sem_inc(o_free, 1)
            with act.Fori(0, NC) as c:
                for k in range(K):
                    e, f = divmod(k, NEF)
                    act.wait_ge(g_ready, c * K + (k + 1))
                    act.wait_ge(v_free, c * K + (k + 1))
                    act.activation(silu[:, k % SL, :], psg[:, f, :], ACT.Silu, bias=w["b1"][:, e, f:f + 1]).then_inc(g_free, 1)
                act.wait_ge(hid_free, c * K + (K + SL))
                act.wait_ge(added, c + 1)
                act.activation(oT[:, :], pso[:, :], ACT.Copy).then_inc(o_free, 1)

        @block.vector
        def _(dve):
            dve.sem_inc(v_free, SL)
            dve.sem_inc(hid_made, 1)
            dve.sem_inc(added, 1)
            with dve.Fori(0, NC) as c:
                for k in range(K):
                    e, f = divmod(k, NEF)
                    dve.wait_ge(v_ready, c * K + (k + 1))
                    dve.wait_ge(g_free, c * K + (k + 3))
                    dve.wait_ge(hid_made, c * K + (k + 1))
                    dve.scalar_tensor_tensor(mid[:, k % 2, :], psv[:, f, :], w["b2"][:, e, f:f + 1], silu[:, k % SL, :],
                                             ALU.add, ALU.mult).then_inc(v_free, 1)
                    dve.wait_ge(v_free, c * K + (k + SL + 1))
                    dve.wait_ge(c_ready, c * NE + (e + 1))
                    dve.wait_ge(hid_free, c * K + (k + 1))
                    dve.tensor_tensor(hid[:, k % SL, :], mid[:, k % 2, :], psc[:, :], ALU.mult).then_inc(hid_made, 1)
                dve.wait_ge(t_ready, c + 1)
                xc = x_flat[:, ds(c * CH, CH)]
                dve.tensor_tensor(xc, pst[:, :], xc, ALU.add).then_inc(added, 1)


def qlora_weights(nc, dram, tag, eff_all, bias3):
    with ExitStack() as ctx:
        m = Memory(nc, ctx, tag)
        w = group(m, dram, "qr", QLORA_RAW)
        psl = m.ps("psl", [P, 2, CH])
        parts = m.sb("parts", [QL // 2, SPL, P], BF16)
        rest = m.sb("rest", [QL // 2, P])
        parts_ready = m.sem("parts_ready")
        stacked = m.sem("stacked")
        chain = m.sem("chain")
        lora_ready = m.sem("lora_ready")
        half = QL // 2
        block = ctx.enter_context(nc.Block())

        @block.sync
        def _(sp):
            start_loads(sp, w.loads)
            sp.wait_ge(parts_ready, SPL)
            for s in range(SPL):
                sp.dma_start(bias3[s:s + 1, :, :], parts[:, s, :]).then_inc(stacked, 16)
            sp.wait_ge(stacked, 16 * SPL)

        @block.tensor
        def _(pe):
            pe.wait_ge(w.loaded, w.full)
            for k in range(QL):
                last = pe.matmul(psl[:, k // half, tile(k % half)], w["lora_a"][:, k, :], w["lora_b_T"][:, k, :],
                                 start=True, stop=True)
            last.then_inc(lora_ready, 1)

        @block.vector
        def _(dve):
            links = [0]

            def link(ins):
                links[0] += 1
                ins.then_inc(chain, 1)
                dve.wait_ge(chain, links[0])

            dve.wait_ge(w.loaded, w.full)
            dve.tensor_copy(parts[:, 0, :], w["bias_0"][:, :]).then_inc(parts_ready, 1)
            dve.wait_ge(parts_ready, 1)
            link(dve.tensor_tensor(rest[:, :], w["bias_0"][:, :], parts[:, 0, :], ALU.subtract))
            dve.tensor_copy(parts[:, 1, :], rest[:, :]).then_inc(parts_ready, 1)
            dve.wait_ge(parts_ready, 2)
            dve.tensor_tensor(parts[:, 2, :], rest[:, :], parts[:, 1, :], ALU.subtract).then_inc(parts_ready, 1)
            link(dve.tensor_copy(eff_all[:, :, :], w["q_T"][:, :, :]))
            link(dve.tensor_scalar(eff_all[:, :, :], eff_all[:, :, :], 1.0 / 7.5, -1.0, ALU.mult, ALU.add))
            link(dve.tensor_tensor(eff_all[:, :, :], eff_all[:, :, :], w["scale_T"][:, :, :], ALU.mult))
            dve.wait_ge(lora_ready, 1)
            for k in range(2):
                eff = eff_all[:, half * k:half * (k + 1), :]
                link(dve.tensor_tensor(eff, psl[:, k, 0:half * P].rearrange("p (m f) -> p m f", f=P), eff, ALU.add))


def qlora_mlp(nc, g, w, tag, x, xn):
    with ExitStack() as ctx:
        m = Memory(nc, ctx, tag)
        hT = m.sb("hT", [P, TOK])
        stats = m.sb("stats", [P, TPC, 6])
        mean_var = m.sb("mean_var", [P, TPC, 2])
        var_eps = m.sb("var_eps", [P, 2, TPC])
        minus_mean = m.sb("minus_mean", [P, 2, TPC])
        rstd = m.sb("rstd", [P, 2, TPC])
        shift = m.sb("shift", [P, 2, TPC])
        yn = m.sb("yn", [P, 2, CH])
        act1 = m.sb("act1", [P, 2, CH])
        psy = m.ps("psy", [P, 2, CH])
        pst = m.ps("pst", [P, 2, CH])
        psz = m.ps("psz", [P, 2, CH])
        psx = m.ps("psx", [P, 2, CH])
        norm = LayerNorm(m, g, x, xn, hT, psx)
        y_ready = m.sem("y_ready")
        stats_done = m.sem("stats_done")
        aggr_done = m.sem("aggr_done")
        mean_ready = m.sem("mean_ready")
        var_ready = m.sem("var_ready")
        rstd_ready = m.sem("rstd_ready")
        shift_ready = m.sem("shift_ready")
        normed = m.sem("normed")
        t_ready = m.sem("t_ready")
        gelu_done = m.sem("gelu_done")
        z_ready = m.sem("z_ready")
        h_ready = m.sem("h_ready")
        x_ready = m.sem("x_ready")
        added = m.sem("added")
        N = QL // 2 * NC
        block = ctx.enter_context(nc.Block())

        @block.tensor
        def _(pe):
            def linear(n):
                b, c = divmod(n, NC)
                if b:
                    pe.wait_ge(h_ready, n - NC + 1)
                else:
                    pe.wait_ge(norm.copied, c + 1)
                if n >= 2:
                    pe.wait_ge(normed, TPC * (n - 1))
                pe.matmul(psy[:, n % 2, :], g["ones_3"][:, :], w["bias3"][:, b, :].unsqueeze(1).broadcast_to([SPL, TPC, P]),
                          start=True, stop=False, skip_group_check=True)
                for j in range(TPC):
                    last = pe.matmul(psy[:, n % 2, tile(j)], hT[:, tile(TPC * c + j)], w["eff"][:, 2 * b, :],
                                     start=False, stop=True, skip_group_check=True)
                last.then_inc(y_ready, 1)

            def turn(n):
                if n >= 2:
                    pe.wait_ge(gelu_done, n - 1)
                for j in range(TPC):
                    pe.wait_ge(normed, TPC * n + j + 1)
                    last = pe.transpose(pst[:, n % 2, tile(j)], yn[:, n % 2, tile(j)], g["ident"][:, :])
                last.then_inc(t_ready, 1)

            def linear2(n):
                pe.wait_ge(gelu_done, n + 1)
                if n >= 2:
                    pe.wait_ge(h_ready, n - 1)
                pe.matmul(psz[:, n % 2, :], w["eff"][:, 2 * (n // NC) + 1, :], act1[:, n % 2, :],
                          start=True, stop=True).then_inc(z_ready, 1)

            norm.turn(pe, 0)
            for n in range(N + 3):
                if n + 1 < NC:
                    norm.turn(pe, n + 1)
                if n >= 3:
                    linear2(n - 3)
                if 2 <= n < N + 2:
                    turn(n - 2)
                if n < N:
                    linear(n)
            for c in range(NC):
                pe.wait_ge(h_ready, N - NC + c + 1)
                if c >= 2:
                    pe.wait_ge(added, c - 1)
                for j in range(TPC):
                    last = pe.transpose(psx[:, c % 2, tile(j)], hT[:, tile(TPC * c + j)], g["ident"][:, :])
                last.then_inc(x_ready, 1)

        @block.vector
        def _(dve):
            def moments(n):
                dve.wait_ge(y_ready, n + 1)
                if n:
                    dve.wait_ge(aggr_done, TPC * n)
                for j in range(TPC):
                    dve.bn_stats(stats[:, j, :], psy[:, n % 2, tile(j)]).then_inc(stats_done, 1)
                if n:
                    dve.wait_ge(var_ready, n)
                for j in range(TPC):
                    dve.wait_ge(stats_done, TPC * n + j + 1)
                    dve.bn_aggr(mean_var[:, j, :], stats[:, j, :]).then_inc(aggr_done, 1)
                dve.wait_ge(aggr_done, TPC * (n + 1))
                if n >= 2:
                    dve.wait_ge(shift_ready, n - 1)
                dve.tensor_scalar(minus_mean[:, n % 2, :], mean_var[:, :, 0], -1.0, None, ALU.mult).then_inc(mean_ready, 1)
                dve.wait_ge(mean_ready, n + 1)
                dve.tensor_scalar(var_eps[:, n % 2, :], mean_var[:, :, 1], 1e-5, None, ALU.add).then_inc(var_ready, 1)

            def residual(n):
                b, c = divmod(n, NC)
                dve.wait_ge(z_ready, n + 1)
                if b:
                    dve.wait_ge(h_ready, n - NC + 1)
                dve.scalar_tensor_tensor(hT[:, chunk(c)], psz[:, n % 2, :], w["bias_cols"][:, 2 * b + 1:2 * b + 2],
                                         hT[:, chunk(c)], ALU.add, ALU.add).then_inc(h_ready, 1)

            norm.stats(dve, 0)
            norm.stats(dve, 1)
            norm.normalise(dve, 0)
            for n in range(N + 3):
                if n + 2 < NC:
                    norm.stats(dve, n + 2)
                if n + 1 < NC:
                    norm.normalise(dve, n + 1)
                if n >= 3:
                    residual(n - 3)
                if n < N:
                    moments(n)
            for c in range(NC):
                dve.wait_ge(x_ready, c + 1)
                xc = x[:, TPC * c:TPC * (c + 1), :]
                dve.tensor_tensor(xc, psx[:, c % 2, :].rearrange("p (j f) -> p j f", f=P), xc, ALU.add).then_inc(added, 1)

        @block.gpsimd
        def _(pool):
            norm.power(pool, 0)
            norm.power(pool, 1)
            for n in range(N):
                if n + 2 < NC:
                    norm.power(pool, n + 2)
                pool.wait_ge(var_ready, n + 1)
                if n >= 2:
                    pool.wait_ge(normed, TPC * (n - 1))
                pool.tensor_tensor(rstd[:, n % 2, :], var_eps[:, n % 2, :], g["minus_half"][:, 0:TPC],
                                   ALU.pow).then_inc(rstd_ready, 1)
                pool.wait_ge(rstd_ready, n + 1)
                pool.tensor_tensor(shift[:, n % 2, :], minus_mean[:, n % 2, :], rstd[:, n % 2, :],
                                   ALU.mult).then_inc(shift_ready, 1)

        @block.scalar
        def _(act):
            def gelu(n):
                act.wait_ge(t_ready, n + 1)
                if n >= 2:
                    act.wait_ge(z_ready, n - 1)
                act.activation(act1[:, n % 2, :], pst[:, n % 2, :], ACT.Gelu, bias=w["beta"][:, n // NC:n // NC + 1],
                               scale=w["gamma"][:, n // NC:n // NC + 1]).then_inc(gelu_done, 1)

            norm.copy(act, 0)
            def normalise(n):
                act.wait_ge(shift_ready, n + 1)
                if n >= 2:
                    act.wait_ge(t_ready, n - 1)
                for j in range(TPC):
                    act.activation(yn[:, n % 2, tile(j)], psy[:, n % 2, tile(j)], ACT.Identity,
                                   bias=shift[:, n % 2, j:j + 1], scale=rstd[:, n % 2, j:j + 1]).then_inc(normed, 1)

            for n in range(N + 2):
                if n + 1 < NC:
                    norm.copy(act, n + 1)
                if n >= 2:
                    gelu(n - 2)
                if 1 <= n <= N:
                    normalise(n - 1)


def attention(nc, g, w, tag, dram, x, xn, alibi):
    with ExitStack() as ctx:
        m = Memory(nc, ctx, tag)
        v = m.sb("v", [P, NT, P])
        q_dram = nc.dram_tensor(tag + "_q_parts", (SPL, P, TOK), BF16, kind="Internal").ap()
        k_dram = nc.dram_tensor(tag + "_k_parts", (HEADS, SPL * DH, TOK), BF16, kind="Internal").ap()
        o_dram = nc.dram_tensor(tag + "_outputs", (HEADS, P, TOK), F32, kind="Internal").ap()
        with ExitStack() as inner:
            xT = Memory(nc, inner, tag).sb("xT", [P, TOK])
            attention_project(nc, g, w, tag + "pr", x, xn, xT, v, q_dram, k_dram, alibi)
        oT = m.sb("oT", [P, 4, TOK])
        sums = m.sb("sums", [HEADS * SB, 4, TOK // SB])
        attention_heads(nc, g, tag + "hd", dram, q_dram, k_dram, v, o_dram, oT, sums, alibi)
        attention_out(nc, g, w, tag + "ou", x, oT, sums)


def attention_project(nc, g, w, tag, x, xn, xT, v, q_dram, k_dram, alibi):
    with ExitStack() as ctx:
        m = Memory(nc, ctx, tag)
        full = [m.sb(n, [P, TOK]) for n in ("q", "k")]
        parts = [m.sb(n, [P, SPL, TOK], BF16) for n in ("q_parts", "k_parts")]
        turned = m.ps("turned", [P, 2, CH])
        acc = m.ps("acc", [P, 2, SPL, CH])
        rounds = 1 if alibi else 2
        norm = LayerNorm(m, g, x, xn, xT, turned, rounds=rounds, w=None if alibi else w)
        projected = m.sem("projected")
        copied = [m.sem(n + "_copied") for n in ("q", "k", "v")]
        first_part = [m.sem(n + "_first_part") for n in ("q", "k")]
        second_part = [m.sem(n + "_second_part") for n in ("q", "k")]
        third_part = [m.sem(n + "_third_part") for n in ("q", "k")]
        left = [m.sem(n + "_left") for n in ("q", "k")]
        stored = [m.sem(n + "_stored") for n in ("q", "k")]
        block = ctx.enter_context(nc.Block())

        @block.tensor
        def _(pe):
            pe.wait_ge(w.loaded, w.full)
            for c in range(NC):
                norm.turn(pe, c)
                pe.wait_ge(norm.copied, c + 1)
                b = c % 2
                for o, wt in enumerate((w["wq"], w["wk"])):
                    if c >= 2:
                        pe.wait_ge(first_part[o], c - 1)
                    pe.matmul(acc[:, b, o, :], wt[:, :], xT[:, chunk(c)], start=True, stop=True).then_inc(projected, 1)
                if c >= 2:
                    pe.wait_ge(copied[2], c - 1)
                for j in range(TPC):
                    last = pe.matmul(acc[:, b, 2, tile(j)], xT[:, tile(TPC * c + j)], w["wv"][:, :], start=True, stop=True)
                last.then_inc(projected, 1)

        @block.scalar
        def _(act):
            norm.copy(act, 0)
            for c in range(NC):
                if c + 1 < NC:
                    norm.copy(act, c + 1)
                b = c % 2
                for o in range(2):
                    scale = float(DH) ** -0.5 if o == 0 else 1.0
                    act.wait_ge(projected, 3 * c + o + 1)
                    act.activation(full[o][:, chunk(c)], acc[:, b, o, :], ACT.Copy, scale=scale).then_inc(copied[o], 1)
                    act.activation(parts[o][:, 0, chunk(c)], acc[:, b, o, :], ACT.Copy, scale=scale).then_inc(first_part[o], 1)
                act.wait_ge(projected, 3 * c + 3)
                act.activation(v[:, TPC * c:TPC * (c + 1), :], acc[:, b, 2, :].rearrange("p (j f) -> p j f", f=P),
                               ACT.Copy).then_inc(copied[2], 1)

        @block.vector
        def _(dve):
            steps = [(r, c) for r in range(rounds) for c in range(NC)]
            norm.stats(dve, 0)
            for n, (r, c) in enumerate(steps):
                if n + 1 < len(steps):
                    norm.stats(dve, steps[n + 1][1], steps[n + 1][0])
                norm.normalise(dve, c, r)
            for c in range(NC):
                r = full[1][:, chunk(c)]
                dve.wait_ge(copied[1], c + 1)
                dve.wait_ge(first_part[1], c + 1)
                dve.tensor_tensor(r, r, parts[1][:, 0, chunk(c)], ALU.subtract).then_inc(left[1], 1)
                dve.wait_ge(left[1], c + 1)
                dve.tensor_copy(parts[1][:, 1, chunk(c)], r).then_inc(second_part[1], 1)
                dve.wait_ge(second_part[1], c + 1)
                dve.tensor_tensor(parts[1][:, 2, chunk(c)], r, parts[1][:, 1, chunk(c)], ALU.subtract).then_inc(third_part[1], 1)
                dve.wait_ge(left[0], c + 1)
                dve.tensor_copy(parts[0][:, 1, chunk(c)], full[0][:, chunk(c)]).then_inc(second_part[0], 1)

        @block.gpsimd
        def _(pool):
            for r in range(rounds):
                for c in range(NC):
                    norm.power(pool, c, r)
            for c in range(NC):
                r = full[0][:, chunk(c)]
                pool.wait_ge(copied[0], c + 1)
                pool.wait_ge(first_part[0], c + 1)
                pool.tensor_tensor(r, r, parts[0][:, 0, chunk(c)], ALU.subtract).then_inc(left[0], 1)
                pool.wait_ge(second_part[0], c + 1)
                pool.tensor_tensor(parts[0][:, 2, chunk(c)], r, parts[0][:, 1, chunk(c)], ALU.subtract).then_inc(third_part[0], 1)

        @block.sync
        def _(sp):
            for c in range(NC):
                sp.wait_ge(third_part[1], c + 1)
                for s in range(SPL):
                    sp.dma_start(k_dram[:, s * DH:(s + 1) * DH, chunk(c)], parts[1][:, s, chunk(c)]).then_inc(stored[1], 16)
                sp.wait_ge(third_part[0], c + 1)
                sp.dma_start(q_dram[:, :, chunk(c)].rearrange("s p t -> p s t"), parts[0][:, :, chunk(c)]).then_inc(stored[0], 16)
            sp.wait_ge(stored[1], 16 * SPL * NC)
            sp.wait_ge(stored[0], 16 * NC)


def attention_heads(nc, g, tag, dram, q_dram, k_dram, v, o_dram, oT, sums, alibi):
    with ExitStack() as ctx:
        m = Memory(nc, ctx, tag)
        NR = PAIRS + (ALIBI if alibi else 0)
        NR_MAX = NR + SPL
        SLOT = 4
        PSLOT = 8
        KB = 3
        QB = 3
        LEAD = 16
        TURN = 4
        q_op = [m.sb(f"q_op{s}", [NR_MAX, TOK], BF16) for s in range(SLOT)]
        k_op = [m.sb(f"k_op{s}", [NR_MAX, TOK], BF16) for s in range(SLOT)]
        vh = [m.sb(f"vh{s}", [P, NT, 32]) for s in range(SLOT)]
        probs = m.sb("probs", [P, PSLOT, CH])
        maxes = m.sb("maxes", [P, NT, NC])
        neg_max = m.sb("neg_max", [P, NT])
        max_parts = m.sb("max_parts", [P, P], BF16)
        max_T = m.sb("max_T", [SPL * NT, P], BF16)
        o_sb = m.sb("o_sb", [P, 2, CH])
        ps_k = m.ps("ps_k", [P, KB, CH])
        ps_q = m.ps("ps_q", [P, QB, CH])
        ps_o = m.ps("ps_o", [P, 2, CH])
        op_loaded = [m.sem(f"op_loaded{s}") for s in range(SLOT)]
        max_loaded = [m.sem(f"max_loaded{s}") for s in range(SLOT)]
        ones_loaded = m.sem("ones_loaded")
        v_set = m.sem("v_set")
        v_ready = m.sem("v_ready")
        q_ready = m.sem("q_ready")
        q_read = m.sem("q_read")
        max_set = m.sem("max_set")
        max_ready = m.sem("max_ready")
        chain = m.sem("chain")
        k_ready = m.sem("k_ready")
        exp_done = m.sem("exp_done")
        pv_done = m.sem("pv_done")
        o_read = m.sem("o_read")
        o_stored = [m.sem(f"o_stored{s}") for s in range(2)]
        OPS = SPL + 1 + (2 if alibi else 0)
        looped = HEADS - SLOT
        o_back = m.sem("o_back")

        q_items = [(t, kc) for t in range(NT) for kc in range(t // TPC + 1)]
        NQ = len(q_items)

        k_items = []
        for c in range(NC):
            k_items += [(c, j, 0, CH) for j in range(TPC * c)]
            k_items += [(c, TPC * c + d, d * P if c else 0, CH - d * P if c else CH) for d in range(TPC)]
        NK = len(k_items)
        ends = [max(i for i, item in enumerate(k_items) if item[0] == c) for c in range(NC)]
        assert NK == NQ and NK % 4 == 0

        def number(i, k):
            return i * SLOT + k

        def use(i, k):
            return i + (k // SLOT + 1)

        def beyond(i, k, n=HEADS):
            return isinstance(i, int) and number(i, k) >= n

        def q_place(n):
            return n + (n >= TURN)

        def q_count(i, k, l):
            if isinstance(i, int) and number(i, k) == 0:
                return l + (l < TURN)
            if beyond(i, k):
                return HEADS * (NQ + 1)
            return number(i, k) * (NQ + 1) + l

        def q_freed(i, k, l):
            if isinstance(i, int) and number(i, k) == 0:
                before = [x for x in range(l % QB, l, QB) if x != TURN]
                return q_count(i, k, before[-1]) if before else 0
            if l < QB:
                return q_count(i, k - 1, max(x for x in range(NQ + 1) if x % QB == l))
            if beyond(i, k):
                return HEADS * (NQ + 1) - 1
            return q_count(i, k, l - QB)

        def stream(turn, item, i, k, p):
            k, n = k + 1 + p // NQ, p % NQ
            if n == TURN and not beyond(i, k, HEADS + 1):
                turn(i, k - 1)
            if not beyond(i, k):
                item(i, k, n)

        def prologue(turn, item):
            for n in range(NQ):
                item(0, 0, n)
            for p in range(LEAD):
                stream(turn, item, 0, 0, p)

        def heads(eng, body):
            with eng.Fori(0, HEADS // SLOT - 1) as i:
                for k in range(SLOT):
                    body(i, k)
            for k in range(SLOT):
                body(HEADS // SLOT - 1, k)

        turned_bank = ps_q[:, TURN % QB, 0:P // 2].bitcast(BF16)

        def stored(i, k, c):
            return number(i, k) * (NC // 2 * 16) + (c // 2 * 16 + 16)

        block = ctx.enter_context(nc.Block())

        @block.tensor
        def _(pe):
            pe.sem_inc(pv_done, PSLOT)

            def turn(i, k):
                pe.wait_ge(max_ready, number(i, k) + 1)
                pe.wait_ge(q_read, q_freed(i, k + 1, TURN))
                pe.transpose(turned_bank, max_parts[:, :], g["ident_b"][:, :]).then_inc(q_ready, 1)

            def item(i, k, n):
                t, kc = q_items[n]
                l = q_place(n)
                bank = l % QB
                width = min(CH, (t + 1) * P - kc * CH)
                if n == 0:
                    pe.wait_ge(op_loaded[k % SLOT], use(i, k) * (16 * OPS))
                freed = q_freed(i, k, l)
                if not isinstance(freed, int) or freed:
                    pe.wait_ge(q_read, freed)
                diagonal = kc == t // TPC
                last = pe.matmul(ps_q[:, bank, 0:width], q_op[k % SLOT][0:NR, tile(t)],
                                 k_op[k % SLOT][0:NR, kc * CH:kc * CH + width], start=True, stop=not diagonal,
                                 skip_group_check=True)
                if diagonal:
                    last = pe.matmul(ps_q[:, bank, width - P:width], g["ident_b"][:, :], g["mask_q"][:, :],
                                     start=False, stop=True, skip_group_check=True)
                last.then_inc(q_ready, 1)

            def scores(i, k, n):
                c, j, first, width = k_items[n]
                if n == 0:
                    pe.wait_ge(max_loaded[k % SLOT], use(i, k) * 16)
                last_use = n - KB if n >= KB else max(x for x in range(NK) if x % KB == n) - NK
                pe.wait_ge(exp_done, number(i, k) * NK + (last_use + 1 + KB))
                d = j - TPC * c
                last = pe.matmul(ps_k[:, n % KB, 0:width], k_op[k % SLOT][:, tile(j)],
                                 q_op[k % SLOT][:, c * CH + first:c * CH + first + width], start=True, stop=d < 0,
                                 skip_group_check=True)
                if d >= 0:
                    m0 = ((TPC - 1 - d) if c == 0 else (TPC - 1)) * P
                    last = pe.matmul(ps_k[:, n % KB, 0:TPC * P - m0], g["ident_b"][:, :],
                                     g["mask_k"][:, m0:TPC * P], start=False, stop=True, skip_group_check=True)
                last.then_inc(k_ready, 1)

            def times_v(i, k, n):
                c, j, first, width = k_items[n]
                if n == 0:
                    pe.wait_ge(v_ready, number(i, k) + 1)
                if n == 0 or n - 1 in ends:
                    pe.wait_ge(o_read, number(i, k) * NC + (c + 1))
                if n % 4 == 0:
                    pe.wait_ge(exp_done, number(i, k) * NK + (n + 4 + KB))
                r = 32 * (j % 4)
                pe.matmul(ps_o[r:r + 32, c % 2, first:first + width], vh[k % SLOT][:, j, :],
                          probs[:, n % PSLOT, 0:width], start=j < 4, stop=j >= TPC * c,
                          skip_group_check=True).then_inc(pv_done, 1)

            def body(i, k):
                for n in range(0, NK, 4):
                    for a in range(n, n + 4):
                        if a + KB < NK:
                            scores(i, k, a + KB)
                        elif not beyond(i, k + 1):
                            scores(i, k + 1, a + KB - NK)
                        stream(turn, item, i, k, a + LEAD)
                    for a in range(n, n + 4):
                        times_v(i, k, a)

            prologue(turn, item)
            for n in range(KB):
                scores(0, 0, n)
            heads(pe, body)

        @block.vector
        def _(dve):
            dve.memset(max_parts[:, :], 0.0).then_inc(max_set, 1)
            dve.memset(maxes[:, :, :], -3e38).then_inc(max_set, 1)
            dve.wait_ge(max_set, 2)

            def turn(i, k):
                dve.wait_ge(q_ready, q_count(i, k + 1, TURN))
                dve.tensor_copy(max_T[:, :], turned_bank[0:SPL * NT, :]).then_inc(q_read, 1)

            def item(i, k, n):
                t, kc = q_items[n]
                l = q_place(n)
                width = min(CH, (t + 1) * P - kc * CH)
                dve.wait_ge(q_ready, q_count(i, k, l))
                dve.tensor_reduce(maxes[:, t, kc:kc + 1], ps_q[:, l % QB, 0:width], AX.X, ALU.max).then_inc(q_read, 1)
                if n == NQ - 1:
                    maxima(i, k)

            def maxima(i, k):
                def part(s):
                    return max_parts[:, s * NT:(s + 1) * NT]

                done = number(i, k) * 5
                dve.wait_ge(q_read, q_count(i, k, NQ))
                dve.tensor_reduce(neg_max[:, :], maxes[:, :, :], AX.X, ALU.max, negate=True).then_inc(chain, 1)
                dve.wait_ge(chain, done + 1)
                dve.tensor_copy(part(0), neg_max[:, :]).then_inc(chain, 1)
                dve.wait_ge(chain, done + 2)
                dve.tensor_tensor(neg_max[:, :], neg_max[:, :], part(0), ALU.subtract).then_inc(chain, 1)
                dve.wait_ge(chain, done + 3)
                dve.tensor_copy(part(1), neg_max[:, :]).then_inc(chain, 1)
                dve.wait_ge(chain, done + 4)
                dve.tensor_tensor(neg_max[:, :], neg_max[:, :], part(1), ALU.subtract).then_inc(chain, 1)
                dve.wait_ge(chain, done + 5)
                dve.tensor_copy(part(2), neg_max[:, :]).then_inc(max_ready, 1)
                dve.wait_ge(max_ready, number(i, k) + 1)

            def body(i, k):
                for n in range(NK):
                    stream(turn, item, i, k, n + LEAD)

            prologue(turn, item)
            heads(dve, body)

        @block.scalar
        def _(act):
            act.sem_inc(exp_done, KB)
            act.sem_inc(o_read, 2)
            AHEAD = 4

            def exps(i, k, n):
                width = k_items[n][3]
                act.wait_ge(k_ready, number(i, k) * NK + (n + 1))
                act.wait_ge(pv_done, number(i, k) * NK + (n + 1))
                act.activation(probs[:, n % PSLOT, 0:width], ps_k[:, n % KB, 0:width], ACT.Exp).then_inc(exp_done, 1)

            def output(i, k, c):
                act.wait_ge(pv_done, number(i, k) * NK + (ends[c] + 1 + PSLOT))
                act.wait_ge(o_stored[c % 2], stored(i, k, c))
                act.activation(o_sb[:, c % 2, :], ps_o[:, c % 2, :], ACT.Copy).then_inc(o_read, 1)

            def body(i, k):
                for n in range(AHEAD, NK):
                    exps(i, k, n)
                    if n - AHEAD in ends:
                        output(i, k, ends.index(n - AHEAD))
                if not beyond(i, k + 1):
                    for n in range(AHEAD):
                        exps(i, k + 1, n)
                output(i, k, NC - 1)

            for n in range(AHEAD):
                exps(0, 0, n)
            heads(act, body)

        @block.gpsimd
        def _(pool):
            for s in range(SLOT):
                pool.memset(vh[s][:, :, :], 0.0).then_inc(v_set, 1)
            pool.wait_ge(v_set, SLOT)
            for s in range(SLOT):
                pool.memset(vh[s][:, :, DH:DH + 1], 1.0).then_inc(v_set, 1)
            pool.wait_ge(v_set, 2 * SLOT)

            def place(i, k):
                pool.tensor_copy(vh[k][:, :, 0:DH], v[:, :, ds(number(i, k) * DH, DH)]).then_inc(v_ready, 1)

            for k in range(SLOT):
                place(0, k)
            with pool.Fori(1, HEADS // SLOT) as i:
                for k in range(SLOT):
                    pool.wait_ge(pv_done, number(i, k - 3) * NK + PSLOT)
                    place(i, k)

        @block.sync
        def _(sp):
            for s in range(2):
                sp.sem_inc(o_stored[s], 16)

            def load(i, k):
                h = number(i, k)
                s = k % SLOT
                PER = SPL * DH
                for a in range(SPL):
                    sp.dma_start(q_op[s][a * PER:(a + 1) * PER, :],
                                 q_dram[a, ds(h * DH, DH), :].unsqueeze(0).broadcast_to([SPL, DH, TOK])).then_inc(op_loaded[s], 16)
                sp.dma_start(k_op[s][0:PAIRS, :],
                             k_dram[ds(h, 1), :, :].broadcast_to([SPL, PER, TOK])).then_inc(op_loaded[s], 16)
                if alibi:
                    sp.dma_start(q_op[s][PAIRS:NR, :], dram["alibi_q"][ds(h, 1), :, :].rearrange("o r t -> (o r) t")).then_inc(op_loaded[s], 16)
                    sp.dma_start(k_op[s][PAIRS:NR, :], dram["alibi_k"][ds(h, 1), :, :].rearrange("o r t -> (o r) t")).then_inc(op_loaded[s], 16)

            def load_maxima(i, k):
                sp.wait_ge(q_read, q_count(i, k + 1, TURN))
                sp.dma_start(q_op[k % SLOT][NR:NR_MAX, :].rearrange("s (t p) -> s t p", p=P),
                             max_T[:, :]).then_inc(max_loaded[k % SLOT], 16)

            def store(i, k, c):
                h = number(i, k)
                sp.wait_ge(o_read, h * NC + (c + 3))
                sp.dma_start(o_dram[ds(h, 1), :, chunk(c)], o_sb[:, c % 2, :]).then_inc(o_stored[c % 2], 16)

            def load_looped():
                for s in range(2):
                    sp.wait_ge(o_stored[s], stored(0, looped, s))
                for r in range(4):
                    rows = o_dram[0:looped, 32 * r:32 * (r + 1), :]
                    sp.dma_start(oT[0:looped * DH, r, :], rows[:, 0:DH, :]).then_inc(o_back, 16)
                    sp.dma_start(sums[0:looped * SB, r, :],
                                 rows[:, DH, :].rearrange("h (b t) -> h b t", b=SB)).then_inc(o_back, 16)

            def load_output(h):
                for s in range(2):
                    sp.wait_ge(o_stored[s], stored(0, h + 1, s))
                rows = o_dram[h, :, :].rearrange("(r d) t -> d r t", r=4)
                sp.dma_start(oT[h * DH:(h + 1) * DH, :, :], rows[0:DH, :, :]).then_inc(o_back, 16)
                sp.dma_start(sums[h * SB:(h + 1) * SB, :, :],
                             rows[DH, :, :].rearrange("r (b t) -> b r t", b=SB)).then_inc(o_back, 16)

            for k in range(SLOT):
                sp.dma_start(k_op[k][NR:NR_MAX, :], dram["ones_b"]).then_inc(ones_loaded, 16)
            sp.wait_ge(ones_loaded, 16 * SLOT)
            for k in range(SLOT):
                load(0, k)
            load_maxima(0, 0)

            def body(i, k):
                for c in range(NC - 1):
                    store(i, k, c)
                if isinstance(i, int) and number(i, k) == looped:
                    load_looped()
                elif beyond(i, k, looped + 1):
                    load_output(number(i, k) - 1)
                if not beyond(i, k + 1):
                    load_maxima(i, k + 1)
                if not beyond(i, k + SLOT):
                    sp.wait_ge(k_ready, number(i, k + 1) * NK)
                    load(i, k + SLOT)
                store(i, k, NC - 1)

            heads(sp, body)
            load_output(HEADS - 1)
            sp.wait_ge(o_back, 16 * (8 + 2 * SLOT))


def attention_out(nc, g, w, tag, x, oT, sums):
    with ExitStack() as ctx:
        m = Memory(nc, ctx, tag)
        inv = m.sb("inv", [HEADS * SB, TOK // SB])
        inv_rows = m.sb("inv_rows", [HEADS, TOK])
        pair = m.sb("pair", [P, 2, TOK // SB])
        total = m.sb("total", [P, 2, CH])
        upper = m.sb("upper", [P, 2, CH])
        ps_s = m.ps("ps_s", [P, 2, CH])
        ps_y = m.ps("ps_y", [P, 2, CH])
        paired = m.sem("paired")
        summed = m.sem("summed")
        inverted = m.sem("inverted")
        rows_ready = m.sem("rows_ready")
        spread_ready = m.sem("spread_ready")
        upper_ready = m.sem("upper_ready")
        lower_ready = m.sem("lower_ready")
        total_ready = m.sem("total_ready")
        normed = m.sem("normed")
        y_ready = m.sem("y_ready")
        added = m.sem("added")
        block = ctx.enter_context(nc.Block())

        @block.tensor
        def _(pe):
            def spread(c):
                if c >= 2:
                    pe.wait_ge(normed, c - 1)
                pe.matmul(ps_s[:, c % 2, :], g["sel_head"][:, :], inv_rows[:, chunk(c)], start=True, stop=True).then_inc(spread_ready, 1)

            pe.wait_ge(rows_ready, 16)
            spread(0)
            for c in range(NC):
                if c + 1 < NC:
                    spread(c + 1)
                pe.wait_ge(normed, c + 1)
                if c >= 2:
                    pe.wait_ge(added, c - 1)
                for j in range(TPC):
                    last = pe.matmul(ps_y[:, c % 2, tile(j)], total[:, c % 2, tile(j)], w["wo"][:, :], start=True, stop=True)
                last.then_inc(y_ready, 1)

        @block.sync
        def _(sp):
            sp.wait_ge(inverted, 1)
            sp.dma_start(inv_rows[:, :].rearrange("h (b t) -> h b t", b=SB), inv[:, :]).then_inc(rows_ready, 16)

        @block.gpsimd
        def _(pool):
            for c in range(NC):
                if c >= 2:
                    pool.wait_ge(total_ready, c - 1)
                pool.tensor_tensor(upper[:, c % 2, :], oT[:, 2, chunk(c)], oT[:, 3, chunk(c)], ALU.add).then_inc(upper_ready, 1)

        @block.vector
        def _(dve):
            def add_partials(c):
                s = c % 2
                if c >= 2:
                    dve.wait_ge(y_ready, c - 1)
                dve.tensor_tensor(total[:, s, :], oT[:, 0, chunk(c)], oT[:, 1, chunk(c)], ALU.add).then_inc(lower_ready, 1)
                dve.wait_ge(lower_ready, c + 1)
                dve.wait_ge(upper_ready, c + 1)
                dve.tensor_tensor(total[:, s, :], total[:, s, :], upper[:, s, :], ALU.add).then_inc(total_ready, 1)

            def add(c):
                dve.wait_ge(y_ready, c + 1)
                xc = x[:, TPC * c:TPC * (c + 1), :]
                dve.tensor_tensor(xc, ps_y[:, c % 2, :].rearrange("p (j f) -> p j f", f=P), xc, ALU.add).then_inc(added, 1)

            dve.tensor_tensor(pair[:, :, :], sums[:, 0:2, :], sums[:, 2:4, :], ALU.add).then_inc(paired, 1)
            dve.wait_ge(paired, 1)
            dve.tensor_tensor(inv[:, :], pair[:, 0, :], pair[:, 1, :], ALU.add).then_inc(summed, 1)
            dve.wait_ge(summed, 1)
            dve.reciprocal(inv[:, :], inv[:, :]).then_inc(inverted, 1)
            for c in range(2):
                add_partials(c)
            for c in range(NC):
                dve.wait_ge(total_ready, c + 1)
                dve.wait_ge(spread_ready, c + 1)
                dve.tensor_tensor(total[:, c % 2, :], total[:, c % 2, :], ps_s[:, c % 2, :], ALU.mult).then_inc(normed, 1)
                if c:
                    add(c - 1)
                    if c + 1 < NC:
                        add_partials(c + 1)
            add(NC - 1)


MAMBA = ["in_T", "conv_w", "conv_b", "x_T", "dt_T", "dt_b", "a_log", "d", "out_T"]
MAMBA_FFN = ["w1_T", "b1", "w2_T", "b2_rows", "norm_w", "ffn_norm_w"]
MOE = ["b1", "b2", "b3", "w1_T", "w2_T", "w3_T"]
QLORA = ["bias_cols", "gamma", "beta"]
QLORA_RAW = ["bias_0", "q_T", "scale_T", "lora_a", "lora_b_T"]
ATT0 = ["wq", "wk", "wv", "wo", "gain"]
ATT1 = ["wq", "wk", "wv", "wo"]
CONST = ["ident", "minus_half"]
CONST_LATE = ["ident_b", "ones_row", "ones_3", "sel", "sel_e", "iota", "mask_q", "mask_k", "sel_head"]


def build(nc, dram, out):
    Memory.count = 0
    with ExitStack() as ctx:
        m = Memory(nc, ctx, "all")
        x = m.sb("x", [P, NT, P])
        xn = m.sb("xn", [P, NT, P])
        x_loaded = m.sem("x_loaded")
        stored = m.sem("stored")
        g = group(m, dram, "c", CONST)
        g.late = group(m, dram, "c", CONST_LATE)
        g.update(g.late)
        m0 = group(m, dram, "m0", MAMBA)
        m0_ffn = group(m, dram, "m0", MAMBA_FFN)
        a0 = group(m, dram, "a0", ATT0)
        m1 = group(m, dram, "m1", MAMBA)
        ql = group(m, dram, "ql", QLORA)
        a1 = group(m, dram, "a1", ATT1)
        ql["eff"] = m.sb("ql_eff", [P, QL, P])
        ql["bias3"] = m.sb("ql_bias3", [SPL, QL // 2, P], BF16)
        late = g.late.loads + m0_ffn.loads + a0.loads + m1.loads + ql.loads + a1.loads

        with nc.Block() as block:
            @block.sync
            def _(sp):
                start_loads(sp, g.loads)
                for c in range(0, NC, 2):
                    sp.dma_start(x[:, TPC * c:TPC * (c + 1), :], dram["x"][:, TPC * c:TPC * (c + 1), :]).then_inc(x_loaded, 16)
                start_loads(sp, m0.loads)
                sp.wait_ge(g.loaded, g.full)
                sp.wait_ge(x_loaded, 16 * NC)

            @block.scalar
            def _(act):
                for c in range(1, NC, 2):
                    act.dma_start(x[:, TPC * c:TPC * (c + 1), :], dram["x"][:, TPC * c:TPC * (c + 1), :]).then_inc(x_loaded, 16)

        plan = [
            lambda: mamba(nc, g, m0, "m0", x, xn, lambda gated: mamba_out_ffn(nc, g, m0, m0_ffn, "m0o", x, xn, gated), late),
            lambda: moe(nc, g, dram, "e0", x, xn),
            lambda: attention(nc, g, a0, "a0", dram, x, xn, False),
            lambda: moe(nc, g, dram, "e1", x, xn),
            lambda: mamba(nc, g, m1, "m1", x, xn, lambda gated: mamba_out_add(nc, m1, "m1o", x, gated)),
            lambda: (qlora_weights(nc, dram, "qw", ql["eff"], ql["bias3"]), qlora_mlp(nc, g, ql, "q0", x, xn)),
            lambda: attention(nc, g, a1, "a1", dram, x, xn, True),
            lambda: qlora_mlp(nc, g, ql, "q1", x, xn),
        ]
        for step in plan:
            with fresh_semaphores(nc):
                step()
        with nc.Block() as block:
            @block.sync
            def _(sp):
                sp.dma_start(out, x[:, :, :]).then_inc(stored, 16)
                for w in (m0, m0_ffn, a0, m1, ql, a1):
                    sp.wait_ge(w.loaded, w.full)
                sp.wait_ge(stored, 16)


def constants():
    bf = mybir.dt.np(BF16)
    k, q = np.arange(P)[:, None], np.arange(P)[None, :]
    sel = np.zeros((SPL, 2 * NS, 2 * NS, P), np.float32)
    for n in range(2 * NS):
        sel[:, n, n] = 1
    sel_e = np.zeros((SPL, NE, NE, P), np.float32)
    for n in range(NE):
        sel_e[:, n, n] = 1
    sel_head = np.zeros((HEADS, HEADS, DH), np.float32)
    for h in range(HEADS):
        sel_head[h, h] = 1
    slopes = (2.0 ** (-8.0 / HEADS * (np.arange(HEADS, dtype=np.float32) + 1.0))).astype(np.float32)
    pos = np.arange(TOK)
    hi, lo = (pos // P * P).astype(np.float32), (pos % P).astype(np.float32)
    qa, ka = np.zeros((HEADS, ALIBI, TOK), np.float32), np.zeros((HEADS, ALIBI, TOK), np.float32)
    rest = slopes.copy()
    for s in range(SPL):
        part = rest.astype(bf).astype(np.float32)
        rest = rest - part
        for r, p in enumerate((hi, lo)):
            row = 4 * s + 2 * r
            qa[:, row], ka[:, row] = part[:, None], p
            qa[:, row + 1], ka[:, row + 1] = p, -part[:, None]
    return {
        "c_ident": np.eye(P, dtype=np.float32),
        "c_ident_b": np.eye(P, dtype=np.float32).astype(bf),
        "c_ones_row": np.ones((1, P), np.float32),
        "c_ones_3": np.ones((SPL, P), np.float32).astype(bf),
        "c_sel": sel.reshape(SPL * 2 * NS, 2 * NS, P).astype(bf),
        "c_sel_e": sel_e.reshape(SPL * NE, NE, P).astype(bf),
        "c_iota": np.tile(np.arange(NE, dtype=np.float32), (P, 1)),
        "c_minus_half": np.full((P, NT), -0.5, np.float32),
        "c_mask_q": np.where(q > k, NEG, 0.0).astype(bf),
        "c_mask_k": np.concatenate([np.full((P, 3 * P), NEG), np.where(k > q, NEG, 0.0)], 1).astype(bf),
        "c_sel_head": sel_head.reshape(HEADS, P),
        "alibi_q": qa.astype(bf),
        "alibi_k": ka.astype(bf),
        "ones_b": np.ones((SPL, TOK), np.float32).astype(bf),
    }


def layouts(i):
    def halves(a):
        return a.reshape((a.shape[0] // P, P) + a.shape[1:]).swapaxes(0, 1)

    def rows(a):
        return np.broadcast_to(a, (P, P))

    r = {"x": i["L0_attn_a_input_tensor"][0].reshape(NT, P, P).swapaxes(0, 1)}
    a = {k[len("L0_attn_a_"):]: v for k, v in i.items() if k.startswith("L0_attn_a_")}
    r.update({
        "m0_in_T": a["in_proj_w"].T, "m0_conv_w": halves(a["conv_w"]), "m0_conv_b": halves(a["conv_b"]),
        "m0_x_T": halves(a["x_proj_w"].T), "m0_dt_T": a["dt_proj_w"].T, "m0_dt_b": halves(a["dt_proj_b"]),
        "m0_a_log": halves(a["A_log"]), "m0_d": halves(a["D"]), "m0_out_T": halves(a["out_proj_w"].T),
        "m0_w1_T": a["ffn_w1"].T, "m0_b1": halves(a["ffn_b1"]), "m0_w2_T": halves(a["ffn_w2"].T),
        "m0_b2_rows": np.tile(a["ffn_b2"], TPC)[None], "m0_norm_w": rows(a["norm_w"]),
        "m0_ffn_norm_w": rows(a["ffn_norm_w"]),
    })
    a = {k[len("L1_attn_a_"):]: v for k, v in i.items() if k.startswith("L1_attn_a_")}
    r.update({
        "m1_in_T": a["W_in"], "m1_conv_w": halves(a["conv_w"]), "m1_conv_b": halves(a["conv_b"]),
        "m1_x_T": halves(a["W_x"]), "m1_dt_T": a["W_dt"], "m1_dt_b": halves(a["b_dt"]),
        "m1_a_log": halves(a["A_log"]), "m1_d": halves(a["D"]), "m1_out_T": halves(a["W_out"]),
    })
    a = {k[len("L0_ffn_"):]: v for k, v in i.items() if k.startswith("L0_ffn_")}
    r.update({
        "me_g_T": a["Wg"].T, "me_w1_T": a["W1"].transpose(2, 0, 1), "me_w2_T": a["W2"].transpose(2, 0, 1),
        "me_w3_T": halves(a["W3"].transpose(2, 0, 1)).transpose(0, 2, 1, 3),
        "me_b1": halves(a["b1"].T).transpose(0, 2, 1), "me_b2": halves(a["b2"].T).transpose(0, 2, 1), "me_b3": a["b3"],
    })
    wkv = i["L0_attn_b_Wkv"]
    r.update({"a0_wq": i["L0_attn_b_Wq"], "a0_wk": wkv[:, :P], "a0_wv": wkv[:, P:], "a0_wo": i["L0_attn_b_Wo"],
              "a0_gain": i["L0_attn_b_g_ln"][:, None]})
    w_in = i["L1_attn_b_w_in"]
    r.update({"a1_wq": w_in[:P].T, "a1_wk": w_in[P:2 * P].T, "a1_wv": w_in[2 * P:].T, "a1_wo": i["L1_attn_b_w_out"].T})
    a = {k[len("L1_ffn_"):]: v for k, v in i.items() if k.startswith("L1_ffn_")}
    r.update({
        "qr_q_T": a["qweights"].transpose(2, 0, 1),
        "qr_scale_T": np.repeat(a["scales"], P // a["scales"].shape[2], axis=2).transpose(2, 0, 1),
        "qr_bias_0": a["biases"][0::2], "ql_bias_cols": a["biases"].T,
        "qr_lora_a": a["lora_a"].swapaxes(0, 1), "qr_lora_b_T": a["lora_b"].transpose(2, 0, 1),
        "ql_gamma": a["ln_gamma"].T, "ql_beta": a["ln_beta"].T,
    })
    return r


def kernel(**inputs):
    import concourse.bacc as bacc
    from concourse.bass_utils import run_bass_kernel_spmd

    nc = bacc.Bacc("TRN2", target_bir_lowering=False, num_devices=1)
    arrays, dram = {}, {}
    laid = layouts({k: np.asarray(v) for k, v in inputs.items()})
    for name, a in {**laid, **constants()}.items():
        a = np.ascontiguousarray(a)
        arrays[f"in_{name}"] = a
        dram[name] = nc.dram_tensor(f"in_{name}", a.shape, mybir.dt.from_np(a.dtype), kind="ExternalInput").ap()
    out = nc.dram_tensor("out_x", (P, NT, P), F32, kind="ExternalOutput").ap()
    build(nc, dram, out)
    r = run_bass_kernel_spmd(nc, [arrays], core_ids=[0])
    got = r.results[0]["out_x"].reshape(P, NT, P).swapaxes(0, 1).reshape(1, TOK, P)
    return np.ascontiguousarray(got)
```

```python
from contextlib import ExitStack, contextmanager

import concourse.bass as bass
import numpy as np
from concourse import mybir

F32 = mybir.dt.float32
BF16 = mybir.dt.bfloat16
I32 = mybir.dt.int32
U32 = mybir.dt.uint32
ALU = mybir.AluOpType
ACT = mybir.ActivationFunctionType
AX = mybir.AxisListType
ds = bass.ds

P = 128
TOK = 2048
NT = TOK // P
CH = 512
NC = TOK // CH
TPC = CH // P
D_IN = 256
NH2 = D_IN // P
NS = 16
RANK = 8
XDBL = RANK + 2 * NS
CONV = 4
SPL = 3
SCT = 1024
NSC = TOK // SCT
FF = 512
NF = FF // P
NE = 8
EF = 256
NEF = EF // P
FE = 1
HEADS = 16
DH = P // HEADS
PAIRS = SPL * SPL * DH
ALIBI = 12
NEG = -1e30
QL = 6
LORA = 32
SB = P // HEADS


class Memory:

    count = 0

    def __init__(self, nc, ctx, tag):
        self.nc, self.ctx, self.tag = nc, ctx, tag

    def name(self, n):
        Memory.count += 1
        return f"{self.tag}_{n}_{Memory.count}"

    def sb(self, n, shape, dt=F32):
        return self.ctx.enter_context(self.nc.sbuf_tensor(self.name(n), list(shape), dt))

    def ps(self, n, shape, dt=F32):
        return self.ctx.enter_context(self.nc.psum_tensor(self.name(n), list(shape), dt))

    def sem(self, n):
        return self.nc.alloc_semaphore(self.name(n))


@contextmanager
def fresh_semaphores(nc):
    before = nc.snapshot_sems()
    yield
    nc.clear_and_free_semaphores(nc.allocated_since(before))
    nc.all_engine_barrier()


def tile(i):
    return slice(i * P, (i + 1) * P)


def chunk(c):
    return slice(c * CH, (c + 1) * CH)


class Weights(dict):
    pass


def group(m, dram, tag, names):
    w = Weights()
    w.loaded = m.sem(tag + "_loaded")
    w.full = 16 * len(names)
    w.loads = []
    for n in names:
        src = dram[f"{tag}_{n}"]
        w[n] = m.sb(f"{tag}_{n}", src.shape, src.dtype)
        w.loads.append((w[n], src, w.loaded))
    return w


def split_load(w, n, first, sem):
    k = [dst is w[n] for dst, _, _ in w.loads].index(True)
    dst, src, loaded = w.loads[k]
    w.loads[k] = (dst[:, :first], src[:, :first], loaded)
    return [(dst[:, first:], src[:, first:], sem)]


def start_loads(eng, loads):
    for dst, src, sem in loads:
        eng.dma_start(dst[tuple(slice(None) for _ in dst.shape)], src).then_inc(sem, 16)


class LayerNorm:

    def __init__(self, m, g, x, xn, xT, turned, rounds=1, w=None):
        self.g, self.x, self.xn, self.xT, self.turned, self.rounds, self.w = g, x, xn, xT, turned, rounds, w
        self.bn = m.sb("bn_stats", [P, NT, 6])
        self.mean_var = m.sb("mean_var", [P, NT, 2])
        self.var_eps = m.sb("var_eps", [P, NT])
        self.rstd = m.sb("rstd", [P, NT])
        self.stats_done = m.sem("stats_done")
        self.aggr_done = m.sem("aggr_done")
        self.var_ready = m.sem("var_ready")
        self.rstd_ready = m.sem("rstd_ready")
        self.normed = m.sem("normed")
        self.turned_ready = m.sem("turned_ready")
        self.copied = m.sem("copied")

    def stats(self, dve, c, r=0):
        src = self.x if r == 0 else self.xn
        done = NT * r + TPC * c
        if r:
            dve.wait_ge(self.normed, NT * (r - 1) + TPC * (c + 1))
        for j in range(TPC):
            dve.bn_stats(self.bn[:, TPC * c + j, :], src[:, TPC * c + j, :]).then_inc(self.stats_done, 1)
        for j in range(TPC):
            dve.wait_ge(self.stats_done, done + j + 1)
            dve.bn_aggr(self.mean_var[:, TPC * c + j, :], self.bn[:, TPC * c + j, :]).then_inc(self.aggr_done, 1)
        dve.wait_ge(self.aggr_done, done + TPC)
        tiles = slice(TPC * c, TPC * (c + 1))
        dve.tensor_scalar(self.var_eps[:, tiles], self.mean_var[:, tiles, 1], 1e-5, None, ALU.add).then_inc(self.var_ready, 1)

    def power(self, pool, c, r=0):
        pool.wait_ge(self.var_ready, NC * r + c + 1)
        tiles = slice(TPC * c, TPC * (c + 1))
        pool.tensor_tensor(self.rstd[:, tiles], self.var_eps[:, tiles], self.g["minus_half"][:, 0:TPC],
                           ALU.pow).then_inc(self.rstd_ready, 1)

    def normalise(self, dve, c, r=0):
        src = self.x if r == 0 else self.xn
        dve.wait_ge(self.rstd_ready, NC * r + c + 1)
        for i in range(TPC * c, TPC * (c + 1)):
            dve.tensor_scalar(self.xn[:, i, :], src[:, i, :], self.mean_var[:, i, 0:1], self.rstd[:, i:i + 1],
                              ALU.subtract, ALU.mult).then_inc(self.normed, 1)

    def turn(self, pe, c):
        if c >= 2:
            pe.wait_ge(self.copied, c - 1)
        for j in range(TPC):
            pe.wait_ge(self.normed, NT * (self.rounds - 1) + TPC * c + j + 1)
            last = pe.transpose(self.turned[:, c % 2, tile(j)], self.xn[:, TPC * c + j, :], self.g["ident"][:, :])
        last.then_inc(self.turned_ready, 1)

    def copy(self, act, c):
        if self.w is not None and c == 0:
            act.wait_ge(self.w.loaded, self.w.full)
        act.wait_ge(self.turned_ready, c + 1)
        act.activation(self.xT[:, chunk(c)], self.turned[:, c % 2, :], ACT.Identity,
                       scale=1.0 if self.w is None else self.w["gain"][:, 0:1]).then_inc(self.copied, 1)


def mamba(nc, g, w, tag, x, xn, finish, loads=()):
    with ExitStack() as ctx:
        m = Memory(nc, ctx, tag)
        gate = m.sb("gate", [P, NH2, TOK])
        u = m.sb("u", [P, NH2, TOK])
        with ExitStack() as inner:
            mi = Memory(nc, inner, tag)
            delta = mi.sb("delta", [P, NH2, TOK])
            du = mi.sb("du", [P, NH2, TOK])
            bc3 = mi.sb("bc3", [SPL * 2 * NS, TOK], BF16)
            neg_a = mi.sb("neg_a", [P, NH2, NS])
            diag_d = mi.sb("diag_d", [P, NH2, P])
            mamba_inputs(nc, g, w, tag + "in", x, xn, u, gate, delta, du, bc3, neg_a, diag_d, loads)
            mamba_scan(nc, g, tag + "sc", u, delta, du, bc3, neg_a, diag_d, gate)
        finish(gate)


def mamba_inputs(nc, g, w, tag, x, xn, u, gate, delta, du, bc3, neg_a, diag_d, loads):
    with ExitStack() as ctx:
        m = Memory(nc, ctx, tag)
        xT = m.sb("xT", [P, TOK])
        raw = m.sb("raw", [P, NH2, CONV - 1 + TOK])
        xd = m.sb("xd", [XDBL, TOK])
        rest = m.sb("rest", [XDBL, 2, CH])
        parts = m.sb("parts", [XDBL, SPL, TOK], BF16)
        e = m.sb("e", [P, NH2, TOK])
        halves = (slice(0, TOK // 2), slice(TOK // 2, TOK))
        ln = raw[:, :, 0:TOK]
        t = du
        turned = m.ps("turned", [P, 2, CH])
        RING = 6
        acc = m.ps("acc", [P, RING, CH])
        norm = LayerNorm(m, g, x, xn, xT, turned)
        made = m.sem("made")
        raw_copied = m.sem("raw_copied")
        padded = m.sem("padded")
        own_tap = m.sem("own_tap")
        conv = m.sem("conv")
        u_ready = m.sem("u_ready")
        xd_ready = m.sem("xd_ready")
        abs_done = m.sem("abs_done")
        relu_done = m.sem("relu_done")
        gate_ready = m.sem("gate_ready")
        exp_done = m.sem("exp_done")
        ln_done = m.sem("ln_done")
        rounded = m.sem("rounded")
        lost = [m.sem(f"lost{n}") for n in range(2)]
        delta_ready = m.sem("delta_ready")
        du_ready = m.sem("du_ready")
        a_exp = m.sem("a_exp")
        chain = m.sem("chain")
        split_0 = m.sem("split_0")
        split_1 = m.sem("split_1")
        split_2 = m.sem("split_2")
        rest_ready = m.sem("rest_ready")
        stacked = m.sem("stacked")
        block = ctx.enter_context(nc.Block())

        STEPS = NC + 3
        items = []
        for s in range(STEPS):
            items += [("u", s, h) for h in range(NH2) if s < NC]
            items += [("dt", s - 3, h) for h in range(NH2) if s >= 3]
            items += [("xd", s - 2, 0)] if 2 <= s < NC + 2 else []
            items += [("gate", s - 1, h) for h in range(NH2) if 1 <= s <= NC]
        late = {"u": 0, "gate": 1, "xd": 2, "dt": 3}
        reader = {"u": raw_copied, "xd": xd_ready, "dt": relu_done, "gate": gate_ready}

        def bank(what, c, h=0):
            return acc[:, items.index((what, c, h)) % RING, :]

        def tap(c, k, h):
            return NH2 * ((CONV - 1) * c + k) + h + 1

        def product_made(what, c, h=0):
            return items.index((what, c, h)) + 1

        @block.tensor
        def _(pe):
            pe.wait_ge(w.loaded, w.full)
            for s in range(STEPS):
                if s < NC:
                    norm.turn(pe, s)
                for k, (what, c, h) in enumerate(items):
                    if c + late[what] != s:
                        continue
                    if k >= RING:
                        what0, c0, h0 = items[k - RING]
                        pe.wait_ge(reader[what0], c0 + 1 if what0 == "xd" else NH2 * c0 + h0 + 1)
                    if what == "u" or what == "gate":
                        if h == 0:
                            pe.wait_ge(norm.copied, c + 1)
                        wt = w["in_T"][:, tile((what == "gate") * NH2 + h)]
                        pe.matmul(bank(what, c, h), wt, xT[:, chunk(c)], start=True, stop=True).then_inc(made, 1)
                    elif what == "xd":
                        pe.wait_ge(u_ready, NH2 * (c + 1))
                        for half in range(NH2):
                            last = pe.matmul(bank("xd", c)[0:XDBL, :], w["x_T"][:, half, :], u[:, half, chunk(c)],
                                             start=half == 0, stop=half == NH2 - 1)
                        last.then_inc(made, 1)
                    else:
                        pe.wait_ge(xd_ready, c + 1)
                        pe.matmul(bank("dt", c, h), w["dt_T"][:, tile(h)], xd[0:RANK, chunk(c)],
                                  start=True, stop=True).then_inc(made, 1)

        @block.scalar
        def _(act):
            act.wait_ge(w.loaded, w.full)
            for s in range(STEPS):
                if 2 <= s < NC + 2:
                    c = s - 2
                    for h in range(NH2):
                        act.wait_ge(conv, tap(c, CONV - 2, h))
                        act.activation(u[:, h, chunk(c)], u[:, h, chunk(c)], ACT.Silu).then_inc(u_ready, 1)
                if s < NC:
                    norm.copy(act, s)
                    for h in range(NH2):
                        act.wait_ge(made, product_made("u", s, h))
                        act.activation(u[:, h, chunk(s)], bank("u", s, h), ACT.Identity, bias=w["conv_b"][:, h:h + 1],
                                       scale=w["conv_w"][:, h, CONV - 1:CONV]).then_inc(own_tap, 1)
                        act.activation(raw[:, h, CONV - 1 + s * CH:CONV - 1 + (s + 1) * CH], bank("u", s, h),
                                       ACT.Copy).then_inc(raw_copied, 1)
                if s >= 3:
                    c = s - 3
                    for h in range(NH2):
                        act.wait_ge(made, product_made("dt", c, h))
                        act.activation(e[:, h, chunk(c)], bank("dt", c, h), ACT.Abs,
                                       bias=w["dt_b"][:, h:h + 1]).then_inc(abs_done, 1)
                    act.wait_ge(rest_ready, c + 1)
                    act.activation(parts[:, 1, chunk(c)], rest[:, c % 2, :], ACT.Copy).then_inc(split_1, 1)
                if 2 <= s < NC + 2:
                    c = s - 2
                    act.wait_ge(made, product_made("xd", c))
                    act.activation(xd[:, chunk(c)], bank("xd", c)[0:XDBL, :], ACT.Copy).then_inc(xd_ready, 1)
                    act.wait_ge(xd_ready, c + 1)
                    act.activation(parts[:, 0, chunk(c)], xd[:, chunk(c)], ACT.Copy).then_inc(split_0, 1)
                if 1 <= s <= NC:
                    c = s - 1
                    for h in range(NH2):
                        act.wait_ge(made, product_made("gate", c, h))
                        act.activation(gate[:, h, chunk(c)], bank("gate", c, h), ACT.Silu).then_inc(gate_ready, 1)
                if s == NC + 1:
                    act.wait_ge(abs_done, NC)
                    act.activation(neg_a[:, :, :], w["a_log"][:, :, :], ACT.Exp).then_inc(a_exp, 1)
                    act.activation(e[:, :, halves[0]], e[:, :, halves[0]], ACT.Exp, scale=-1.0).then_inc(exp_done, 1)
            act.wait_ge(abs_done, NH2 * NC)
            act.activation(e[:, :, halves[1]], e[:, :, halves[1]], ACT.Exp, scale=-1.0).then_inc(exp_done, 1)
            act.wait_ge(conv, tap(NC - 1, CONV - 2, NH2 - 1))
            for n, half in enumerate(halves):
                act.wait_ge(exp_done, n + 1)
                act.activation(ln[:, :, half], e[:, :, half], ACT.Ln, bias=1.0).then_inc(ln_done, 1)

        def lost_in_rounding(eng, n):
            half = halves[n]
            eng.wait_ge(rounded, n + 1)
            eng.tensor_tensor(t[:, :, half], e[:, :, half], t[:, :, half], ALU.subtract).then_inc(lost[n], 1)
            eng.wait_ge(lost[n], 1)
            eng.wait_ge(relu_done, NC * (n + 1))
            eng.tensor_tensor(delta[:, :, half], delta[:, :, half], t[:, :, half], ALU.add).then_inc(lost[n], 1)

        def times_u(eng, n):
            eng.wait_ge(delta_ready, n + 1)
            eng.tensor_tensor(du[:, :, halves[n]], delta[:, :, halves[n]], u[:, :, halves[n]], ALU.mult).then_inc(du_ready, 1)

        def round_sum(dve, n):
            half = halves[n]
            dve.wait_ge(exp_done, n + 1)
            dve.tensor_scalar(t[:, :, half], e[:, :, half], 1.0, 1.0, ALU.add, ALU.subtract).then_inc(rounded, 1)

        @block.vector
        def _(dve):
            links = [0]

            def link(ins):
                links[0] += 1
                ins.then_inc(chain, 1)
                dve.wait_ge(chain, links[0])

            dve.memset(raw[:, :, 0:CONV - 1], 0.0).then_inc(padded, 1)
            norm.stats(dve, 0)
            for s in range(STEPS):
                if s + 1 < NC:
                    norm.stats(dve, s + 1)
                if s < NC:
                    norm.normalise(dve, s)
                if s == 0:
                    dve.wait_ge(padded, 1)
                    dve.wait_ge(w.loaded, w.full)
                if 1 <= s <= NC:
                    c = s - 1
                    for h in range(NH2):
                        dve.wait_ge(raw_copied, NH2 * c + h + 1)
                        dve.wait_ge(own_tap, NH2 * c + h + 1)
                    for k in range(CONV - 1):
                        for h in range(NH2):
                            if k:
                                dve.wait_ge(conv, tap(c, k - 1, h))
                            dve.scalar_tensor_tensor(u[:, h, chunk(c)], raw[:, h, k + c * CH:k + (c + 1) * CH],
                                                     w["conv_w"][:, h, k:k + 1], u[:, h, chunk(c)],
                                                     ALU.mult, ALU.add).then_inc(conv, 1)
                if s >= 3:
                    c = s - 3
                    for h in range(NH2):
                        dve.wait_ge(abs_done, NH2 * c + h + 1)
                        dve.tensor_scalar(delta[:, h, chunk(c)], bank("dt", c, h), w["dt_b"][:, h:h + 1], 0.0,
                                          ALU.add, ALU.max).then_inc(relu_done, 1)
                if s == NC + 1:
                    round_sum(dve, 0)
            dve.wait_ge(a_exp, 1)
            link(dve.tensor_scalar(neg_a[:, :, :], neg_a[:, :, :], -1.0, None, ALU.mult))
            for h in range(NH2):
                link(dve.tensor_scalar(diag_d[:, h, :], g["ident"][:, :], w["d"][:, h:h + 1], None, ALU.mult))
            round_sum(dve, 1)
            lost_in_rounding(dve, 1)
            for n, half in enumerate(halves):
                dve.wait_ge(ln_done, n + 1)
                dve.wait_ge(lost[n], 2)
                dve.tensor_tensor(delta[:, :, half], delta[:, :, half], ln[:, :, half], ALU.add).then_inc(delta_ready, 1)
            times_u(dve, 1)

        @block.gpsimd
        def _(pool):
            norm.power(pool, 0)
            for s in range(STEPS):
                if s + 1 < NC:
                    norm.power(pool, s + 1)
                if s >= 3:
                    c = s - 3
                    pool.wait_ge(split_1, c + 1)
                    pool.tensor_tensor(parts[:, 2, chunk(c)], rest[:, c % 2, :], parts[:, 1, chunk(c)],
                                       ALU.subtract).then_inc(split_2, 1)
                if 2 <= s < NC + 2:
                    c = s - 2
                    pool.wait_ge(split_0, c + 1)
                    if c >= 2:
                        pool.wait_ge(split_2, c - 1)
                    pool.tensor_tensor(rest[:, c % 2, :], xd[:, chunk(c)], parts[:, 0, chunk(c)], ALU.subtract).then_inc(rest_ready, 1)
                if s == NC + 1:
                    lost_in_rounding(pool, 0)
            times_u(pool, 0)

        @block.sync
        def _(sp):
            start_loads(sp, loads)
            for c in range(NC):
                sp.wait_ge(split_2, c + 1)
                for s in range(SPL):
                    sp.dma_start(bc3[2 * NS * s:2 * NS * (s + 1), chunk(c)],
                                 parts[RANK:XDBL, s, chunk(c)]).then_inc(stacked, 16)
            sp.wait_ge(stacked, 16 * SPL * NC)
            sp.wait_ge(g.late.loaded, g.late.full)


def mamba_scan(nc, g, tag, u, delta, du, bc3, neg_a, diag_d, gate):
    with ExitStack() as ctx:
        m = Memory(nc, ctx, tag)
        decay = [m.sb(f"decay{s}", [P, NH2, SCT]) for s in range(2)]
        state = [m.sb(f"state{s}", [P, NH2, SCT]) for s in range(2)]
        read = [m.sb(f"read{s}", [P, NH2, SCT]) for s in range(2)]
        c_rows = [m.sb(f"c_rows{s}", [P, SCT]) for s in range(2)]
        drive = m.sb("drive", [P, NH2, SCT])
        carry = m.sb("carry", [P, NH2, NS])
        psy = m.ps("psy", [P, NH2, SCT])
        psb = m.ps("psb", [P, SCT])
        psc = m.ps("psc", [P, SCT])
        b_ready = m.sem("b_ready")
        c_ready = m.sem("c_ready")
        c_copied = m.sem("c_copied")
        decay_ready = m.sem("decay_ready")
        drive_ready = m.sem("drive_ready")
        scanned = m.sem("scanned")
        carried = m.sem("carried")
        read_ready = m.sem("read_ready")
        summed = m.sem("summed")
        skip_done = m.sem("skip_done")
        gated = m.sem("gated")
        cleared = m.sem("cleared")
        NB = SCT // CH
        block = ctx.enter_context(nc.Block())

        def first_pair(k, step):
            for s in range(2):
                step(k, NS * k + s, s, s)

        def other_pairs(eng, k, step):
            with eng.Fori(1, NS // 2) as i:
                for s in range(2):
                    step(k, 2 * i + (NS * k + s), 2 * i + s, s)

        def in_pairs(eng, step):
            for k in range(NSC):
                first_pair(k, step)
                other_pairs(eng, k, step)

        def at_least(eng, sem, q, value):
            if not isinstance(q, int) or value > 0:
                eng.wait_ge(sem, value)

        @block.tensor
        def _(pe):
            def sum_states(q, s, ends):
                pe.wait_ge(read_ready, q + 1)
                for h in range(NH2):
                    for b in range(NB):
                        last = pe.matmul(psy[:, h, chunk(b)], g["ident"][:, :], read[s][:, h, chunk(b)],
                                         start=False, stop=ends, skip_group_check=True)
                last.then_inc(summed, 1)

            def rows(k, q, n, s):
                at_least(pe, drive_ready, q, q * NH2)
                for b in range(NB):
                    last = pe.matmul(psb[:, chunk(b)], g["sel"][:, n, :],
                                     bc3[:, k * SCT + b * CH:k * SCT + (b + 1) * CH], start=True, stop=True)
                last.then_inc(b_ready, 1)
                at_least(pe, c_copied, q, q)
                for b in range(NB):
                    last = pe.matmul(psc[:, chunk(b)], g["sel"][:, n + NS, :],
                                     bc3[:, k * SCT + b * CH:k * SCT + (b + 1) * CH], start=True, stop=True)
                last.then_inc(c_ready, 1)

            first_pair(0, rows)
            for k in range(NSC):
                if k:
                    pe.wait_ge(gated, k)
                for h in range(NH2):
                    for b in range(NB):
                        pe.matmul(psy[:, h, chunk(b)], diag_d[:, h, :],
                                  u[:, h, k * SCT + b * CH:k * SCT + (b + 1) * CH],
                                  start=True, stop=False, skip_group_check=True)
                with pe.Fori(1, NS // 2) as i:
                    for s in range(2):
                        rows(k, 2 * i + (NS * k + s), 2 * i + s, s)
                        sum_states(2 * i + (NS * k + s - 2), s, False)
                if k + 1 < NSC:
                    first_pair(k + 1, rows)
                for s in range(2):
                    sum_states(NS * (k + 1) - 2 + s, s, s == 1)

        @block.scalar
        def _(act):
            def step(k, q, n, s):
                at_least(act, scanned, q, q * NH2 - NH2)
                for h in range(NH2):
                    act.activation(decay[s][:, h, :], delta[:, h, k * SCT:(k + 1) * SCT], ACT.Exp,
                                   scale=neg_a[:, h, ds(n, 1)]).then_inc(decay_ready, 1)
                act.wait_ge(c_ready, q + 1)
                at_least(act, read_ready, q, q - 1)
                act.activation(c_rows[s][:, :], psc[:, :], ACT.Copy).then_inc(c_copied, 1)

            in_pairs(act, step)

        @block.vector
        def _(dve):
            dve.memset(carry[:, :, :], 0.0).then_inc(cleared, 1)
            dve.wait_ge(cleared, 1)

            def step(k, q, n, s):
                dve.wait_ge(b_ready, q + 1)
                for h in range(NH2):
                    at_least(dve, scanned, q, q * NH2 + (h - 1))
                    dve.tensor_tensor(drive[:, h, :], du[:, h, k * SCT:(k + 1) * SCT], psb[:, :], ALU.mult).then_inc(drive_ready, 1)
                at_least(dve, carried, q, q - 1 if k + 1 < NSC else NS * (NSC - 1))
                at_least(dve, read_ready, q, q - 1)
                for h in range(NH2):
                    dve.wait_ge(drive_ready, q * NH2 + (h + 1))
                    dve.wait_ge(decay_ready, q * NH2 + (h + 1))
                    dve.tensor_tensor_scan(state[s][:, h, :], decay[s][:, h, :], drive[:, h, :],
                                           carry[:, h, ds(n, 1)], ALU.mult, ALU.add).then_inc(scanned, 1)

            first_pair(0, step)
            for k in range(NSC):
                other_pairs(dve, k, step)
                if k + 1 < NSC:
                    first_pair(k + 1, step)
                dve.wait_ge(summed, NS * (k + 1))
                dve.tensor_tensor(gate[:, :, k * SCT:(k + 1) * SCT], psy[:, :, :],
                                  gate[:, :, k * SCT:(k + 1) * SCT], ALU.mult).then_inc(gated, 1)

        @block.gpsimd
        def _(pool):
            def step(k, q, n, s):
                pool.wait_ge(scanned, q * NH2 + NH2)
                if k + 1 < NSC:
                    pool.tensor_copy(carry[:, :, ds(n, 1)], state[s][:, :, SCT - 1:SCT]).then_inc(carried, 1)
                pool.wait_ge(c_copied, q + 1)
                at_least(pool, summed, q, q - 1)
                pool.tensor_tensor(read[s][:, :, :], state[s][:, :, :],
                                   c_rows[s][:, :].unsqueeze(1).broadcast_to([P, NH2, SCT]),
                                   ALU.mult).then_inc(read_ready, 1)

            in_pairs(pool, step)


def mamba_out_add(nc, w, tag, x, gated, raw, eff_all, bias3):
    with ExitStack() as ctx:
        m = Memory(nc, ctx, tag)
        parts = m.sb("parts", [QL // 2, SPL, P], BF16)
        rest = m.sb("rest", [QL // 2, P])
        acc = m.ps("acc", [P, NC, CH])
        psl = m.ps("psl", [P, 2, CH])
        summed = m.sem("summed")
        added = m.sem("added")
        chain = m.sem("chain")
        lora_ready = m.sem("lora_ready")
        parts_ready = m.sem("parts_ready")
        stacked = m.sem("stacked")
        half = QL // 2
        block = ctx.enter_context(nc.Block())

        @block.sync
        def _(sp):
            sp.wait_ge(parts_ready, SPL)
            for s in range(SPL):
                sp.dma_start(bias3[s:s + 1, :, :], parts[:, s, :]).then_inc(stacked, 16)
            sp.wait_ge(stacked, 16 * SPL)

        @block.tensor
        def _(pe):
            pe.wait_ge(raw.loaded, raw.full)
            for k in range(QL):
                last = pe.matmul(psl[:, k // half, tile(k % half)], raw["lora_a"][:, k, :], raw["lora_b_T"][:, k, :],
                                 start=True, stop=True)
            last.then_inc(lora_ready, 1)
            for c in range(NC):
                for j in range(TPC):
                    for h in range(NH2):
                        last = pe.matmul(acc[:, c, tile(j)], gated[:, h, tile(TPC * c + j)], w["out_T"][:, h, :],
                                         start=h == 0, stop=h == NH2 - 1)
                last.then_inc(summed, 1)

        @block.vector
        def _(dve):
            links = [0]

            def link(ins):
                links[0] += 1
                ins.then_inc(chain, 1)
                dve.wait_ge(chain, links[0])

            dve.wait_ge(raw.loaded, raw.full)
            dve.tensor_copy(parts[:, 0, :], raw["bias_0"][:, :]).then_inc(parts_ready, 1)
            dve.wait_ge(parts_ready, 1)
            link(dve.tensor_tensor(rest[:, :], raw["bias_0"][:, :], parts[:, 0, :], ALU.subtract))
            dve.tensor_copy(parts[:, 1, :], rest[:, :]).then_inc(parts_ready, 1)
            dve.wait_ge(parts_ready, 2)
            dve.tensor_tensor(parts[:, 2, :], rest[:, :], parts[:, 1, :], ALU.subtract).then_inc(parts_ready, 1)
            link(dve.tensor_copy(eff_all[:, :, :], raw["q_T"][:, :, :]))
            link(dve.tensor_scalar(eff_all[:, :, :], eff_all[:, :, :], 1.0 / 7.5, -1.0, ALU.mult, ALU.add))
            link(dve.tensor_tensor(eff_all[:, :, :], eff_all[:, :, :], raw["scale_T"][:, :, :], ALU.mult))
            dve.wait_ge(lora_ready, 1)
            for k in range(2):
                eff = eff_all[:, half * k:half * (k + 1), :]
                link(dve.tensor_tensor(eff, psl[:, k, 0:half * P].rearrange("p (m f) -> p m f", f=P), eff, ALU.add))
            for c in range(NC):
                dve.wait_ge(summed, c + 1)
                xc = x[:, TPC * c:TPC * (c + 1), :]
                dve.tensor_tensor(xc, acc[:, c, :].rearrange("p (j f) -> p j f", f=P), xc, ALU.add).then_inc(added, 1)


def mamba_out_ffn(nc, g, w_out, w, tag, x, xn, gated):
    with ExitStack() as ctx:
        m = Memory(nc, ctx, tag)
        r = m.sb("r", [P, TPC, P])
        sq = m.sb("sq", [P, TPC, P])
        ms = m.sb("ms", [P, TPC])
        rms = m.sb("rms", [P, TPC])
        hm = m.sb("hm", [P, NT, P])
        hT = m.sb("hT", [P, CH])
        act1 = m.sb("act1", [P, NF, CH])
        pso = m.ps("pso", [P, CH])
        pst = m.ps("pst", [P, CH])
        ps1 = m.ps("ps1", [P, NF, CH])
        ps2 = m.ps("ps2", [P, CH])
        o_ready = m.sem("o_ready")
        o_read = m.sem("o_read")
        h_ready = m.sem("h_ready")
        t_ready = m.sem("t_ready")
        hT_ready = m.sem("hT_ready")
        f1_ready = m.sem("f1_ready")
        gelu_done = m.sem("gelu_done")
        f2_ready = m.sem("f2_ready")
        f2_read = m.sem("f2_read")
        ms_ready = m.sem("ms_ready")
        rms_ready = m.sem("rms_ready")
        chain = m.sem("chain")
        added = m.sem("added")
        block = ctx.enter_context(nc.Block())

        @block.tensor
        def _(pe):
            def project(c):
                if c:
                    pe.wait_ge(o_read, c)
                for j in range(TPC):
                    for h in range(NH2):
                        last = pe.matmul(pso[:, tile(j)], gated[:, h, tile(TPC * c + j)], w_out["out_T"][:, h, :],
                                         start=h == 0, stop=h == NH2 - 1)
                last.then_inc(o_ready, 1)

            def turn(c):
                if c:
                    pe.wait_ge(hT_ready, c)
                for j in range(TPC):
                    pe.wait_ge(h_ready, TPC * c + j + 1)
                    last = pe.transpose(pst[:, tile(j)], hm[:, TPC * c + j, :], g["ident"][:, :])
                last.then_inc(t_ready, 1)

            project(0)
            project(1)
            turn(0)
            pe.wait_ge(w.loaded, w.full)
            for c in range(NC):
                pe.wait_ge(hT_ready, c + 1)
                for k in range(NF):
                    if c:
                        pe.wait_ge(gelu_done, NF * (c - 1) + k + 1)
                    pe.matmul(ps1[:, k, :], w["w1_T"][:, tile(k)], hT[:, :], start=True, stop=True).then_inc(f1_ready, 1)
                if c + 2 < NC:
                    project(c + 2)
                if c + 1 < NC:
                    turn(c + 1)
                pe.wait_ge(gelu_done, NF * (c + 1))
                if c:
                    pe.wait_ge(f2_read, c)
                pe.matmul(ps2[:, :], g["ones_row"][:, 0:P], w["b2_rows"][:, :], start=True, stop=False, skip_group_check=True)
                for j in range(TPC):
                    for k in range(NF):
                        last = pe.matmul(ps2[:, tile(j)], act1[:, k, tile(j)], w["w2_T"][:, k, :],
                                         start=False, stop=k == NF - 1, skip_group_check=True)
                last.then_inc(f2_ready, 1)

        @block.scalar
        def _(act):
            def turned(c):
                act.wait_ge(t_ready, c + 1)
                if c:
                    act.wait_ge(f1_ready, NF * c)
                act.activation(hT[:, :], pst[:, :], ACT.Copy).then_inc(hT_ready, 1)

            act.wait_ge(w.loaded, w.full)
            for c in range(NC):
                if c == 0:
                    turned(0)
                if c:
                    act.wait_ge(f2_ready, c)
                for k in range(NF):
                    act.wait_ge(f1_ready, NF * c + k + 1)
                    act.activation(act1[:, k, :], ps1[:, k, :], ACT.Gelu, bias=w["b1"][:, k:k + 1]).then_inc(gelu_done, 1)
                if c + 1 < NC:
                    turned(c + 1)

        @block.gpsimd
        def _(pool):
            for n in range(2 * NC):
                pool.wait_ge(ms_ready, n + 1)
                pool.tensor_tensor(rms[:, :], ms[:, :], g["minus_half"][:, 0:TPC], ALU.pow).then_inc(rms_ready, 1)

        @block.vector
        def _(dve):
            links = [0]
            norms = [0]

            def link(ins):
                links[0] += 1
                ins.then_inc(chain, 1)
                dve.wait_ge(chain, links[0])

            def rms_of_r():
                link(dve.tensor_tensor(sq[:, :, :], r[:, :, :], r[:, :, :], ALU.mult))
                link(dve.tensor_reduce(ms[:, :], sq[:, :, :], AX.X, ALU.add))
                dve.tensor_scalar(ms[:, :], ms[:, :], 1.0 / P, 1e-12, ALU.mult, ALU.add).then_inc(ms_ready, 1)
                norms[0] += 1
                dve.wait_ge(rms_ready, norms[0])

            def first(c):
                dve.wait_ge(o_ready, c + 1)
                dve.tensor_tensor(r[:, :, :], pso[:, :].rearrange("p (j f) -> p j f", f=P),
                                  xn[:, TPC * c:TPC * (c + 1), :], ALU.add).then_inc(o_read, 1)
                dve.wait_ge(o_read, c + 1)
                rms_of_r()
                for j in range(TPC):
                    dve.scalar_tensor_tensor(hm[:, TPC * c + j, :], r[:, j, :], rms[:, j:j + 1], w["norm_w"][:, :],
                                             ALU.mult, ALU.mult).then_inc(h_ready, 1)
                dve.wait_ge(h_ready, TPC * (c + 1))

            def second(c):
                dve.wait_ge(f2_ready, c + 1)
                dve.tensor_tensor(r[:, :, :], ps2[:, :].rearrange("p (j f) -> p j f", f=P),
                                  hm[:, TPC * c:TPC * (c + 1), :], ALU.add).then_inc(f2_read, 1)
                dve.wait_ge(f2_read, c + 1)
                rms_of_r()
                for j in range(TPC):
                    link(dve.scalar_tensor_tensor(r[:, j, :], r[:, j, :], rms[:, j:j + 1], w["ffn_norm_w"][:, :],
                                                  ALU.mult, ALU.mult))
                xc = x[:, TPC * c:TPC * (c + 1), :]
                dve.tensor_tensor(xc, r[:, :, :], xc, ALU.add).then_inc(added, 1)
                dve.wait_ge(added, c + 1)

            dve.wait_ge(w.loaded, w.full)
            first(0)
            first(1)
            for c in range(NC):
                if c + 2 < NC:
                    first(c + 2)
                second(c)


def moe(nc, g, dram, tag, x, xn):
    with ExitStack() as ctx:
        m = Memory(nc, ctx, tag)
        w1 = group(m, dram, "me", ["b1", "w1_T"])
        w2 = group(m, dram, "me", ["b2", "w2_T"])
        rest_loaded = m.sem("rest_loaded")
        w1_rest, w2_rest = split_load(w1, "w1_T", FE, rest_loaded), split_load(w2, "w2_T", FE, rest_loaded)
        wg = group(m, dram, "me", ["g_T"])
        w3 = group(m, dram, "me", ["w3_T", "b3_rows"])
        K = NE * NEF
        TURN = K - 3
        SL = 4
        xT = m.sb("xT", [P, TOK])
        comb3_T = m.sb("comb3_T", [SPL * NE, TOK], BF16)
        b3_rest = m.sb("b3_rest", [SPL * NE, P])
        b3_parts = m.sb("b3_parts", [SPL * NE, SPL, P], BF16)
        silu = m.sb("silu", [P, SL, CH])
        mid = m.sb("mid", [P, K, CH])
        hid = m.sb("hid", [P, SL, CH])
        oT = m.sb("oT", [P, CH])
        logits = m.sb("logits", [P, NT, NE])
        best = m.sb("best", [P, NT, 8])
        index = m.sb("index", [P, NT, 8], U32)
        index_f = m.sb("index_f", [P, NT, 2])
        gap = m.sb("gap", [P, NT, 1])
        e_gap = m.sb("e_gap", [P, NT, 1])
        weight0 = m.sb("weight0", [P, NT, 1])
        weight1 = m.sb("weight1", [P, NT, 1])
        is0 = m.sb("is0", [P, NT, NE])
        is1 = m.sb("is1", [P, NT, NE])
        parts = m.sb("parts", [P, NT, SPL * NE], BF16)
        psg = m.ps("psg", [P, NEF, CH])
        psv = m.ps("psv", [P, NEF, CH])
        with ExitStack() as early:
            me = Memory(nc, early, tag + "ln")
            turned = me.ps("turned", [P, 2, CH])
            psl = me.ps("psl", [P, CH])[:, 0:NT * NE].rearrange("p (i e) -> p i e", e=NE)
        norm = LayerNorm(m, g, x, xn, xT, turned)
        pso = m.ps("pso", [P, CH])
        pst = m.ps("pst", [P, CH])
        with ExitStack() as early:
            psp = Memory(nc, early, tag + "tp").ps("psp", [SPL * NE, 2, TOK // 2], BF16)
        psc = m.ps("psc", [P, 2, CH])
        logits_ready = m.sem("logits_ready")
        maxed = m.sem("maxed")
        indexed = m.sem("indexed")
        gap_ready = m.sem("gap_ready")
        exp_done = m.sem("exp_done")
        chain = m.sem("chain")
        weights_ready = m.sem("weights_ready")
        parts_ready = m.sem("parts_ready")
        parts_turned = m.sem("parts_turned")
        parts_copied = m.sem("parts_copied")
        b3_chain = m.sem("b3_chain")
        g_ready = m.sem("g_ready")
        v_ready = m.sem("v_ready")
        c_ready = m.sem("c_ready")
        g_free = m.sem("g_free")
        v_free = m.sem("v_free")
        hid_made = m.sem("hid_made")
        hid_free = m.sem("hid_free")
        o_free = m.sem("o_free")
        t_ready = m.sem("t_ready")
        added = m.sem("added")
        x_flat = x[:, :, :].rearrange("p i f -> p (i f)")
        block = ctx.enter_context(nc.Block())

        @block.sync
        def _(sp):
            start_loads(sp, w1.loads + wg.loads + w1_rest + w3.loads)

        @block.tensor
        def _(pe):
            pe.sem_inc(hid_free, SL)

            def tokens(c):
                return chunk(c) if isinstance(c, int) else ds(c * CH, CH)

            def product(c, e):
                for f in range(NEF):
                    k = NEF * e + f
                    pe.wait_ge(hid_made, c * K + (k + 2))
                    if k == 0:
                        pe.wait_ge(o_free, c + 1)
                    pe.matmul(pso[:, :], w3["w3_T"][:, e, f, :], hid[:, k % SL, :], start=k == 0,
                              stop=k == K - 1, skip_group_check=True).then_inc(hid_free, 1)

            def add_b3(c):
                for s in range(SPL):
                    pe.matmul(pso[:, :], b3_parts[:, s, :], comb3_T[:, tokens(c)], start=False, stop=False,
                              skip_group_check=True)

            def item(c, e, f):
                k = NEF * e + f
                fs = slice(f * P, (f + 1) * P)
                pe.wait_ge(g_free, c * K + (k + 1))
                pe.matmul(psg[:, f, :], w1["w1_T"][:, e, fs], xT[:, tokens(c)], start=True, stop=True).then_inc(g_ready, 1)
                pe.wait_ge(v_free, c * K + (k + 3))
                pe.matmul(psv[:, f, :], w2["w2_T"][:, e, fs], xT[:, tokens(c)], start=True, stop=True).then_inc(v_ready, 1)

            def weight(c, e):
                pe.matmul(psc[:, e % 2, :], g["sel_e"][:, e, :], comb3_T[:, tokens(c)], start=True,
                          stop=True).then_inc(c_ready, 1)

            def turn(c):
                pe.wait_ge(o_free, c + 2)
                pe.wait_ge(added, c + 1)
                for j in range(TPC):
                    last = pe.transpose(pst[:, tile(j)], oT[:, tile(j)], g["ident"][:, :])
                last.then_inc(t_ready, 1)

            def tail(c, more):
                add_b3(c)
                if more:
                    item(c + 1, 0, 0)
                product(c, NE - 1)
                if more:
                    weight(c + 1, 0)
                    item(c + 1, 0, 1)
                turn(c)

            def body(c, more):
                for e in range(1, NE):
                    item(c, e, 0)
                    product(c, e - 1)
                    weight(c, e)
                    item(c, e, 1)
                tail(c, more)

            for k in range(K):
                if k < NC:
                    norm.turn(pe, k)
                if k == 0:
                    pe.wait_ge(norm.copied, 1)
                    pe.wait_ge(w1.loaded, w1.full)
                    pe.wait_ge(w2.loaded, w2.full)
                if k == NEF * FE:
                    pe.wait_ge(rest_loaded, 32)
                item(0, k // NEF, k % NEF)
                if k == 0:
                    pe.wait_ge(wg.loaded, wg.full)
                if k < NC:
                    pe.wait_ge(norm.copied, k + 1)
                    for i in range(TPC * k, TPC * (k + 1)):
                        last = pe.matmul(psl[:, i, :], xT[:, tile(i)], wg["g_T"][:, :], start=True, stop=True)
                if k == NC - 1:
                    last.then_inc(logits_ready, 1)
                if k == TURN + 1:
                    pe.wait_ge(parts_copied, 1)
                    weight(0, 0)
                if k == TURN:
                    pe.wait_ge(parts_ready, SPL)
                    for i in range(NT):
                        last = pe.transpose(psp[:, i // (NT // 2), tile(i % (NT // 2))], parts[:, i, :], g["ident_b"][:, :])
                        if i % (NT // 2) == NT // 2 - 1:
                            last.then_inc(parts_turned, 1)
            pe.wait_ge(parts_copied, 2)
            weight(0, 1)
            pe.wait_ge(w3.loaded, w3.full)
            for e in range(NE - 1):
                product(0, e)
                if e + 2 < NE:
                    weight(0, e + 2)
            pe.wait_ge(b3_chain, 5)
            tail(0, True)
            with pe.Fori(1, NC - 1) as c:
                body(c, True)
            body(NC - 1, False)

        @block.scalar
        def _(act):
            start_loads(act, w2.loads + w2_rest)
            act.sem_inc(g_free, 2)
            act.sem_inc(o_free, 1)

            def gate(c, k):
                e, f = divmod(k, NEF)
                act.wait_ge(g_ready, c * K + (k + 1))
                act.wait_ge(v_free, c * K + (k + 1))
                act.activation(silu[:, k % SL, :], psg[:, f, :], ACT.Silu, bias=w1["b1"][:, e, f:f + 1]).then_inc(g_free, 1)

            def tail(c, more):
                if more:
                    gate(c + 1, 0)
                act.wait_ge(hid_free, c * K + (K + SL))
                act.wait_ge(added, c + 1)
                act.activation(oT[:, :], pso[:, :], ACT.Copy).then_inc(o_free, 1)

            def body(c, more):
                for k in range(1, K):
                    gate(c, k)
                tail(c, more)

            act.wait_ge(w1.loaded, w1.full)
            for k in range(K):
                if k < NC:
                    norm.copy(act, k)
                gate(0, k)
                if k == 6:
                    act.wait_ge(gap_ready, 1)
                    act.activation(e_gap[:, :, :], gap[:, :, :], ACT.Exp).then_inc(exp_done, 1)
                if k in (TURN, TURN + 1):
                    h = k - TURN
                    act.wait_ge(parts_turned, h + 1)
                    act.activation(comb3_T[:, h * (TOK // 2):(h + 1) * (TOK // 2)], psp[:, h, :], ACT.Copy).then_inc(parts_copied, 1)
            tail(0, True)
            with act.Fori(1, NC - 1) as c:
                body(c, True)
            body(NC - 1, False)

        @block.vector
        def _(dve):
            dve.sem_inc(v_free, SL)
            dve.sem_inc(hid_made, 1)
            dve.sem_inc(added, 1)
            links = [0]

            def link(ins):
                links[0] += 1
                ins.then_inc(chain, 1)
                dve.wait_ge(chain, links[0])

            def spread(col, n):
                return col.broadcast_to([P, NT, n])

            def find_best():
                dve.wait_ge(logits_ready, 1)
                link(dve.tensor_copy(logits[:, :, :], psl[:, :, :]))
                for i in range(NT):
                    dve.max(best[:, i, :], logits[:, i, :]).then_inc(maxed, 1)

            def find_index():
                for i in range(NT):
                    dve.wait_ge(maxed, i + 1)
                    dve.max_index(index[:, i, :], best[:, i, :], logits[:, i, :]).then_inc(indexed, 1)

            def find_gap():
                dve.wait_ge(maxed, NT)
                dve.tensor_tensor(gap[:, :, :], best[:, :, 1:2], best[:, :, 0:1], ALU.subtract).then_inc(gap_ready, 1)

            def mark():
                dve.wait_ge(indexed, NT)
                link(dve.tensor_copy(index_f[:, :, :], index[:, :, 0:2]))
                iota = g["iota"][:, :].unsqueeze(1).broadcast_to([P, NT, NE])
                link(dve.tensor_tensor(is0[:, :, :], iota, spread(index_f[:, :, 0:1], NE), ALU.is_equal))
                link(dve.tensor_tensor(is1[:, :, :], iota, spread(index_f[:, :, 1:2], NE), ALU.is_equal))

            def softmax():
                dve.wait_ge(exp_done, 1)
                link(dve.tensor_scalar(weight1[:, :, :], e_gap[:, :, :], 1.0, None, ALU.add))
                link(dve.reciprocal(weight0[:, :, :], weight1[:, :, :]))
                link(dve.tensor_tensor(weight1[:, :, :], e_gap[:, :, :], weight0[:, :, :], ALU.mult))

            def put_weights():
                link(dve.tensor_tensor(is0[:, :, :], is0[:, :, :], spread(weight0[:, :, :], NE), ALU.mult))
                link(dve.tensor_tensor(is1[:, :, :], is1[:, :, :], spread(weight1[:, :, :], NE), ALU.mult))
                dve.tensor_tensor(is0[:, :, :], is0[:, :, :], is1[:, :, :], ALU.add).then_inc(weights_ready, 1)

            def split_high():
                dve.wait_ge(weights_ready, 1)
                dve.tensor_copy(parts[:, :, 0:NE], is0[:, :, :]).then_inc(parts_ready, 1)
                dve.wait_ge(parts_ready, 1)
                link(dve.tensor_tensor(is1[:, :, :], is0[:, :, :], parts[:, :, 0:NE], ALU.subtract))

            def split_low():
                dve.tensor_copy(parts[:, :, NE:2 * NE], is1[:, :, :]).then_inc(parts_ready, 1)
                dve.wait_ge(parts_ready, 2)
                dve.tensor_tensor(parts[:, :, 2 * NE:3 * NE], is1[:, :, :], parts[:, :, NE:2 * NE],
                                  ALU.subtract).then_inc(parts_ready, 1)

            def split_b3():
                dve.wait_ge(w3.loaded, w3.full)
                b3 = w3["b3_rows"]
                dve.tensor_copy(b3_parts[:, 0, :], b3[:, :]).then_inc(b3_chain, 1)
                dve.wait_ge(b3_chain, 1)
                dve.tensor_tensor(b3_rest[:, :], b3[:, :], b3_parts[:, 0, :], ALU.subtract).then_inc(b3_chain, 1)
                dve.wait_ge(b3_chain, 2)
                dve.tensor_copy(b3_parts[:, 1, :], b3_rest[:, :]).then_inc(b3_chain, 1)
                dve.wait_ge(b3_chain, 3)
                dve.tensor_tensor(b3[:, :], b3_rest[:, :], b3_parts[:, 1, :], ALU.subtract).then_inc(b3_chain, 1)
                dve.wait_ge(b3_chain, 4)
                dve.tensor_copy(b3_parts[:, 2, :], b3[:, :]).then_inc(b3_chain, 1)

            def make_mid(c, k, slot):
                e, f = divmod(k, NEF)
                dve.wait_ge(v_ready, c * K + (k + 1))
                dve.wait_ge(g_free, c * K + (k + 3))
                dve.scalar_tensor_tensor(mid[:, slot, :], psv[:, f, :], w2["b2"][:, e, f:f + 1], silu[:, k % SL, :],
                                         ALU.add, ALU.mult).then_inc(v_free, 1)

            def make_hid(c, k, slot):
                e = k // NEF
                dve.wait_ge(v_free, c * K + (k + SL + 1))
                dve.wait_ge(c_ready, c * NE + (e + 1))
                dve.wait_ge(hid_free, c * K + (k + 1))
                dve.tensor_tensor(hid[:, k % SL, :], mid[:, slot, :], psc[:, e % 2, :], ALU.mult).then_inc(hid_made, 1)

            def hidden(c, k):
                dve.wait_ge(hid_made, c * K + (k + 1))
                make_mid(c, k, k % 2)
                make_hid(c, k, k % 2)

            def tail(c, more):
                if more:
                    for k in range(NEF):
                        hidden(c + 1, k)
                dve.wait_ge(t_ready, c + 1)
                xc = x_flat[:, ds(c * CH, CH)]
                dve.tensor_tensor(xc, pst[:, :], xc, ALU.add).then_inc(added, 1)

            def body(c, more):
                for k in range(NEF, K):
                    hidden(c, k)
                tail(c, more)

            norm.stats(dve, 0)
            norm.stats(dve, 1)
            norm.normalise(dve, 0)
            norm.stats(dve, 2)
            norm.normalise(dve, 1)
            dve.wait_ge(w2.loaded, w2.full)
            make_mid(0, 0, 0)
            norm.stats(dve, 3)
            norm.normalise(dve, 2)
            make_mid(0, 1, 1)
            norm.normalise(dve, 3)
            make_mid(0, 2, 2)
            find_best()
            make_mid(0, 3, 3)
            find_gap()
            find_index()
            make_mid(0, 4, 4)
            make_mid(0, 5, 5)
            mark()
            make_mid(0, 6, 6)
            make_mid(0, 7, 7)
            softmax()
            make_mid(0, 8, 8)
            put_weights()
            make_mid(0, 9, 9)
            split_high()
            make_mid(0, 10, 10)
            split_low()
            for k in range(11, K - 1):
                make_mid(0, k, k)
            make_hid(0, 0, 0)
            make_hid(0, 1, 1)
            make_mid(0, K - 1, K - 1)
            for k in range(2, K):
                make_hid(0, k, k)
                if k == K // 2:
                    split_b3()
            tail(0, True)
            with dve.Fori(1, NC - 1) as c:
                body(c, True)
            body(NC - 1, False)

        @block.gpsimd
        def _(pool):
            for c in range(NC):
                norm.power(pool, c)


def qlora_mlp(nc, g, w, tag, x, xn):
    with ExitStack() as ctx:
        m = Memory(nc, ctx, tag)
        hT = m.sb("hT", [P, TOK])
        stats = m.sb("stats", [P, TPC, 6])
        mean_var = m.sb("mean_var", [P, TPC, 2])
        var_eps = m.sb("var_eps", [P, 2, TPC])
        minus_mean = m.sb("minus_mean", [P, 2, TPC])
        rstd = m.sb("rstd", [P, 2, TPC])
        shift = m.sb("shift", [P, 2, TPC])
        yn = m.sb("yn", [P, 2, CH])
        act1 = m.sb("act1", [P, 2, CH])
        psy = m.ps("psy", [P, 2, CH])
        pst = m.ps("pst", [P, 2, CH])
        psz = m.ps("psz", [P, 2, CH])
        psx = m.ps("psx", [P, 2, CH])
        norm = LayerNorm(m, g, x, xn, hT, psx)
        y_ready = m.sem("y_ready")
        stats_done = m.sem("stats_done")
        aggr_done = m.sem("aggr_done")
        mean_ready = m.sem("mean_ready")
        var_ready = m.sem("var_ready")
        rstd_ready = m.sem("rstd_ready")
        shift_ready = m.sem("shift_ready")
        normed = m.sem("normed")
        t_ready = m.sem("t_ready")
        gelu_done = m.sem("gelu_done")
        z_ready = m.sem("z_ready")
        h_ready = m.sem("h_ready")
        x_ready = m.sem("x_ready")
        added = m.sem("added")
        N = QL // 2 * NC
        block = ctx.enter_context(nc.Block())

        @block.tensor
        def _(pe):
            def linear(n):
                b, c = divmod(n, NC)
                if b:
                    pe.wait_ge(h_ready, n - NC + 1)
                else:
                    pe.wait_ge(norm.copied, c + 1)
                if n >= 2:
                    pe.wait_ge(normed, TPC * (n - 1))
                pe.matmul(psy[:, n % 2, :], g["ones_3"][:, :], w["bias3"][:, b, :].unsqueeze(1).broadcast_to([SPL, TPC, P]),
                          start=True, stop=False, skip_group_check=True)
                for j in range(TPC):
                    last = pe.matmul(psy[:, n % 2, tile(j)], hT[:, tile(TPC * c + j)], w["eff"][:, 2 * b, :],
                                     start=False, stop=True, skip_group_check=True)
                last.then_inc(y_ready, 1)

            def turn(n):
                if n >= 2:
                    pe.wait_ge(gelu_done, n - 1)
                for j in range(TPC):
                    pe.wait_ge(normed, TPC * n + j + 1)
                    last = pe.transpose(pst[:, n % 2, tile(j)], yn[:, n % 2, tile(j)], g["ident"][:, :])
                last.then_inc(t_ready, 1)

            def linear2(n):
                pe.wait_ge(gelu_done, n + 1)
                if n >= 2:
                    pe.wait_ge(h_ready, n - 1)
                pe.matmul(psz[:, n % 2, :], w["eff"][:, 2 * (n // NC) + 1, :], act1[:, n % 2, :],
                          start=True, stop=True).then_inc(z_ready, 1)

            norm.turn(pe, 0)
            for n in range(N + 3):
                if n + 1 < NC:
                    norm.turn(pe, n + 1)
                if n >= 3:
                    linear2(n - 3)
                if 2 <= n < N + 2:
                    turn(n - 2)
                if n < N:
                    linear(n)
            for c in range(NC):
                pe.wait_ge(h_ready, N - NC + c + 1)
                if c >= 2:
                    pe.wait_ge(added, c - 1)
                for j in range(TPC):
                    last = pe.transpose(psx[:, c % 2, tile(j)], hT[:, tile(TPC * c + j)], g["ident"][:, :])
                last.then_inc(x_ready, 1)

        @block.vector
        def _(dve):
            def moments(n):
                dve.wait_ge(y_ready, n + 1)
                if n:
                    dve.wait_ge(aggr_done, TPC * n)
                for j in range(TPC):
                    dve.bn_stats(stats[:, j, :], psy[:, n % 2, tile(j)]).then_inc(stats_done, 1)
                if n:
                    dve.wait_ge(var_ready, n)
                for j in range(TPC):
                    dve.wait_ge(stats_done, TPC * n + j + 1)
                    dve.bn_aggr(mean_var[:, j, :], stats[:, j, :]).then_inc(aggr_done, 1)
                dve.wait_ge(aggr_done, TPC * (n + 1))
                if n >= 2:
                    dve.wait_ge(shift_ready, n - 1)
                dve.tensor_scalar(minus_mean[:, n % 2, :], mean_var[:, :, 0], -1.0, None, ALU.mult).then_inc(mean_ready, 1)
                dve.wait_ge(mean_ready, n + 1)
                dve.tensor_scalar(var_eps[:, n % 2, :], mean_var[:, :, 1], 1e-5, None, ALU.add).then_inc(var_ready, 1)

            def residual(n):
                b, c = divmod(n, NC)
                dve.wait_ge(z_ready, n + 1)
                if b:
                    dve.wait_ge(h_ready, n - NC + 1)
                dve.scalar_tensor_tensor(hT[:, chunk(c)], psz[:, n % 2, :], w["bias_cols"][:, 2 * b + 1:2 * b + 2],
                                         hT[:, chunk(c)], ALU.add, ALU.add).then_inc(h_ready, 1)

            norm.stats(dve, 0)
            norm.stats(dve, 1)
            norm.normalise(dve, 0)
            for n in range(N + 3):
                if n + 2 < NC:
                    norm.stats(dve, n + 2)
                if n + 1 < NC:
                    norm.normalise(dve, n + 1)
                if n >= 3:
                    residual(n - 3)
                if n < N:
                    moments(n)
            for c in range(NC):
                dve.wait_ge(x_ready, c + 1)
                xc = x[:, TPC * c:TPC * (c + 1), :]
                dve.tensor_tensor(xc, psx[:, c % 2, :].rearrange("p (j f) -> p j f", f=P), xc, ALU.add).then_inc(added, 1)

        @block.gpsimd
        def _(pool):
            norm.power(pool, 0)
            norm.power(pool, 1)
            for n in range(N):
                if n + 2 < NC:
                    norm.power(pool, n + 2)
                pool.wait_ge(var_ready, n + 1)
                if n >= 2:
                    pool.wait_ge(normed, TPC * (n - 1))
                pool.tensor_tensor(rstd[:, n % 2, :], var_eps[:, n % 2, :], g["minus_half"][:, 0:TPC],
                                   ALU.pow).then_inc(rstd_ready, 1)
                pool.wait_ge(rstd_ready, n + 1)
                pool.tensor_tensor(shift[:, n % 2, :], minus_mean[:, n % 2, :], rstd[:, n % 2, :],
                                   ALU.mult).then_inc(shift_ready, 1)

        @block.scalar
        def _(act):
            def gelu(n):
                act.wait_ge(t_ready, n + 1)
                if n >= 2:
                    act.wait_ge(z_ready, n - 1)
                act.activation(act1[:, n % 2, :], pst[:, n % 2, :], ACT.Gelu, bias=w["beta"][:, n // NC:n // NC + 1],
                               scale=w["gamma"][:, n // NC:n // NC + 1]).then_inc(gelu_done, 1)

            norm.copy(act, 0)
            def normalise(n):
                act.wait_ge(shift_ready, n + 1)
                if n >= 2:
                    act.wait_ge(t_ready, n - 1)
                for j in range(TPC):
                    act.activation(yn[:, n % 2, tile(j)], psy[:, n % 2, tile(j)], ACT.Identity,
                                   bias=shift[:, n % 2, j:j + 1], scale=rstd[:, n % 2, j:j + 1]).then_inc(normed, 1)

            for n in range(N + 2):
                if n + 1 < NC:
                    norm.copy(act, n + 1)
                if n >= 2:
                    gelu(n - 2)
                if 1 <= n <= N:
                    normalise(n - 1)


def attention(nc, g, w, tag, dram, x, xn, alibi):
    with ExitStack() as ctx:
        m = Memory(nc, ctx, tag)
        v = m.sb("v", [P, NT, P])
        q_dram = nc.dram_tensor(tag + "_q_parts", (HEADS, SPL, DH, TOK), BF16, kind="Internal").ap()
        k_dram = nc.dram_tensor(tag + "_k_parts", (HEADS, DH, SPL, TOK), BF16, kind="Internal").ap()
        o_dram = nc.dram_tensor(tag + "_outputs", (HEADS, P, TOK), F32, kind="Internal").ap()
        with ExitStack() as inner:
            xT = Memory(nc, inner, tag).sb("xT", [P, TOK])
            attention_project(nc, g, w, tag + "pr", x, xn, xT, v, q_dram, k_dram, alibi)
        oT = m.sb("oT", [P, 4, TOK])
        sums = m.sb("sums", [HEADS * SB, 4, TOK // SB])
        attention_heads(nc, g, tag + "hd", dram, q_dram, k_dram, v, o_dram, oT, sums, alibi)
        attention_out(nc, g, w, tag + "ou", x, oT, sums)


def attention_project(nc, g, w, tag, x, xn, xT, v, q_dram, k_dram, alibi):
    with ExitStack() as ctx:
        m = Memory(nc, ctx, tag)
        rest = [m.sb(n + "_rest", [P, TOK]) for n in ("q", "k")]
        parts = [m.sb(n, [P, SPL, TOK], BF16) for n in ("q_parts", "k_parts")]
        turned = m.ps("turned", [P, 2, CH])
        acc = m.ps("acc", [P, 2, SPL, CH])
        rounds = 1 if alibi else 2
        scale = (float(DH) ** -0.5, 1.0)
        norm = LayerNorm(m, g, x, xn, xT, turned, rounds=rounds, w=None if alibi else w)
        projected = m.sem("projected")
        v_copied = m.sem("v_copied")
        first_part = [m.sem(n + "_first_part") for n in ("q", "k")]
        second_part = [m.sem(n + "_second_part") for n in ("q", "k")]
        third_part = [m.sem(n + "_third_part") for n in ("q", "k")]
        left = [m.sem(n + "_left") for n in ("q", "k")]
        stored = [m.sem(n + "_stored") for n in ("q", "k")]
        block = ctx.enter_context(nc.Block())

        @block.tensor
        def _(pe):
            pe.wait_ge(w.loaded, w.full)
            for c in range(NC):
                norm.turn(pe, c)
                pe.wait_ge(norm.copied, c + 1)
                b = c % 2
                for o, wt in enumerate((w["wq"], w["wk"])):
                    if c >= 2:
                        pe.wait_ge(left[o], c - 1)
                    pe.matmul(acc[:, b, o, :], wt[:, :], xT[:, chunk(c)], start=True, stop=True).then_inc(projected, 1)
                if c >= 2:
                    pe.wait_ge(v_copied, c - 1)
                for j in range(TPC):
                    last = pe.matmul(acc[:, b, 2, tile(j)], xT[:, tile(TPC * c + j)], w["wv"][:, :], start=True, stop=True)
                last.then_inc(projected, 1)

        @block.scalar
        def _(act):
            def second(c):
                for o in range(2):
                    act.wait_ge(left[o], c + 1)
                    act.activation(parts[o][:, 1, chunk(c)], rest[o][:, chunk(c)], ACT.Copy).then_inc(second_part[o], 1)

            norm.copy(act, 0)
            for c in range(NC):
                b = c % 2
                for o in range(2):
                    act.wait_ge(projected, 3 * c + o + 1)
                    act.activation(parts[o][:, 0, chunk(c)], acc[:, b, o, :], ACT.Copy, scale=scale[o]).then_inc(first_part[o], 1)
                if c + 1 < NC:
                    norm.copy(act, c + 1)
                act.wait_ge(projected, 3 * c + 3)
                act.activation(v[:, TPC * c:TPC * (c + 1), :], acc[:, b, 2, :].rearrange("p (j f) -> p j f", f=P),
                               ACT.Copy).then_inc(v_copied, 1)
                if c:
                    second(c - 1)
            second(NC - 1)

        @block.vector
        def _(dve):
            def remove_first(c):
                for o in range(2):
                    dve.wait_ge(first_part[o], c + 1)
                    dve.scalar_tensor_tensor(rest[o][:, chunk(c)], acc[:, c % 2, o, :], scale[o], parts[o][:, 0, chunk(c)],
                                             ALU.mult, ALU.subtract).then_inc(left[o], 1)

            def third_of_k(c):
                dve.wait_ge(second_part[1], c + 1)
                dve.tensor_tensor(parts[1][:, 2, chunk(c)], rest[1][:, chunk(c)], parts[1][:, 1, chunk(c)],
                                  ALU.subtract).then_inc(third_part[1], 1)

            steps = [(r, c) for r in range(rounds) for c in range(NC)]
            norm.stats(dve, 0)
            for n, (r, c) in enumerate(steps):
                if n + 1 < len(steps):
                    norm.stats(dve, steps[n + 1][1], steps[n + 1][0])
                norm.normalise(dve, c, r)
                if r == rounds - 1 and c >= 2:
                    remove_first(c - 2)
            for c in range(NC - 2, NC):
                third_of_k(c - 2)
                remove_first(c)
            for c in range(NC - 2, NC):
                third_of_k(c)

        @block.gpsimd
        def _(pool):
            for r in range(rounds):
                for c in range(NC):
                    norm.power(pool, c, r)
            for c in range(NC):
                pool.wait_ge(second_part[0], c + 1)
                pool.tensor_tensor(parts[0][:, 2, chunk(c)], rest[0][:, chunk(c)], parts[0][:, 1, chunk(c)],
                                   ALU.subtract).then_inc(third_part[0], 1)

        @block.sync
        def _(sp):
            for half in range(2):
                tokens = slice(half * TOK // 2, (half + 1) * TOK // 2)
                for s, ready in enumerate((first_part, second_part, third_part)):
                    for o, dst in enumerate((q_dram[:, s, :, tokens], k_dram[:, :, s, tokens])):
                        sp.wait_ge(ready[o], NC // 2 * (half + 1))
                        sp.dma_start(dst, parts[o][:, s, tokens]).then_inc(stored[o], 16)
            for o in range(2):
                sp.wait_ge(stored[o], 16 * SPL * 2)


def attention_heads(nc, g, tag, dram, q_dram, k_dram, v, o_dram, oT, sums, alibi):
    with ExitStack() as ctx:
        m = Memory(nc, ctx, tag)
        NR = PAIRS + (ALIBI if alibi else 0)
        NR_MAX = NR + SPL
        SLOT = 4
        PSLOT = 8
        KB = 3
        QB = 3
        LEAD = 14
        TURN = 6
        q_op = [m.sb(f"q_op{s}", [NR_MAX, TOK], BF16) for s in range(SLOT)]
        k_op = [m.sb(f"k_op{s}", [NR_MAX, TOK], BF16) for s in range(SLOT)]
        vh = [m.sb(f"vh{s}", [P, NT, 32]) for s in range(SLOT)]
        probs = m.sb("probs", [P, PSLOT, CH])
        maxes = m.sb("maxes", [P, NT, NC])
        neg_max = m.sb("neg_max", [P, NT])
        max_parts = m.sb("max_parts", [P, P], BF16)
        zeros = m.sb("zeros", [SPL * 2 * NS, 32], BF16)
        max_T = m.sb("max_T", [SPL * NT, P], BF16)
        o_sb = m.sb("o_sb", [P, 2, CH])
        ps_k = m.ps("ps_k", [P, KB, CH])
        ps_q = m.ps("ps_q", [P, QB, CH])
        ps_o = m.ps("ps_o", [P, 2, CH])
        op_loaded = [m.sem(f"op_loaded{s}") for s in range(SLOT)]
        max_loaded = [m.sem(f"max_loaded{s}") for s in range(SLOT)]
        ones_loaded = m.sem("ones_loaded")
        v_set = m.sem("v_set")
        v_ready = m.sem("v_ready")
        q_ready = m.sem("q_ready")
        q_read = m.sem("q_read")
        max_set = m.sem("max_set")
        max_ready = m.sem("max_ready")
        chain = m.sem("chain")
        k_ready = m.sem("k_ready")
        exp_done = m.sem("exp_done")
        pv_done = m.sem("pv_done")
        o_read = m.sem("o_read")
        o_stored = [m.sem(f"o_stored{s}") for s in range(2)]
        OPS = 2 + (2 if alibi else 0)
        looped = HEADS - SLOT
        o_back = m.sem("o_back")

        q_items = [(t, kc) for t in range(NT) for kc in range(t // TPC + 1)]
        NQ = len(q_items)

        k_items = []
        for c in range(NC):
            k_items += [(c, j, 0, CH) for j in range(TPC * c)]
            k_items += [(c, TPC * c + d, d * P, CH - d * P) for d in range(TPC)]
        NK = len(k_items)
        ends = [max(i for i, item in enumerate(k_items) if item[0] == c) for c in range(NC)]
        assert NK == NQ and NK % 4 == 0

        def number(i, k):
            return i * SLOT + k

        def use(i, k):
            return i + (k // SLOT + 1)

        def beyond(i, k, n=HEADS):
            return isinstance(i, int) and number(i, k) >= n

        def q_place(n):
            return n + (n >= TURN)

        def q_count(i, k, l):
            if isinstance(i, int) and number(i, k) == 0:
                return l + (l < TURN)
            if beyond(i, k):
                return HEADS * (NQ + 1)
            return number(i, k) * (NQ + 1) + l

        def q_freed(i, k, l):
            if isinstance(i, int) and number(i, k) == 0:
                before = [x for x in range(l % QB, l, QB) if x != TURN]
                return q_count(i, k, before[-1]) if before else 0
            if l < QB:
                return q_count(i, k - 1, max(x for x in range(NQ + 1) if x % QB == l))
            if beyond(i, k):
                return HEADS * (NQ + 1) - 1
            return q_count(i, k, l - QB)

        def stream(turn, item, i, k, p):
            k, n = k + 1 + p // NQ, p % NQ
            if n == TURN and not beyond(i, k, HEADS + 1):
                turn(i, k - 1)
            if not beyond(i, k):
                item(i, k, n)

        def prologue(turn, item):
            for n in range(NQ):
                item(0, 0, n)
            for p in range(LEAD):
                stream(turn, item, 0, 0, p)

        def heads(eng, body):
            with eng.Fori(0, HEADS // SLOT - 1) as i:
                for k in range(SLOT):
                    body(i, k)
            for k in range(SLOT):
                body(HEADS // SLOT - 1, k)

        turned_bank = ps_q[:, TURN % QB, 0:P // 2].bitcast(BF16)

        def stored(i, k, c):
            return number(i, k) * (NC // 2 * 16) + (c // 2 * 16 + 16)

        block = ctx.enter_context(nc.Block())

        @block.tensor
        def _(pe):
            pe.sem_inc(pv_done, PSLOT)

            def turn(i, k):
                pe.wait_ge(max_ready, number(i, k) + 1)
                pe.wait_ge(q_read, q_freed(i, k + 1, TURN))
                pe.transpose(turned_bank, max_parts[:, :], g["ident_b"][:, :]).then_inc(q_ready, 1)

            def item(i, k, n):
                t, kc = q_items[n]
                l = q_place(n)
                bank = l % QB
                width = min(CH, (t + 1) * P - kc * CH)
                if n == 0:
                    pe.wait_ge(op_loaded[k % SLOT], use(i, k) * (16 * OPS))
                freed = q_freed(i, k, l)
                if not isinstance(freed, int) or freed:
                    pe.wait_ge(q_read, freed)
                diagonal = kc == t // TPC
                last = pe.matmul(ps_q[:, bank, 0:width], q_op[k % SLOT][0:NR, tile(t)],
                                 k_op[k % SLOT][0:NR, kc * CH:kc * CH + width], start=True, stop=not diagonal,
                                 skip_group_check=True)
                if diagonal:
                    last = pe.matmul(ps_q[:, bank, width - P:width], g["ident_b"][:, :], g["mask_q"][:, :],
                                     start=False, stop=True, skip_group_check=True)
                last.then_inc(q_ready, 1)

            def scores(i, k, n):
                c, j, first, width = k_items[n]
                if n == 0:
                    pe.wait_ge(max_loaded[k % SLOT], use(i, k) * 16)
                last_use = n - KB if n >= KB else max(x for x in range(NK) if x % KB == n) - NK
                pe.wait_ge(exp_done, number(i, k) * NK + (last_use + 1 + KB))
                d = j - TPC * c
                last = pe.matmul(ps_k[:, n % KB, 0:width], k_op[k % SLOT][:, tile(j)],
                                 q_op[k % SLOT][:, c * CH + first:c * CH + first + width], start=True, stop=d < 0,
                                 skip_group_check=True)
                if d >= 0:
                    last = pe.matmul(ps_k[:, n % KB, 0:P], g["ident_b"][:, :], g["mask_k"][:, :],
                                     start=False, stop=True, skip_group_check=True)
                last.then_inc(k_ready, 1)

            def times_v(i, k, n):
                c, j, first, width = k_items[n]
                if n == 0:
                    pe.wait_ge(v_ready, number(i, k) + 1)
                if n == 0 or n - 1 in ends:
                    pe.wait_ge(o_read, number(i, k) * NC + (c + 1))
                if n % 4 == 0:
                    pe.wait_ge(exp_done, number(i, k) * NK + (n + 4 + KB))
                r = 32 * (j % 4)
                if c == 0 and j:
                    pe.matmul(ps_o[r:r + 32, 0, 0:first], zeros[:, :], g["sel"][:, 0:j, :], start=True, stop=True,
                              skip_group_check=True)
                pe.matmul(ps_o[r:r + 32, c % 2, first:first + width], vh[k % SLOT][:, j, :],
                          probs[:, n % PSLOT, 0:width], start=j < 4, stop=j >= TPC * c,
                          skip_group_check=True).then_inc(pv_done, 1)

            def body(i, k):
                for n in range(0, NK, 4):
                    for a in range(n, n + 4):
                        if a + KB < NK:
                            scores(i, k, a + KB)
                        elif not beyond(i, k + 1):
                            scores(i, k + 1, a + KB - NK)
                        stream(turn, item, i, k, a + LEAD)
                    for a in range(n, n + 4):
                        times_v(i, k, a)

            prologue(turn, item)
            pe.wait_ge(ones_loaded, 16 * SLOT)
            pe.wait_ge(max_set, 3)
            for n in range(KB):
                scores(0, 0, n)
            heads(pe, body)

        @block.vector
        def _(dve):
            dve.memset(max_parts[:, :], 0.0).then_inc(max_set, 1)
            dve.memset(maxes[:, :, :], -3e38).then_inc(max_set, 1)
            dve.memset(zeros[:, :], 0.0).then_inc(max_set, 1)
            dve.wait_ge(max_set, 3)

            def turn(i, k):
                dve.wait_ge(q_ready, q_count(i, k + 1, TURN))
                dve.tensor_copy(max_T[:, :], turned_bank[0:SPL * NT, :]).then_inc(q_read, 1)

            def item(i, k, n):
                t, kc = q_items[n]
                l = q_place(n)
                width = min(CH, (t + 1) * P - kc * CH)
                dve.wait_ge(q_ready, q_count(i, k, l))
                dve.tensor_reduce(maxes[:, t, kc:kc + 1], ps_q[:, l % QB, 0:width], AX.X, ALU.max).then_inc(q_read, 1)
                if n == NQ - 1:
                    maxima(i, k)

            def maxima(i, k):
                def part(s):
                    return max_parts[:, s * NT:(s + 1) * NT]

                done = number(i, k) * 5
                dve.wait_ge(q_read, q_count(i, k, NQ))
                dve.tensor_reduce(neg_max[:, :], maxes[:, :, :], AX.X, ALU.max, negate=True).then_inc(chain, 1)
                dve.wait_ge(chain, done + 1)
                dve.tensor_copy(part(0), neg_max[:, :]).then_inc(chain, 1)
                dve.wait_ge(chain, done + 2)
                dve.tensor_tensor(neg_max[:, :], neg_max[:, :], part(0), ALU.subtract).then_inc(chain, 1)
                dve.wait_ge(chain, done + 3)
                dve.tensor_copy(part(1), neg_max[:, :]).then_inc(chain, 1)
                dve.wait_ge(chain, done + 4)
                dve.tensor_tensor(neg_max[:, :], neg_max[:, :], part(1), ALU.subtract).then_inc(chain, 1)
                dve.wait_ge(chain, done + 5)
                dve.tensor_copy(part(2), neg_max[:, :]).then_inc(max_ready, 1)
                dve.wait_ge(max_ready, number(i, k) + 1)

            def body(i, k):
                for n in range(NK):
                    stream(turn, item, i, k, n + LEAD)

            prologue(turn, item)
            heads(dve, body)

        @block.scalar
        def _(act):
            act.sem_inc(exp_done, KB)
            act.sem_inc(o_read, 2)
            AHEAD = 4

            def exps(i, k, n):
                width = k_items[n][3]
                act.wait_ge(k_ready, number(i, k) * NK + (n + 1))
                act.wait_ge(pv_done, number(i, k) * NK + (n + 1))
                act.activation(probs[:, n % PSLOT, 0:width], ps_k[:, n % KB, 0:width], ACT.Exp).then_inc(exp_done, 1)

            def output(i, k, c):
                act.wait_ge(pv_done, number(i, k) * NK + (ends[c] + 1 + PSLOT))
                act.wait_ge(o_stored[c % 2], stored(i, k, c))
                act.activation(o_sb[:, c % 2, :], ps_o[:, c % 2, :], ACT.Copy).then_inc(o_read, 1)

            def body(i, k):
                for n in range(AHEAD, NK):
                    exps(i, k, n)
                    if n - AHEAD in ends:
                        output(i, k, ends.index(n - AHEAD))
                if not beyond(i, k + 1):
                    for n in range(AHEAD):
                        exps(i, k + 1, n)
                output(i, k, NC - 1)

            for n in range(AHEAD):
                exps(0, 0, n)
            heads(act, body)

        @block.gpsimd
        def _(pool):
            for s in range(SLOT):
                pool.memset(vh[s][:, :, :], 0.0).then_inc(v_set, 1)
            pool.wait_ge(v_set, SLOT)
            for s in range(SLOT):
                pool.memset(vh[s][:, :, DH:DH + 1], 1.0).then_inc(v_set, 1)
            pool.wait_ge(v_set, 2 * SLOT)

            def place(i, k):
                pool.tensor_copy(vh[k][:, :, 0:DH], v[:, :, ds(number(i, k) * DH, DH)]).then_inc(v_ready, 1)

            for k in range(SLOT):
                place(0, k)
            with pool.Fori(1, HEADS // SLOT) as i:
                for k in range(SLOT):
                    pool.wait_ge(pv_done, number(i, k - 3) * NK + PSLOT)
                    place(i, k)

        @block.sync
        def _(sp):
            for s in range(2):
                sp.sem_inc(o_stored[s], 16)

            def load(i, k):
                h = number(i, k)
                s = k % SLOT
                q_rows = q_dram[ds(h, 1), :, :, :].rearrange("o a d t -> (o a d) t").unsqueeze(1)
                k_rows = k_dram[ds(h, 1), :, :, :].rearrange("o d b t -> o (d b) t")
                sp.dma_start(q_op[s][0:PAIRS, :], q_rows.broadcast_to([SPL * DH, SPL, TOK])).then_inc(op_loaded[s], 16)
                sp.dma_start(k_op[s][0:PAIRS, :], k_rows.broadcast_to([SPL, SPL * DH, TOK])).then_inc(op_loaded[s], 16)
                if alibi:
                    sp.dma_start(q_op[s][PAIRS:NR, :], dram["alibi_q"][ds(h, 1), :, :].rearrange("o r t -> (o r) t")).then_inc(op_loaded[s], 16)
                    sp.dma_start(k_op[s][PAIRS:NR, :], dram["alibi_k"][ds(h, 1), :, :].rearrange("o r t -> (o r) t")).then_inc(op_loaded[s], 16)

            def load_maxima(i, k):
                sp.wait_ge(q_read, q_count(i, k + 1, TURN))
                sp.dma_start(q_op[k % SLOT][NR:NR_MAX, :].rearrange("s (t p) -> s t p", p=P),
                             max_T[:, :]).then_inc(max_loaded[k % SLOT], 16)

            def store(i, k, c):
                h = number(i, k)
                sp.wait_ge(o_read, h * NC + (c + 3))
                sp.dma_start(o_dram[ds(h, 1), :, chunk(c)], o_sb[:, c % 2, :]).then_inc(o_stored[c % 2], 16)

            def load_looped():
                for s in range(2):
                    sp.wait_ge(o_stored[s], stored(0, looped, s))
                for r in range(4):
                    rows = o_dram[0:looped, 32 * r:32 * (r + 1), :]
                    sp.dma_start(oT[0:looped * DH, r, :], rows[:, 0:DH, :]).then_inc(o_back, 16)
                    sp.dma_start(sums[0:looped * SB, r, :],
                                 rows[:, DH, :].rearrange("h (b t) -> h b t", b=SB)).then_inc(o_back, 16)

            def load_output(h):
                for s in range(2):
                    sp.wait_ge(o_stored[s], stored(0, h + 1, s))
                rows = o_dram[h, :, :].rearrange("(r d) t -> d r t", r=4)
                sp.dma_start(oT[h * DH:(h + 1) * DH, :, :], rows[0:DH, :, :]).then_inc(o_back, 16)
                sp.dma_start(sums[h * SB:(h + 1) * SB, :, :],
                             rows[DH, :, :].rearrange("r (b t) -> b r t", b=SB)).then_inc(o_back, 16)

            load(0, 0)
            for k in range(SLOT):
                sp.dma_start(k_op[k][NR:NR_MAX, :], dram["ones_b"]).then_inc(ones_loaded, 16)
            for k in range(1, SLOT):
                load(0, k)
            load_maxima(0, 0)

            def body(i, k):
                for c in range(NC - 1):
                    store(i, k, c)
                if isinstance(i, int) and number(i, k) == looped:
                    load_looped()
                elif beyond(i, k, looped + 1):
                    load_output(number(i, k) - 1)
                if not beyond(i, k + 1):
                    load_maxima(i, k + 1)
                if not beyond(i, k + SLOT):
                    sp.wait_ge(k_ready, number(i, k + 1) * NK)
                    load(i, k + SLOT)
                store(i, k, NC - 1)

            heads(sp, body)
            load_output(HEADS - 1)
            sp.wait_ge(o_back, 16 * (8 + 2 * SLOT))


def attention_out(nc, g, w, tag, x, oT, sums):
    with ExitStack() as ctx:
        m = Memory(nc, ctx, tag)
        BPC = SB // NC
        inv = m.sb("inv", [HEADS * SB, TOK // SB])
        pair = m.sb("pair", [P, 2, TOK // SB])
        total = m.sb("total", [P, 2, CH])
        upper = m.sb("upper", [P, 2, CH])
        ps_s = m.ps("ps_s", [P, 2, CH])
        ps_y = m.ps("ps_y", [P, 2, CH])
        paired = m.sem("paired")
        summed = m.sem("summed")
        inverted = m.sem("inverted")
        spread_ready = m.sem("spread_ready")
        upper_ready = m.sem("upper_ready")
        lower_ready = m.sem("lower_ready")
        total_ready = m.sem("total_ready")
        normed = m.sem("normed")
        y_ready = m.sem("y_ready")
        added = m.sem("added")
        block = ctx.enter_context(nc.Block())

        @block.tensor
        def _(pe):
            def spread(c):
                if c >= 2:
                    pe.wait_ge(normed, c - 1)
                for b in range(BPC):
                    last = pe.matmul(ps_s[:, c % 2, b * (TOK // SB):(b + 1) * (TOK // SB)], g["sel_head"][:, BPC * c + b, :],
                                     inv[:, :], start=True, stop=True)
                last.then_inc(spread_ready, 1)

            pe.wait_ge(inverted, 1)
            spread(0)
            for c in range(NC):
                if c + 1 < NC:
                    spread(c + 1)
                pe.wait_ge(normed, c + 1)
                if c >= 2:
                    pe.wait_ge(added, c - 1)
                for j in range(TPC):
                    last = pe.matmul(ps_y[:, c % 2, tile(j)], total[:, c % 2, tile(j)], w["wo"][:, :], start=True, stop=True)
                last.then_inc(y_ready, 1)

        @block.gpsimd
        def _(pool):
            for c in range(NC):
                if c >= 2:
                    pool.wait_ge(total_ready, c - 1)
                pool.tensor_tensor(upper[:, c % 2, :], oT[:, 2, chunk(c)], oT[:, 3, chunk(c)], ALU.add).then_inc(upper_ready, 1)

        @block.vector
        def _(dve):
            def add_partials(c):
                s = c % 2
                if c >= 2:
                    dve.wait_ge(y_ready, c - 1)
                dve.tensor_tensor(total[:, s, :], oT[:, 0, chunk(c)], oT[:, 1, chunk(c)], ALU.add).then_inc(lower_ready, 1)
                dve.wait_ge(lower_ready, c + 1)
                dve.wait_ge(upper_ready, c + 1)
                dve.tensor_tensor(total[:, s, :], total[:, s, :], upper[:, s, :], ALU.add).then_inc(total_ready, 1)

            def add(c):
                dve.wait_ge(y_ready, c + 1)
                xc = x[:, TPC * c:TPC * (c + 1), :]
                dve.tensor_tensor(xc, ps_y[:, c % 2, :].rearrange("p (j f) -> p j f", f=P), xc, ALU.add).then_inc(added, 1)

            dve.tensor_tensor(pair[:, :, :], sums[:, 0:2, :], sums[:, 2:4, :], ALU.add).then_inc(paired, 1)
            dve.wait_ge(paired, 1)
            dve.tensor_tensor(inv[:, :], pair[:, 0, :], pair[:, 1, :], ALU.add).then_inc(summed, 1)
            dve.wait_ge(summed, 1)
            dve.reciprocal(inv[:, :], inv[:, :]).then_inc(inverted, 1)
            for c in range(2):
                add_partials(c)
            for c in range(NC):
                dve.wait_ge(total_ready, c + 1)
                dve.wait_ge(spread_ready, c + 1)
                dve.tensor_tensor(total[:, c % 2, :], total[:, c % 2, :], ps_s[:, c % 2, :], ALU.mult).then_inc(normed, 1)
                if c:
                    add(c - 1)
                    if c + 1 < NC:
                        add_partials(c + 1)
            add(NC - 1)


MAMBA = ["in_T", "conv_w", "conv_b", "x_T", "dt_T", "dt_b", "a_log", "d", "out_T"]
MAMBA_FFN = ["w1_T", "b1", "w2_T", "b2_rows", "norm_w", "ffn_norm_w"]
QLORA = ["bias_cols", "gamma", "beta"]
QLORA_RAW = ["bias_0", "q_T", "scale_T", "lora_a", "lora_b_T"]
ATT0 = ["wq", "wk", "wv", "wo", "gain"]
ATT1 = ["wq", "wk", "wv", "wo"]
CONST = ["ident", "minus_half"]
CONST_LATE = ["ident_b", "ones_row", "ones_3", "sel", "sel_e", "iota", "mask_q", "mask_k", "sel_head"]


def build(nc, dram, out):
    Memory.count = 0
    with ExitStack() as ctx:
        m = Memory(nc, ctx, "all")
        x = m.sb("x", [P, NT, P])
        xn = m.sb("xn", [P, NT, P])
        x_loaded = m.sem("x_loaded")
        stored = m.sem("stored")
        g = group(m, dram, "c", CONST)
        g.late = group(m, dram, "c", CONST_LATE)
        g.update(g.late)
        m0 = group(m, dram, "m0", MAMBA)
        m0_ffn = group(m, dram, "m0", MAMBA_FFN)
        a0 = group(m, dram, "a0", ATT0)
        m1 = group(m, dram, "m1", MAMBA)
        ql = group(m, dram, "ql", QLORA)
        qr = group(m, dram, "qr", QLORA_RAW)
        a1 = group(m, dram, "a1", ATT1)
        ql["eff"] = m.sb("ql_eff", [P, QL, P])
        ql["bias3"] = m.sb("ql_bias3", [SPL, QL // 2, P], BF16)
        late = g.late.loads + m0_ffn.loads + a0.loads + m1.loads + ql.loads + qr.loads + a1.loads

        with nc.Block() as block:
            @block.sync
            def _(sp):
                start_loads(sp, g.loads)
                for c in range(0, NC, 2):
                    sp.dma_start(x[:, TPC * c:TPC * (c + 1), :], dram["x"][:, TPC * c:TPC * (c + 1), :]).then_inc(x_loaded, 16)
                start_loads(sp, m0.loads)
                sp.wait_ge(g.loaded, g.full)
                sp.wait_ge(x_loaded, 16 * NC)

            @block.scalar
            def _(act):
                for c in range(1, NC, 2):
                    act.dma_start(x[:, TPC * c:TPC * (c + 1), :], dram["x"][:, TPC * c:TPC * (c + 1), :]).then_inc(x_loaded, 16)

        plan = [
            lambda: mamba(nc, g, m0, "m0", x, xn, lambda gated: mamba_out_ffn(nc, g, m0, m0_ffn, "m0o", x, xn, gated), late),
            lambda: moe(nc, g, dram, "e0", x, xn),
            lambda: attention(nc, g, a0, "a0", dram, x, xn, False),
            lambda: moe(nc, g, dram, "e1", x, xn),
            lambda: mamba(nc, g, m1, "m1", x, xn, lambda gated: mamba_out_add(nc, m1, "m1o", x, gated, qr, ql["eff"], ql["bias3"])),
            lambda: qlora_mlp(nc, g, ql, "q0", x, xn),
            lambda: attention(nc, g, a1, "a1", dram, x, xn, True),
            lambda: qlora_mlp(nc, g, ql, "q1", x, xn),
        ]
        for step in plan:
            with fresh_semaphores(nc):
                step()
        with nc.Block() as block:
            @block.sync
            def _(sp):
                sp.dma_start(out, x[:, :, :]).then_inc(stored, 16)
                for w in (m0, m0_ffn, a0, m1, ql, qr, a1):
                    sp.wait_ge(w.loaded, w.full)
                sp.wait_ge(stored, 16)


def constants():
    bf = mybir.dt.np(BF16)
    k, q = np.arange(P)[:, None], np.arange(P)[None, :]
    sel = np.zeros((SPL, 2 * NS, 2 * NS, P), np.float32)
    for n in range(2 * NS):
        sel[:, n, n] = 1
    sel_e = np.zeros((SPL, NE, NE, P), np.float32)
    for n in range(NE):
        sel_e[:, n, n] = 1
    sel_head = np.zeros((HEADS, SB, SB, HEADS, DH), np.float32)
    for h in range(HEADS):
        for b in range(SB):
            sel_head[h, b, b, h] = 1
    slopes = (2.0 ** (-8.0 / HEADS * (np.arange(HEADS, dtype=np.float32) + 1.0))).astype(np.float32)
    pos = np.arange(TOK)
    hi, lo = (pos // P * P).astype(np.float32), (pos % P).astype(np.float32)
    qa, ka = np.zeros((HEADS, ALIBI, TOK), np.float32), np.zeros((HEADS, ALIBI, TOK), np.float32)
    rest = slopes.copy()
    for s in range(SPL):
        part = rest.astype(bf).astype(np.float32)
        rest = rest - part
        for r, p in enumerate((hi, lo)):
            row = 4 * s + 2 * r
            qa[:, row], ka[:, row] = part[:, None], p
            qa[:, row + 1], ka[:, row + 1] = p, -part[:, None]
    return {
        "c_ident": np.eye(P, dtype=np.float32),
        "c_ident_b": np.eye(P, dtype=np.float32).astype(bf),
        "c_ones_row": np.ones((1, P), np.float32),
        "c_ones_3": np.ones((SPL, P), np.float32).astype(bf),
        "c_sel": sel.reshape(SPL * 2 * NS, 2 * NS, P).astype(bf),
        "c_sel_e": sel_e.reshape(SPL * NE, NE, P).astype(bf),
        "c_iota": np.tile(np.arange(NE, dtype=np.float32), (P, 1)),
        "c_minus_half": np.full((P, NT), -0.5, np.float32),
        "c_mask_q": np.where(q > k, NEG, 0.0).astype(bf),
        "c_mask_k": np.where(k > q, NEG, 0.0).astype(bf),
        "c_sel_head": sel_head.reshape(P, SB, P),
        "alibi_q": qa.astype(bf),
        "alibi_k": ka.astype(bf),
        "ones_b": np.ones((SPL, TOK), np.float32).astype(bf),
    }


def layouts(i):
    def halves(a):
        return a.reshape((a.shape[0] // P, P) + a.shape[1:]).swapaxes(0, 1)

    def rows(a):
        return np.broadcast_to(a, (P, P))

    r = {"x": i["L0_attn_a_input_tensor"][0].reshape(NT, P, P).swapaxes(0, 1)}
    a = {k[len("L0_attn_a_"):]: v for k, v in i.items() if k.startswith("L0_attn_a_")}
    r.update({
        "m0_in_T": a["in_proj_w"].T, "m0_conv_w": halves(a["conv_w"]), "m0_conv_b": halves(a["conv_b"]),
        "m0_x_T": halves(a["x_proj_w"].T), "m0_dt_T": a["dt_proj_w"].T, "m0_dt_b": halves(a["dt_proj_b"]),
        "m0_a_log": halves(a["A_log"]), "m0_d": halves(a["D"]), "m0_out_T": halves(a["out_proj_w"].T),
        "m0_w1_T": a["ffn_w1"].T, "m0_b1": halves(a["ffn_b1"]), "m0_w2_T": halves(a["ffn_w2"].T),
        "m0_b2_rows": np.tile(a["ffn_b2"], TPC)[None], "m0_norm_w": rows(a["norm_w"]),
        "m0_ffn_norm_w": rows(a["ffn_norm_w"]),
    })
    a = {k[len("L1_attn_a_"):]: v for k, v in i.items() if k.startswith("L1_attn_a_")}
    r.update({
        "m1_in_T": a["W_in"], "m1_conv_w": halves(a["conv_w"]), "m1_conv_b": halves(a["conv_b"]),
        "m1_x_T": halves(a["W_x"]), "m1_dt_T": a["W_dt"], "m1_dt_b": halves(a["b_dt"]),
        "m1_a_log": halves(a["A_log"]), "m1_d": halves(a["D"]), "m1_out_T": halves(a["W_out"]),
    })
    a = {k[len("L0_ffn_"):]: v for k, v in i.items() if k.startswith("L0_ffn_")}
    r.update({
        "me_g_T": a["Wg"].T, "me_w1_T": a["W1"].transpose(2, 0, 1), "me_w2_T": a["W2"].transpose(2, 0, 1),
        "me_w3_T": halves(a["W3"].transpose(2, 0, 1)).transpose(0, 2, 1, 3),
        "me_b1": halves(a["b1"].T).transpose(0, 2, 1), "me_b2": halves(a["b2"].T).transpose(0, 2, 1), "me_b3_rows": np.tile(a["b3"], (SPL, 1)),
    })
    wkv = i["L0_attn_b_Wkv"]
    r.update({"a0_wq": i["L0_attn_b_Wq"], "a0_wk": wkv[:, :P], "a0_wv": wkv[:, P:], "a0_wo": i["L0_attn_b_Wo"],
              "a0_gain": i["L0_attn_b_g_ln"][:, None]})
    w_in = i["L1_attn_b_w_in"]
    r.update({"a1_wq": w_in[:P].T, "a1_wk": w_in[P:2 * P].T, "a1_wv": w_in[2 * P:].T, "a1_wo": i["L1_attn_b_w_out"].T})
    a = {k[len("L1_ffn_"):]: v for k, v in i.items() if k.startswith("L1_ffn_")}
    r.update({
        "qr_q_T": a["qweights"].transpose(2, 0, 1),
        "qr_scale_T": np.repeat(a["scales"], P // a["scales"].shape[2], axis=2).transpose(2, 0, 1),
        "qr_bias_0": a["biases"][0::2], "ql_bias_cols": a["biases"].T,
        "qr_lora_a": a["lora_a"].swapaxes(0, 1), "qr_lora_b_T": a["lora_b"].transpose(2, 0, 1),
        "ql_gamma": a["ln_gamma"].T, "ql_beta": a["ln_beta"].T,
    })
    return r


def kernel(**inputs):
    import concourse.bacc as bacc
    from concourse.bass_utils import run_bass_kernel_spmd

    nc = bacc.Bacc("TRN2", target_bir_lowering=False, num_devices=1)
    arrays, dram = {}, {}
    laid = layouts({k: np.asarray(v) for k, v in inputs.items()})
    for name, a in {**laid, **constants()}.items():
        a = np.ascontiguousarray(a)
        arrays[f"in_{name}"] = a
        dram[name] = nc.dram_tensor(f"in_{name}", a.shape, mybir.dt.from_np(a.dtype), kind="ExternalInput").ap()
    out = nc.dram_tensor("out_x", (P, NT, P), F32, kind="ExternalOutput").ap()
    build(nc, dram, out)
    r = run_bass_kernel_spmd(nc, [arrays], core_ids=[0])
    got = r.results[0]["out_x"].reshape(P, NT, P).swapaxes(0, 1).reshape(1, TOK, P)
    return np.ascontiguousarray(got)
```
